# Optimizing a Trainium2 kernel written in Bass

```python
import numpy as np
import jax
import jax.numpy as jnp

def _softmax(x, axis=-1):
    return jax.nn.softmax(x, axis=axis)

def _gelu(x):
    return jax.nn.gelu(x, approximate=True)

def _silu(x):
    return jax.nn.silu(x)

def _sigmoid(x):
    return jax.nn.sigmoid(x)

def _layernorm(x, axis=-1, eps=1e-05):
    m = jnp.mean(x, axis=axis, keepdims=True)
    v = jnp.var(x, axis=axis, keepdims=True)
    return (x - m) / jnp.sqrt(v + eps)

def _scatter_add(tgt, idx, src, axis=0):
    return tgt.at[idx].add(src)

def _segment_sum(src, seg, n):
    return jax.ops.segment_sum(src, seg, n)
kernel_name = 'mk_decoder_preln_d1_seqx_r8_6490e1'

def setup_inputs(seed: int=0):
    np.random.seed(seed)
    _w = jnp.asarray

    def _rec_inputs():
        import jax
        import jax.numpy as jnp
        _rk = jax.random.key(seed)
        x = 7.22e-05 + 1 * jax.random.normal(jax.random.fold_in(_rk, 1), (16, 128, 256), jnp.float32)
        _lenS = 128 - jax.random.randint(jax.random.fold_in(_rk, 7), (16,), 0, max(1, 128 // 4) + 1, jnp.int32)
        _lenS2 = 128 - jax.random.randint(jax.random.fold_in(_rk, 8), (16,), 0, max(1, 128 // 4) + 1, jnp.int32)
        _ctx_512P = jax.random.normal(jax.random.fold_in(_rk, 11), (16, 16, 64), jnp.float32)
        _ctx_512c = jax.random.dirichlet(jax.random.fold_in(_rk, 511), 0.3 * jnp.ones((16,), jnp.float32), (16, 128))
        _ctx_512t = jnp.einsum('bsk,bkd->bsd', _ctx_512c, _ctx_512P)
        _ctx_512t = _ctx_512t * jax.lax.rsqrt(jnp.mean(jnp.square(_ctx_512t)) + 1e-12) * 0.953939
        ctx_512 = -0.000514642 + 1.00011 * (_ctx_512t + 0.3 * jax.random.normal(jax.random.fold_in(_rk, 611), (16, 128, 64), jnp.float32))
        return (x, ctx_512)
    x, ctx_512 = _rec_inputs()

    def _L0_attn_setup():
        import jax, jax.numpy as jnp
        import numpy as np
        B, T, C, H = (4, 256, 256, 32)
        N = C // H
        N_LAYER, LAYER_ID = (24, 12)
        EPS = 1e-05 * 64
        key = jax.random.key(seed)
        ks = jax.random.split(key, 8)
        r01 = LAYER_ID / (N_LAYER - 1)
        r10 = 1.0 - LAYER_ID / N_LAYER
        ddd = np.arange(C, dtype=np.float64) / C
        maa_k = (1.0 - ddd ** r10).astype(np.float32)
        maa_v = (1.0 - (ddd ** r10 + 0.3 * r01)).astype(np.float32)
        maa_r = (1.0 - ddd ** (0.5 * r10)).astype(np.float32)
        maa_g = maa_r.copy()
        h = np.arange(H, dtype=np.float64)
        time_decay = (-6.0 + 5.0 * (h / (H - 1)) ** (0.7 + 1.3 * r01)).astype(np.float32)
        time_faaaa = (r01 * (1.0 - h / (H - 1))).astype(np.float32)
        s = C ** (-0.5)
        lin = lambda k: jax.random.normal(k, (C, C), jnp.float32) * s
        z = jnp.zeros((C,), jnp.float32)
        return dict(x=jax.random.normal(ks[0], (B, T, C), jnp.float32), Wr=lin(ks[1]), br=z, Wk=lin(ks[2]), bk=z, Wv=lin(ks[3]), bv=z, Wg=lin(ks[4]), bg=z, Wo=lin(ks[5]), bo=z, ln_g=jnp.ones((C,), jnp.float32), ln_b=z, maa_k=jnp.asarray(maa_k), maa_v=jnp.asarray(maa_v), maa_r=jnp.asarray(maa_r), maa_g=jnp.asarray(maa_g), time_decay=jnp.asarray(time_decay), time_faaaa=jnp.asarray(time_faaaa))
    _L0_attn_all = _L0_attn_setup()
    _L0_attn_in = {k: v for k, v in _L0_attn_all.items() if k in ('Wr', 'br', 'Wk', 'bk', 'Wv', 'bv', 'Wg', 'bg', 'Wo', 'bo', 'ln_g', 'ln_b', 'maa_k', 'maa_v', 'maa_r', 'maa_g', 'time_decay', 'time_faaaa')}
    del _L0_attn_all

    def _L0_xattn_setup():
        import jax, jax.numpy as jnp
        import numpy as np
        B, S, H, NH, L = (2, 256, 256, 16, 64)
        HD = H // NH
        key = jax.random.key(seed)
        k1, k2, k3, k4, k5 = jax.random.split(key, 5)
        scale = 0.02
        return {'q': jax.random.normal(k1, (B, S, H), dtype=jnp.float32), 'latent_kv': jax.random.normal(k2, (B, S, L), dtype=jnp.float32), 'Wq': jax.random.normal(k3, (H, H), dtype=jnp.float32) * scale, 'Wkv_expand': jax.random.normal(k4, (2 * H, L), dtype=jnp.float32) * scale, 'Wout': jax.random.normal(k5, (H, H), dtype=jnp.float32) * scale}
    _L0_xattn_all = _L0_xattn_setup()
    _L0_xattn_in = {k: v for k, v in _L0_xattn_all.items() if k in ('Wq', 'Wkv_expand', 'Wout')}
    del _L0_xattn_all

    def _L0_ffn_setup():
        import jax, jax.numpy as jnp
        import numpy as np
        E = 8
        TOP_K = 2
        H = 256
        I = 176
        SI = 704
        key = jax.random.key(seed)
        ks = jax.random.split(key, 9)
        s = lambda fan_in: 1.0 / np.sqrt(fan_in)
        return {'hidden_states': jax.random.normal(ks[0], (4, 256, H), dtype=jnp.float32), 'router_w': jax.random.normal(ks[1], (E, H), dtype=jnp.float32) * s(H), 'w_gate': jax.random.normal(ks[2], (E, H, I), dtype=jnp.float32) * s(H), 'w_up': jax.random.normal(ks[3], (E, H, I), dtype=jnp.float32) * s(H), 'w_down': jax.random.normal(ks[4], (E, I, H), dtype=jnp.float32) * s(I), 'sw_gate': jax.random.normal(ks[5], (H, SI), dtype=jnp.float32) * s(H), 'sw_up': jax.random.normal(ks[6], (H, SI), dtype=jnp.float32) * s(H), 'sw_down': jax.random.normal(ks[7], (SI, H), dtype=jnp.float32) * s(SI), 'shared_gate_w': jax.random.normal(ks[8], (H,), dtype=jnp.float32) * s(H)}
    _L0_ffn_all = _L0_ffn_setup()
    _L0_ffn_in = {k: v for k, v in _L0_ffn_all.items() if k in ('router_w', 'w_gate', 'w_up', 'w_down', 'sw_gate', 'sw_up', 'sw_down', 'shared_gate_w')}
    del _L0_ffn_all
    return {'x': x, 'ctx_512': ctx_512, 'L0_attn_Wr': _L0_attn_in['Wr'], 'L0_attn_br': _L0_attn_in['br'], 'L0_attn_Wk': _L0_attn_in['Wk'], 'L0_attn_bk': _L0_attn_in['bk'], 'L0_attn_Wv': _L0_attn_in['Wv'], 'L0_attn_bv': _L0_attn_in['bv'], 'L0_attn_Wg': _L0_attn_in['Wg'], 'L0_attn_bg': _L0_attn_in['bg'], 'L0_attn_Wo': _L0_attn_in['Wo'], 'L0_attn_bo': _L0_attn_in['bo'], 'L0_attn_ln_g': _L0_attn_in['ln_g'], 'L0_attn_ln_b': _L0_attn_in['ln_b'], 'L0_attn_maa_k': _L0_attn_in['maa_k'], 'L0_attn_maa_v': _L0_attn_in['maa_v'], 'L0_attn_maa_r': _L0_attn_in['maa_r'], 'L0_attn_maa_g': _L0_attn_in['maa_g'], 'L0_attn_time_decay': _L0_attn_in['time_decay'], 'L0_attn_time_faaaa': _L0_attn_in['time_faaaa'], 'L0_xattn_Wq': _L0_xattn_in['Wq'], 'L0_xattn_Wkv_expand': _L0_xattn_in['Wkv_expand'], 'L0_xattn_Wout': _L0_xattn_in['Wout'], 'L0_ffn_router_w': _L0_ffn_in['router_w'], 'L0_ffn_w_gate': _L0_ffn_in['w_gate'], 'L0_ffn_w_up': _L0_ffn_in['w_up'], 'L0_ffn_w_down': _L0_ffn_in['w_down'], 'L0_ffn_sw_gate': _L0_ffn_in['sw_gate'], 'L0_ffn_sw_up': _L0_ffn_in['sw_up'], 'L0_ffn_sw_down': _L0_ffn_in['sw_down'], 'L0_ffn_shared_gate_w': _L0_ffn_in['shared_gate_w']}

def reference(x, ctx_512, L0_attn_Wr, L0_attn_br, L0_attn_Wk, L0_attn_bk, L0_attn_Wv, L0_attn_bv, L0_attn_Wg, L0_attn_bg, L0_attn_Wo, L0_attn_bo, L0_attn_ln_g, L0_attn_ln_b, L0_attn_maa_k, L0_attn_maa_v, L0_attn_maa_r, L0_attn_maa_g, L0_attn_time_decay, L0_attn_time_faaaa, L0_xattn_Wq, L0_xattn_Wkv_expand, L0_xattn_Wout, L0_ffn_router_w, L0_ffn_w_gate, L0_ffn_w_up, L0_ffn_w_down, L0_ffn_sw_gate, L0_ffn_sw_up, L0_ffn_sw_down, L0_ffn_shared_gate_w):
    import jax
    import jax.numpy as jnp

    def _L0_attn_ref(x, Wr, br, Wk, bk, Wv, bv, Wg, bg, Wo, bo, ln_g, ln_b, maa_k, maa_v, maa_r, maa_g, time_decay, time_faaaa):
        import jax, jax.numpy as jnp
        import numpy as np
        B, T, C, H = (4, 256, 256, 32)
        N = C // H
        N_LAYER, LAYER_ID = (24, 12)
        EPS = 1e-05 * 64
        Bx, Tx, Cx = x.shape
        Q = 32 if Tx % 32 == 0 else 128 if Tx % 128 == 0 else Tx
        nc = Tx // Q
        xx = jnp.pad(x, ((0, 0), (1, 0), (0, 0)))[:, :Tx] - x
        xk = x + xx * maa_k
        xv = x + xx * maa_v
        xr = x + xx * maa_r
        xg = x + xx * maa_g
        r = (xr @ Wr.T + br).reshape(Bx, Tx, H, N).transpose(0, 2, 1, 3)
        k = (xk @ Wk.T + bk).reshape(Bx, Tx, H, N).transpose(0, 2, 3, 1)
        v = (xv @ Wv.T + bv).reshape(Bx, Tx, H, N).transpose(0, 2, 1, 3)
        g = jax.nn.silu(xg @ Wg.T + bg)
        w = jnp.exp(-jnp.exp(time_decay))
        u = time_faaaa
        t = jnp.arange(Q)
        ws = (w ** Q)[None, :, None, None]
        wkv = (w[:, None] ** (Q - 1 - t))[None, :, None, :]
        wb = (w[:, None] ** t)[None, :, :, None]
        diff = t[:, None] - t[None, :]
        pw = w[:, None, None] ** jnp.maximum(diff - 1, 0)
        Wm = jnp.where(diff > 0, pw, jnp.where(diff == 0, u[:, None, None], 0.0))
        r_c = r.reshape(Bx, H, nc, Q, N).transpose(2, 0, 1, 3, 4)
        k_c = k.reshape(Bx, H, N, nc, Q).transpose(3, 0, 1, 2, 4)
        v_c = v.reshape(Bx, H, nc, Q, N).transpose(2, 0, 1, 3, 4)

        def step(state, chunk):
            rr, kk, vv = chunk
            att = rr @ kk * Wm
            y = att @ vv + rr @ state * wb
            state = ws * state + kk * wkv @ vv
            return (state, y)
        state0 = jnp.zeros((Bx, H, N, N), x.dtype)
        _, ys = jax.lax.scan(step, state0, (r_c, k_c, v_c))
        y = ys.transpose(1, 2, 0, 3, 4).reshape(Bx, H, Tx, N)
        y = y.transpose(0, 2, 1, 3).reshape(Bx, Tx, Cx)
        z = y.reshape(Bx * Tx, H, N)
        mu = z.mean(-1, keepdims=True)
        var = z.var(-1, keepdims=True)
        zn = ((z - mu) * jax.lax.rsqrt(var + EPS)).reshape(Bx, Tx, Cx)
        y = (zn * ln_g + ln_b) * g
        return y @ Wo.T + bo

    def _L0_xattn_ref(q, latent_kv, Wq, Wkv_expand, Wout):
        import jax, jax.numpy as jnp
        import numpy as np
        B, S, H, NH, L = (2, 256, 256, 16, 64)
        HD = H // NH
        b, sq, _ = q.shape
        sk = latent_kv.shape[1]
        qp = q @ Wq.T
        kv = latent_kv @ Wkv_expand.T
        k, v = jnp.split(kv, 2, axis=-1)
        qh = qp.reshape(b, sq, NH, HD).transpose(0, 2, 1, 3)
        kh = k.reshape(b, sk, NH, HD).transpose(0, 2, 1, 3)
        vh = v.reshape(b, sk, NH, HD).transpose(0, 2, 1, 3)
        inv_sqrt_d = 1.0 / jnp.sqrt(jnp.float32(HD))
        scores = jnp.einsum('bhqd,bhkd->bhqk', qh, kh) * inv_sqrt_d
        causal = jnp.tril(jnp.ones((sq, sk), dtype=bool))
        scores = jnp.where(causal, scores, jnp.finfo(scores.dtype).min)
        attn = jax.nn.softmax(scores, axis=-1)
        out = jnp.einsum('bhqk,bhkd->bhqd', attn, vh)
        out = out.transpose(0, 2, 1, 3).reshape(b, sq, H)
        return out @ Wout.T

    def _L0_ffn_ref(hidden_states, router_w, w_gate, w_up, w_down, sw_gate, sw_up, sw_down, shared_gate_w):
        import jax, jax.numpy as jnp
        import numpy as np
        E = 8
        TOP_K = 2
        H = 256
        I = 176
        SI = 704
        B, S, Hd = hidden_states.shape
        x = hidden_states.reshape(-1, Hd)
        shared = jnp.einsum('ts,sh->th', jax.nn.silu(x @ sw_gate) * (x @ sw_up), sw_down)
        logits = x @ router_w.T
        probs = jax.nn.softmax(logits.astype(jnp.float32), axis=-1)
        top_w, top_i = jax.lax.top_k(probs, TOP_K)
        top_w = top_w / jnp.sum(top_w, axis=-1, keepdims=True)
        combine = jnp.sum(jax.nn.one_hot(top_i, E, dtype=x.dtype) * top_w[..., None].astype(x.dtype), axis=1)
        h = jax.nn.silu(jnp.einsum('th,ehi->eti', x, w_gate)) * jnp.einsum('th,ehi->eti', x, w_up)
        expert_out = jnp.einsum('eti,eih->eth', h, w_down)
        routed = jnp.einsum('eth,te->th', expert_out, combine)
        shared_out = jax.nn.sigmoid(x @ shared_gate_w)[:, None] * shared
        return (routed + shared_out).reshape(B, S, Hd)
    x = x + _L0_attn_ref(_layernorm(x, axis=-1), L0_attn_Wr, L0_attn_br, L0_attn_Wk, L0_attn_bk, L0_attn_Wv, L0_attn_bv, L0_attn_Wg, L0_attn_bg, L0_attn_Wo, L0_attn_bo, L0_attn_ln_g, L0_attn_ln_b, L0_attn_maa_k, L0_attn_maa_v, L0_attn_maa_r, L0_attn_maa_g, L0_attn_time_decay, L0_attn_time_faaaa)
    x = x + _L0_xattn_ref(_layernorm(x, axis=-1), ctx_512, L0_xattn_Wq, L0_xattn_Wkv_expand, L0_xattn_Wout)
    x = x + _L0_ffn_ref(_layernorm(x, axis=-1), L0_ffn_router_w, L0_ffn_w_gate, L0_ffn_w_up, L0_ffn_w_down, L0_ffn_sw_gate, L0_ffn_sw_up, L0_ffn_sw_down, L0_ffn_shared_gate_w)
    return x

_drawn_inputs = setup_inputs


def setup_inputs(seed=0):
    import zlib

    import numpy as np

    out = dict(_drawn_inputs(seed))
    spreads = {'L0_attn_br': (0.0, 0.1),
     'L0_attn_bk': (0.0, 0.1),
     'L0_attn_bv': (0.0, 0.1),
     'L0_attn_bg': (0.0, 0.1),
     'L0_attn_bo': (0.0, 0.1),
     'L0_attn_ln_g': (1.0, 0.2),
     'L0_attn_ln_b': (0.0, 0.1)}
    factors = {'L0_xattn_Wq': 30.839}
    for name, (base, spread) in spreads.items():
        noise = np.random.default_rng([zlib.crc32(name.encode()), seed]).standard_normal(out[name].shape)
        drawn = base * np.exp(spread * noise) if base else spread * noise
        out[name] = jnp.asarray(drawn.astype(out[name].dtype))
    for name, factor in factors.items():
        out[name] = (out[name] * factor).astype(out[name].dtype)
    return out
```

```python
from contextlib import ExitStack

import concourse.bass as bass
from concourse import mybir

F32 = mybir.dt.float32
F32R = mybir.dt.float32r
BF16 = mybir.dt.bfloat16
I32 = mybir.dt.int32
ALU = mybir.AluOpType
ACT = mybir.ActivationFunctionType
AX = mybir.AxisListType.X

P = 128
NEG = -1.0e30


def decoder_layer(nc, x, ctx_in, Wr, br, Wk, bk, Wv, bv, Wg, bg, Wo, bo, ln_g, ln_b,
                  maa_k, maa_v, maa_r, maa_g, time_decay, time_faaaa, Wq, Wkv, Wout,
                  router_w, w_gate, w_up, w_down, sw_gate, sw_up, sw_down, shared_gate_w, out):
    B, T, C = x.shape
    H = time_decay.shape[0]
    N = C // H
    L = ctx_in.shape[2]
    XH = 16
    XD = C // XH
    E, _, I = w_gate.shape
    SI = sw_gate.shape[1]
    KC = C // P
    GB = 4
    NG = B // GB
    GT = GB * T
    NR = E * I
    NF = NR + SI
    FB = -(-NF // P)
    FP = FB * P
    LN_EPS = 1e-5
    GN_EPS = 1e-5 * 64
    assert T == P and KC == 2 and GT == 512 and N == 8 and XD == 16 and NF - (FB - 1) * P == 64

    es = ExitStack()
    with es:
        def sb(name, shape, dt):
            return es.enter_context(nc.sbuf_tensor(name, shape, dt))

        def sem(name):
            return es.enter_context(nc.semaphore(name))

        ident = sb("ident", [P, P], F32)
        identb = sb("identb", [P, P], BF16)
        wAh = sb("wAh", [P, 5, KC, C], F32R)
        wAl = sb("wAl", [P, 5, KC, C], F32R)
        wXh = sb("wXh", [P, 2, KC, C], F32R)
        wXl = sb("wXl", [P, 2, KC, C], F32R)
        wKh = sb("wKh", [L, 2 * C], F32R)
        wKl = sb("wKl", [L, 2 * C], F32R)
        wGh = sb("wGh", [P, KC, FP], F32R)
        wGl = sb("wGl", [P, KC, FP], F32R)
        wUh = sb("wUh", [P, KC, FP], F32R)
        wUl = sb("wUl", [P, KC, FP], F32R)
        wDh = sb("wDh", [P, FB, C], F32R)
        wDl = sb("wDl", [P, FB, C], F32R)
        wRh = sb("wRh", [P, KC, E + 2], F32R)
        wRl = sb("wRl", [P, KC, E + 2], F32R)
        selC = sb("selC", [96, FP], BF16)
        selH = sb("selH", [16, 8, P], BF16)
        maskS = sb("maskS", [P, P], BF16)
        maskT = sb("maskT", [P, P], BF16)
        decay = sb("decay", [P, H, P], F32)
        bvB = sb("bvB", [P, C], F32)
        boB = sb("boB", [P, C], F32)
        cols = sb("cols", [P, 9, KC], F32)
        BR, BK, BG, LNG, LNB, MR, MK, MV, MG = range(9)
        mhalf = sb("mhalf", [P, GB], F32)
        rev = sb("rev", [P, E], F32)
        td = sb("td", [P, H], F32)
        tf = sb("tf", [P, H], F32)

        AF = sb("AF", [P, 6216], F32)
        AR = sb("AR", [P, 5120], F32R)
        dist = AF[:, 5632:5760]
        cx = AF[:, 5192:5448].rearrange("p (b l) -> p b l", b=GB)
        st = sb("st", [P, GB, 6], F32)
        mv = sb("mv", [P, GB, 2], F32)
        ve = sb("ve", [P, GB], F32)
        rstd = sb("rstd", [P, GB], F32)
        gs = sb("gs", [P, 2, 64], F32)
        gx = sb("gx", [P, 64], F32)
        gy = sb("gy", [P, 64], F32)
        gt = sb("gt", [P, 64], F32)
        nm = sb("nm", [P, 2, 8], F32)
        nmr = sb("nmr", [P, 2, 8], F32)
        nm2 = sb("nm2", [P, 2, 16], BF16)
        nmT = sb("nmT", [16, 2, P], BF16)
        rec = sb("rec", [P, 2, XH], F32)
        c3 = sb("c3", [P, GB, 96], BF16)
        cwT = AF[0:96, 5448:5704].bitcast(BF16)
        taken = [4104]

        def small(n, w):
            taken[0] += n * w
            return AF[:, taken[0] - n * w:taken[0]].rearrange("p (n w) -> p n w", n=n)

        lg = small(GB, E + 2)
        r_m = small(4, GB)
        r_a, r_o1, r_o2, r_l2 = (small(GB, E) for _ in range(4))
        r_z, r_e, r_d, r_w = (small(GB, 2) for _ in range(4))
        cw, cr, cr2 = (small(GB, E + 1) for _ in range(3))

        def tokens(a):
            return AF[:, a:a + GB * C].rearrange("p (b c) -> p b c", b=GB)

        X = tokens(0)
        XX = AF[:, 0:1024].rearrange("p (k b t) -> p k b t", k=KC, b=GB)
        tok = tokens(1024)
        R0 = 2048
        xnT = AF[:, R0:R0 + KC * GB * (T + 1)].rearrange("p (k b t) -> p k b t", k=KC, b=GB)
        xm = AF[:, R0 + 1032:R0 + 2056].rearrange("p (s n) -> p s n", s=2)
        ring = AF[:, R0:R0 + 2048].rearrange("p (s n) -> p s n", s=4)
        gact = AF[:, 4104:5128].rearrange("p (k n) -> p k n", k=KC)
        xv = AF[:, 4104:5192].rearrange("p (b h d) -> p b h d", b=GB, h=XH)
        zn = AF[:, 5192:6216].rearrange("p (q n) -> p q n", q=2)

        def hl(a, n):
            return AR[:, a:a + 2 * n].rearrange("p (s n) -> p s n", s=2)

        mix = [hl(c * 1024, 512) for c in range(2)]
        stage = [hl(2048 + n * 1024, 512) for n in range(2)]
        xT = AR[:, 0:2048].rearrange("p (s k n) -> p s k n", s=2, k=KC)
        cT = AR[0:L, 4096:5120].rearrange("p (s n) -> p s n", s=2)
        hT = [hl(2048 + s * 1024, 512) for s in range(2)]
        rbd = [AR[:, s * 1280:s * 1280 + 1024].rearrange("p (a j t) -> p a j t", a=2, j=4) for s in range(4)]
        kst = [AR[:, s * 1280 + 1024:s * 1280 + 1280].rearrange("p (a t) -> p a t", a=2) for s in range(4)]
        qbd = [AR[:, s * 1536:s * 1536 + 1024].rearrange("p (a j t) -> p a j t", a=4, j=2) for s in range(3)]
        kx = [AR[:, s * 1536 + 1024:s * 1536 + 1536].rearrange("p (a t) -> p a t", a=4) for s in range(3)]

        rD = nc.dram_tensor("r_parts", (H, 4 * N, GT), F32, kind="Internal").ap()
        kD = nc.dram_tensor("k_parts", (H, 4 * N, GT), F32, kind="Internal").ap()
        qD = nc.dram_tensor("q_parts", (XH, 4 * XD, GT), F32, kind="Internal").ap()
        xkD = nc.dram_tensor("xk_parts", (XH, 4 * XD, GT), F32, kind="Internal").ap()

        PS = [es.enter_context(nc.psum_tensor(f"bank{i}", [P, 512], F32)) for i in range(8)]

        w_in = [sem(f"w_in{i}") for i in range(2)]
        small_in = sem("small_in")
        consts = sem("consts")
        w_tp = sem("w_tp")
        w_hi = sem("w_hi")
        w_lo = sem("w_lo")
        f_in = [sem(f"f_in{i}") for i in range(2)]
        f_hi = sem("f_hi")
        f_lo = [sem("f_lo_dve"), sem("f_lo_pool")]
        tail_in = sem("tail_in")
        pads = sem("pads")
        dk_i = sem("dk_i")
        dk_a = sem("dk_a")
        dk_p = sem("dk_p")
        dk_v = sem("dk_v")

        waited_pe = sem("waited_pe")
        waited_pool = sem("waited_pool")
        waited_dve = sem("waited_dve")

        x_in = sem("x_in")
        xres_in = sem("xres_in")
        ctx_arrived = sem("ctx_arrived")
        ln_stats = sem("ln_stats")
        ln_mean = sem("ln_mean")
        ln_var = sem("ln_var")
        ln_rstd = sem("ln_rstd")
        xn_ready = sem("xn_ready")
        xn_turned = sem("xn_turned")
        xnT_act = sem("xnT_act")
        xnT_dve = sem("xnT_dve")
        edge_zero = sem("edge_zero")
        xx_ready = sem("xx_ready")
        xm_ready = sem("xm_ready")
        mix_hi = sem("mix_hi")
        mix_lo = sem("mix_lo")
        mix_used = sem("mix_used")
        rk_hi = sem("rk_hi")
        rk_lo = sem("rk_lo")
        rk_out = [sem("rk_out0"), sem("rk_out1")]
        v_ready = sem("v_ready")
        g_ready = sem("g_ready")
        z_wkv = sem("z_wkv")
        wkv_in = [sem(f"wkv_in{s}") for s in range(4)]
        s_ready = sem("s_ready")
        pt_ready = sem("pt_ready")
        y_part = sem("y_part")
        gn_sum = sem("gn_sum")
        gn_cent = sem("gn_cent")
        gn_sq = sem("gn_sq")
        gn_step = sem("gn_step")
        zn_ready = sem("zn_ready")
        zn_turned = sem("zn_turned")
        y_aff = sem("y_aff")
        y_gated = sem("y_gated")
        y_hi = sem("y_hi")
        y_lo = sem("y_lo")
        wo_ready = sem("wo_ready")
        xbo_ready = sem("xbo_ready")
        x1_ready = sem("x1_ready")
        ctx_turned = sem("ctx_turned")
        cT_hi = sem("cT_hi")
        cT_lo = sem("cT_lo")
        kp_ready = sem("kp_ready")
        vp_ready = sem("vp_ready")
        xv_one = sem("xv_one")
        xv_ready = sem("xv_ready")
        xT_hi = sem("xT_hi")
        xT_lo = sem("xT_lo")
        qp_ready = sem("qp_ready")
        qk_hi = sem("qk_hi")
        qk_lo = sem("qk_lo")
        qk_out = [sem("qk_out0"), sem("qk_out1")]
        z_x = sem("z_x")
        xa_in = [sem(f"xa_in{s}") for s in range(3)]
        sm_ready = sem("sm_ready")
        max_ready = sem("max_ready")
        nm_step = sem("nm_step")
        nm_turned = sem("nm_turned")
        nmT_ready = sem("nmT_ready")
        t_ready = sem("t_ready")
        p_ready = sem("p_ready")
        o_part = sem("o_part")
        rec_ready = sem("rec_ready")
        yo_ready = sem("yo_ready")
        yo_turned = sem("yo_turned")
        yT_hi = sem("yT_hi")
        yT_lo = sem("yT_lo")
        wout_ready = sem("wout_ready")
        x2_ready = sem("x2_ready")
        route_ready = sem("route_ready")
        r_step = sem("r_step")
        r_exp = sem("r_exp")
        c3_ready = sem("c3_ready")
        cw_turned = sem("cw_turned")
        cwT_ready = sem("cwT_ready")
        gate_ready = sem("gate_ready")
        up_ready = sem("up_ready")
        cwb_ready = sem("cwb_ready")
        silu_done = sem("silu_done")
        gu_done = sem("gu_done")
        h_done = sem("h_done")
        h_hi = sem("h_hi")
        h_lo = sem("h_lo")
        down_done = sem("down_done")
        x3_ready = sem("x3_ready")
        out_done = sem("out_done")
        PRIMED = 1
        GN_STEPS = 13
        R_EXP = 14
        R_STEPS = 25

        CONSTS = 4 + 4 + 3 + 1 + 3 * 4 + 1 + E + 1

        block = es.enter_context(nc.Block())

        SQ = [(Wr, wAh[:, 0], wAl[:, 0]), (Wk, wAh[:, 1], wAl[:, 1]), (Wv, wAh[:, 2], wAl[:, 2]),
              (Wg, wAh[:, 3], wAl[:, 3]), (Wo, wAh[:, 4], wAl[:, 4]),
              (Wq, wXh[:, 0], wXl[:, 0]), (Wout, wXh[:, 1], wXl[:, 1])]
        NSQ = len(SQ)

        def sq_raw(n):
            return AF[:, 4608 + (n % 2) * 512:5120 + (n % 2) * 512].rearrange("p (o i) -> p o i", o=KC)

        kv_raw = AF[:, 4352:4608].rearrange("p (o l) -> p o l", o=4)
        FW = []
        for hi_t, lo_t, we, ws in ((wGh, wGl, w_gate, sw_gate), (wUh, wUl, w_up, sw_up)):
            for k in range(KC):
                FW.append((hi_t[:, k, 0:NF], lo_t[:, k, 0:NF], NF,
                           [(0, NR, we[:, k * P:(k + 1) * P, :].rearrange("e p i -> p e i"), E),
                            (NR, NF, ws[k * P:(k + 1) * P, :], 0)]))
        wd = w_down.rearrange("e i h -> (e i) h")
        RB = NR // P
        SB = SI // P
        for j0, j1, src in ((0, 6, wd), (6, RB, wd), (RB, RB + SB, sw_down)):
            s0 = (j0 - (RB if j0 >= RB else 0)) * P
            FW.append((wDh[:, j0:j1, :], wDl[:, j0:j1, :], (j1 - j0) * C,
                       [(0, (j1 - j0) * C, src[s0:s0 + (j1 - j0) * P, :].rearrange("(j p) c -> p j c", p=P), j1 - j0)]))
        NFW = len(FW)
        DMA_FW = [len(f[3]) for f in FW]

        def fw_raw(n):
            raw = AF[:, (n % 2) * NF:(n % 2) * NF + FW[n][2]]
            return raw.rearrange("p (j c) -> p j c", c=C) if len(FW[n][0].shape) == 3 else raw

        def fw_in(n):
            return 16 * sum(DMA_FW[m] for m in range(n % 2, n + 1, 2))

        tail_raw = AF[0:64, 4608:4608 + C]
        rw_raw = AF[0:E + 2, 5760:5760 + C]
        SMALL = 1 + 9 + 4 + 2

        @block.sync
        def _(sp):
            sp.dma_start(kv_raw, Wkv.rearrange("(o p) l -> p o l", p=P)).then_inc(small_in, 16)
            for n, v in ((BR, br), (BK, bk), (BG, bg), (LNG, ln_g), (LNB, ln_b), (MR, maa_r), (MK, maa_k), (MV, maa_v), (MG, maa_g)):
                with nc.allow_non_contiguous_dma(reason="256 values"):
                    sp.dma_start(cols[:, n, :], v.rearrange("(k p) -> p k", p=P)).then_inc(small_in, 16)
            sp.dma_start(td[:], time_decay.partition_broadcast(P)).then_inc(small_in, 16)
            sp.dma_start(tf[:], time_faaaa.partition_broadcast(P)).then_inc(small_in, 16)
            sp.dma_start(bvB[:], bv.partition_broadcast(P)).then_inc(small_in, 16)
            sp.dma_start(boB[:], bo.partition_broadcast(P)).then_inc(small_in, 16)
            sp.wait_ge(dk_v, 1)
            sp.dma_start(rw_raw[0:E, :], router_w).then_inc(small_in, 16)
            sp.dma_start(rw_raw[E:E + 1, :], shared_gate_w.unsqueeze(0)).then_inc(small_in, 16)
            for n in range(NSQ):
                if n >= 2:
                    sp.wait_ge(w_tp, n - 1)
                sp.dma_start(sq_raw(n), SQ[n][0].rearrange("(o p) i -> p o i", p=P)).then_inc(w_in[n % 2], 16)
            for n in range(NFW):
                if n >= 2:
                    sp.wait_ge(f_hi, n - 1)
                    sp.wait_ge(f_lo[n % 2], n // 2)
                for a, b, src, parts in FW[n][3]:
                    dst = AF[:, (n % 2) * NF + a:(n % 2) * NF + b]
                    if parts:
                        dst = dst.rearrange("p (e i) -> p e i", e=parts)
                    sp.dma_start(dst, src).then_inc(f_in[n % 2], 16)
            sp.wait_ge(w_tp, NSQ + 2)
            sp.dma_start(tail_raw, sw_down[SB * P:SI, :]).then_inc(tail_in, 16)
            sp.wait_ge(f_hi, NFW + 1)
            sp.wait_ge(f_lo[0], (NFW + 1) // 2 + 1)
            sp.wait_ge(f_lo[1], NFW // 2)

            with sp.Fori(0, NG) as g:
                sp.wait_ge(xn_turned, g * 12 + PRIMED)
                sp.dma_start(tok, x[bass.ds(g * GB, GB)].rearrange("b t c -> t b c")).then_inc(x_in, 16)
                for n in range(4):
                    m = n % 2
                    sp.wait_ge(rk_hi, g * 4 + n + 1)
                    sp.wait_ge(rk_lo, g * 4 + n + 1)
                    D, order = (rD, (0, 1, 0, 1)) if n < 2 else (kD, (0, 1, 1, 0))
                    for i, part in enumerate(order):
                        sp.dma_start(D[m * 16:(m + 1) * 16, i * N:(i + 1) * N, :],
                                     stage[m][:, part, :].bitcast(F32)).then_inc(rk_out[m], 16)
                sp.wait_ge(xm_ready, g * 8 + 8)
                sp.dma_start(X, x[bass.ds(g * GB, GB)].rearrange("b t c -> t b c")).then_inc(xres_in, 16)
                for m in range(2):
                    sp.wait_ge(rk_out[m], g * 128 + 128)
                for u in range(16):
                    b, hg, s = u // 4, 2 * (u % 4), u % 4
                    if u < 4:
                        sp.wait_ge(z_wkv, g * 4 + s + 1)
                    else:
                        sp.wait_ge(s_ready, g * 32 + 2 * (u - 4) + 2)
                    t0 = b * T
                    for j in range(4):
                        src = bass.AP(rD.tensor, (hg * 4 + j) * 4 * N * GT + t0, [[GT, 4 * N], [P * GT, 2], [1, T]])
                        sp.dma_start(rbd[s][32 * j:32 * j + 32, :, j, :].bitcast(F32), src).then_inc(wkv_in[s], 16)
                    src = bass.AP(kD.tensor, hg * P * GT + t0, [[GT, P], [P * GT, 2], [1, T]])
                    sp.dma_start(kst[s].bitcast(F32), src).then_inc(wkv_in[s], 16)
                sp.wait_ge(zn_turned, g + 1)
                sp.dma_start(cx, ctx_in[bass.ds(g * GB, GB)].rearrange("b t c -> t b c")).then_inc(ctx_arrived, 16)
                for n in range(4):
                    m = n % 2
                    sp.wait_ge(qk_hi, g * 4 + n + 1)
                    sp.wait_ge(qk_lo, g * 4 + n + 1)
                    D, order = (xkD, (0, 1, 1, 0)) if n < 2 else (qD, (0, 1, 0, 1))
                    for i, part in enumerate(order):
                        sp.dma_start(D[m * 8:(m + 1) * 8, i * XD:(i + 1) * XD, :],
                                     stage[m][:, part, :].bitcast(F32)).then_inc(qk_out[m], 16)
                for m in range(2):
                    sp.wait_ge(qk_out[m], g * 128 + 128)
                for u in range(8):
                    b, h0, s = u // 2, 8 * (u % 2), u % 3
                    if u < 3:
                        sp.wait_ge(z_x, g * 3 + s + 1)
                    else:
                        sp.wait_ge(t_ready, g * 16 + 2 * (u - 3) + 2)
                    t0 = b * T
                    for j in range(2):
                        src = bass.AP(qD.tensor, (h0 + j) * 4 * XD * GT + t0, [[GT, 4 * XD], [P * GT, 4], [1, T]])
                        sp.dma_start(qbd[s][64 * j:64 * j + 64, :, j, :].bitcast(F32), src).then_inc(xa_in[s], 16)
                    src = bass.AP(xkD.tensor, h0 * 4 * XD * GT + t0, [[GT, P], [P * GT, 4], [1, T]])
                    sp.dma_start(kx[s].bitcast(F32), src).then_inc(xa_in[s], 16)
            sp.wait_ge(out_done, 16 * NG + 16 * PRIMED)

        @block.gpsimd
        def _(pool):
            done = [0]

            def made(ins):
                done[0] += 1
                ins.then_inc(consts, 1)
                pool.wait_ge(consts, done[0])

            for t in (ident, identb):
                made(pool.memset(t[:], 0.0))
                made(pool.affine_select(out=t[:], in_=t[:], compare_op=ALU.not_equal, fill=1.0, base=0,
                                        pattern=[[-1, P]], channel_multiplier=1))
            for t, sign in ((maskS, -1), (maskT, 1)):
                made(pool.memset(t[:], 0.0))
                made(pool.affine_select(out=t[:], in_=t[:], compare_op=ALU.is_ge, fill=NEG, base=0,
                                        pattern=[[sign, P]], channel_multiplier=-sign))
            made(pool.memset(selH[:], 0.0))
            for part in range(2):
                made(pool.affine_select(out=selH[:], in_=selH[:], compare_op=ALU.not_equal, fill=1.0,
                                        base=-8 * part, pattern=[[-1, 8], [0, P]], channel_multiplier=1))
            made(pool.memset(selC[:], 0.0))
            for part in range(3):
                rows = selC[32 * part:32 * part + E + 1, :]
                made(pool.memset(rows[:, 0:NF], 1.0))
                made(pool.affine_select(out=rows[:, 0:NF], in_=rows[:, 0:NF], compare_op=ALU.is_ge, fill=0.0,
                                        base=0, pattern=[[1, NF]], channel_multiplier=-I))
                made(pool.affine_select(out=rows[:, 0:NR], in_=rows[:, 0:NR], compare_op=ALU.is_ge, fill=0.0,
                                        base=I - 1, pattern=[[-1, NR]], channel_multiplier=I))
                made(pool.affine_select(out=rows[:, NR:NF], in_=rows[:, NR:NF], compare_op=ALU.is_ge, fill=0.0,
                                        base=-E, pattern=[[0, SI]], channel_multiplier=1))
            made(pool.memset(mhalf[:], -0.5))
            for n in range(E):
                made(pool.memset(rev[:, n:n + 1], float(E - n)))
            made(pool.memset(c3[:], 0.0))
            assert done[0] == CONSTS
            pool.iota(dist, pattern=[[1, P]], base=-1, channel_multiplier=-1,
                      allow_small_or_imprecise_dtypes=True).then_inc(dk_i, 1)
            pool.wait_ge(dk_i, 1)
            pool.tensor_scalar(dist, dist, 0.0, None, ALU.max).then_inc(dk_p, 1)
            pool.wait_ge(dk_a, 1 + H)
            pool.affine_select(out=decay[:], in_=decay[:], compare_op=ALU.is_gt, fill=0.0, base=0,
                               pattern=[[0, H], [1, P]], channel_multiplier=-1).then_inc(dk_p, 1)
            for t in (wGh, wGl, wUh, wUl):
                pool.memset(t[:, :, NF:FP].bitcast(F32), 0.0).then_inc(pads, 1)
            pool.wait_ge(pads, 4)
            for t in (wDh, wDl):
                pool.memset(t[64:P, FB - 1, :].bitcast(F32), 0.0).then_inc(pads, 1)
            pool.wait_ge(pads, 6)
            for n in range(1, NFW, 2):
                pool.wait_ge(f_hi, n + 1)
                hi, lo, raw = FW[n][0], FW[n][1], fw_raw(n)
                pool.tensor_tensor(lo, raw, hi.bitcast(F32), ALU.subtract).then_inc(f_lo[1], 1)

            with pool.Fori(0, NG) as g:
                def layer_rstd(s):
                    pool.wait_ge(ln_mean, g * 12 + 4 * s + 4)
                    pool.sem_inc(waited_pool, 1)
                    pool.tensor_scalar(ve[:], mv[:, :, 1], LN_EPS, None, ALU.add).then_inc(ln_var, 1)
                    pool.wait_ge(ln_var, g * 3 + s + 1)
                    pool.tensor_tensor(rstd[:], ve[:], mhalf[:], ALU.pow).then_inc(ln_rstd, 1)

                layer_rstd(0)
                pool.memset(xnT[:, :, :, 0:1], 0.0).then_inc(edge_zero, 1)
                for c in range(8):
                    pool.wait_ge(mix_hi, g * 8 + c + 1)
                    pool.tensor_tensor(mix[c % 2][:, 1, :], xm[:, c % 2, :], mix[c % 2][:, 0, :].bitcast(F32),
                                       ALU.subtract).then_inc(mix_lo, 1)
                pool.wait_ge(mix_used, g * 8 + 8)
                for m in range(2):
                    pool.wait_ge(rk_out[m], g * 128 + 128)
                pool.sem_inc(waited_pool, 1)
                for s in range(4):
                    pool.memset(AR[:, s * 1280:s * 1280 + 1024].bitcast(F32), 0.0).then_inc(z_wkv, 1)
                pool.wait_ge(xres_in, g * 16 + 16)
                pool.tensor_tensor(X, X, boB[:].unsqueeze(1).to_broadcast([P, GB, C]), ALU.add).then_inc(xbo_ready, 1)
                pool.wait_ge(y_gated, g * 2 + 2)
                pool.sem_inc(waited_pool, 1)
                pool.memset(xv[:, :, :, XD:XD + 1], 1.0).then_inc(xv_one, 1)
                layer_rstd(1)
                pool.wait_ge(qp_ready, g * 2 + 2)
                pool.wait_ge(vp_ready, g * 2 + 2)
                for m in range(2):
                    pool.wait_ge(qk_out[m], g * 128 + 128)
                pool.sem_inc(waited_pool, 1)
                for s in range(3):
                    pool.memset(AR[:, s * 1536:s * 1536 + 1024].bitcast(F32), 0.0).then_inc(z_x, 1)
                layer_rstd(2)
                for j in range(FB):
                    pool.wait_ge(h_hi, g * FB + j + 1)
                    pool.tensor_tensor(hT[j % 2][:, 1, :], ring[:, 2 + j % 2, :], hT[j % 2][:, 0, :].bitcast(F32),
                                       ALU.subtract).then_inc(h_lo, 1)

        @block.scalar
        def _(act):
            act.wait_ge(small_in, 16 * SMALL)
            act.activation(td[:], td[:], ACT.Exp).then_inc(dk_a, 1)
            act.wait_ge(dk_v, 2)
            act.wait_ge(dk_p, 1)
            for h in range(H):
                act.activation(decay[:, h, :], dist, ACT.Exp, scale=td[:, h:h + 1]).then_inc(dk_a, 1)
            for n in range(NSQ):
                act.wait_ge(w_tp, n + 1)
                act.activation(SQ[n][1], PS[n % 2][:, :].rearrange("p (i o) -> p i o", i=KC), ACT.Copy).then_inc(w_hi, 1)
            act.wait_ge(w_tp, NSQ + 1)
            act.activation(wKh[:], PS[NSQ % 2][0:L, :], ACT.Copy).then_inc(w_hi, 1)
            act.wait_ge(w_tp, NSQ + 2)
            act.activation(wRh[:], PS[(NSQ + 1) % 2][:, 0:KC * (E + 2)].rearrange("p (k e) -> p k e", k=KC), ACT.Copy).then_inc(w_hi, 1)
            for n in range(NFW):
                act.wait_ge(f_in[n % 2], fw_in(n))
                act.activation(FW[n][0], fw_raw(n), ACT.Copy).then_inc(f_hi, 1)
            act.wait_ge(tail_in, 16)
            act.activation(wDh[0:64, FB - 1, :], tail_raw, ACT.Copy).then_inc(f_hi, 1)

            act.sem_inc(out_done, 16 * PRIMED)

            with act.Fori(0, NG) as g:
                act.wait_ge(xn_turned, g * 12 + 4 + PRIMED)
                act.activation(xnT[:, 0, :, 1:T + 1], PS[6][:, :].rearrange("p (b t) -> p b t", b=GB), ACT.Copy).then_inc(xnT_act, 1)

                def mix_part(c):
                    act.wait_ge(xm_ready, g * 8 + c + 1)
                    if c >= 2:
                        act.wait_ge(mix_used, g * 8 + c - 1)
                    act.activation(mix[c % 2][:, 0, :], xm[:, c % 2, :], ACT.Copy).then_inc(mix_hi, 1)

                def rk_part(n):
                    i, m = n // 2, n % 2
                    act.wait_ge(mix_used, g * 8 + 2 * i + 2)
                    if i:
                        act.wait_ge(rk_out[m], g * 128 + 64)
                    act.activation(stage[m][:, 0, :], PS[2 * i + m][:, :], ACT.Identity,
                                   bias=cols[:, BR + i, m:m + 1]).then_inc(rk_hi, 1)

                for c in range(4):
                    mix_part(c)
                rk_part(0)
                rk_part(1)
                mix_part(4)
                mix_part(5)
                rk_part(2)
                rk_part(3)
                mix_part(6)
                mix_part(7)
                act.wait_ge(mix_used, g * 8 + 8)
                for m in range(2):
                    act.activation(gact[:, m, :], PS[2 + m][:, :], ACT.Silu, bias=cols[:, BG, m:m + 1]).then_inc(g_ready, 1)
                for q in range(2):
                    act.wait_ge(gn_cent, g * 2 + q + 1)
                    act.activation(PS[6 + q][:, :], zn[:, q, :], ACT.Square).then_inc(gn_sq, 1)
                act.wait_ge(zn_turned, g + 1)
                for m in range(2):
                    act.activation(ring[:, m, :], PS[6 + m][:, :], ACT.Identity, bias=cols[:, LNB, m:m + 1],
                                   scale=cols[:, LNG, m:m + 1]).then_inc(y_aff, 1)
                for m in range(2):
                    act.wait_ge(y_gated, g * 2 + m + 1)
                    act.activation(xT[:, 0, m, :], ring[:, 2 + m, :], ACT.Copy).then_inc(y_hi, 1)
                act.wait_ge(ctx_turned, g + 1)
                act.activation(cT[:, 0, :], PS[2][0:L, :], ACT.Copy).then_inc(cT_hi, 1)
                for m in range(2):
                    act.wait_ge(kp_ready, g * 2 + m + 1)
                    act.activation(stage[m][:, 0, :], PS[3 + m][:, :], ACT.Copy).then_inc(qk_hi, 1)
                act.wait_ge(xn_turned, g * 12 + 8 + PRIMED)
                for k in range(2):
                    act.activation(xT[:, 0, k, :], PS[6 + k][:, :], ACT.Copy).then_inc(xT_hi, 1)
                for m in range(2):
                    act.wait_ge(qp_ready, g * 2 + m + 1)
                    act.wait_ge(qk_out[m], g * 128 + 64)
                    act.activation(stage[m][:, 0, :], PS[m][:, :], ACT.Copy, scale=float(XD) ** -0.5).then_inc(qk_hi, 1)

                def turned_max(u):
                    act.wait_ge(nm_turned, g * 8 + u + 1)
                    act.activation(nmT[:, u % 2, :], PS[6 + u % 2][:, :].bitcast(BF16)[0:16, 0:P], ACT.Copy).then_inc(nmT_ready, 1)

                def exps(u):
                    for qd in (2 * u, 2 * u + 1):
                        act.wait_ge(t_ready, g * 16 + qd + 1)
                        if qd >= 4:
                            act.wait_ge(o_part, g * 16 + qd - 3)
                        act.activation(ring[:, qd % 4, :], PS[2 + qd % 2][:, :], ACT.Exp).then_inc(p_ready, 1)

                turned_max(0)
                for u in range(8):
                    exps(u)
                    if u + 1 < 8:
                        turned_max(u + 1)
                act.wait_ge(yo_turned, g + 1)
                for k in range(2):
                    act.activation(xT[:, 0, k, :], PS[6 + k][:, :], ACT.Copy).then_inc(yT_hi, 1)
                act.wait_ge(xn_turned, g * 12 + 12 + PRIMED)
                for k in range(2):
                    act.activation(xT[:, 0, k, :], PS[6 + k][:, :], ACT.Copy).then_inc(xT_hi, 1)
                act.wait_ge(r_step, g * R_STEPS + R_EXP)
                act.activation(r_e[:], r_z[:], ACT.Exp).then_inc(r_exp, 1)

                def silu(j):
                    act.wait_ge(gate_ready, g * FB + j + 1)
                    if j >= 2:
                        act.wait_ge(gu_done, g * FB + j - 1)
                    act.activation(ring[:, j % 2, :], PS[j % 2][:, :], ACT.Silu).then_inc(silu_done, 1)

                silu(0)
                silu(1)
                act.wait_ge(cw_turned, g + 1)
                act.activation(cwT, PS[5][:, :].bitcast(BF16)[0:96, 0:GT], ACT.Copy).then_inc(cwT_ready, 1)
                for j in range(FB):
                    act.wait_ge(h_done, g * FB + j + 1)
                    if j >= 2:
                        act.wait_ge(down_done, g * FB + j - 1)
                    act.activation(hT[j % 2][:, 0, :], ring[:, 2 + j % 2, :], ACT.Copy).then_inc(h_hi, 1)
                    if j + 2 < FB:
                        silu(j + 2)
                act.wait_ge(x3_ready, g * 2 + 2 + PRIMED)
                act.dma_start(out[bass.ds(g * GB, GB)].rearrange("b t c -> t b c"), X).then_inc(out_done, 16)

        @block.tensor
        def _(pe):
            mm = nc.tensor.matmul
            pe.wait_ge(consts, 4)
            for n in range(NSQ):
                pe.wait_ge(w_in[n % 2], 16 * (n // 2 + 1))
                if n >= 2:
                    pe.wait_ge(w_lo, n - 1)
                for i in range(KC):
                    for o in range(KC):
                        last = nc.tensor.transpose(PS[n % 2][:, i * C + o * P:i * C + (o + 1) * P],
                                                   sq_raw(n)[:, o, i * P:(i + 1) * P], ident[:])
                last.then_inc(w_tp, 1)
            pe.wait_ge(small_in, 16 * SMALL)
            pe.wait_ge(w_lo, NSQ - 1)
            for o in range(4):
                last = nc.tensor.transpose(PS[NSQ % 2][0:L, o * P:(o + 1) * P], kv_raw[:, o, :], ident[:])
            last.then_inc(w_tp, 1)
            pe.wait_ge(w_lo, NSQ)
            for k in range(KC):
                last = nc.tensor.transpose(PS[(NSQ + 1) % 2][:, k * (E + 2):(k + 1) * (E + 2)], rw_raw[:, k * P:(k + 1) * P],
                                           ident[0:E + 2, 0:E + 2])
            last.then_inc(w_tp, 1)
            pe.wait_ge(w_lo, NSQ + 2)
            pe.wait_ge(f_lo[0], (NFW + 1) // 2 + 1)
            pe.wait_ge(f_lo[1], NFW // 2)
            pe.wait_ge(pads, 6)

            pe.sem_inc(xn_turned, PRIMED)

            with pe.Fori(0, NG) as g:
                def three(out_ap, wh, wl, xh, xl, start, stop, skip=False):
                    mm(out_ap, wh, xh, start=start, stop=False, skip_group_check=skip)
                    mm(out_ap, wh, xl, start=False, stop=False, skip_group_check=skip)
                    return mm(out_ap, wl, xh, start=False, stop=stop, skip_group_check=skip)

                def turn_norm(s):
                    for b in range(GB):
                        pe.wait_ge(xn_ready, g * 12 + 4 * s + b + 1)
                        for k in range(KC):
                            last = nc.tensor.transpose(PS[6 + k][:, b * T:(b + 1) * T], tok[:, b, k * P:(k + 1) * P], ident[:])
                        last.then_inc(xn_turned, 1)

                pe.wait_ge(x3_ready, g * 2 + PRIMED)
                turn_norm(0)
                for i in range(4):
                    base = 2 * (i % 2)
                    if i >= 2:
                        pe.wait_ge(rk_lo, g * 4 + 2 * (i - 1))
                    for k in range(KC):
                        c = 2 * i + k
                        pe.wait_ge(mix_hi, g * 8 + c + 1)
                        pe.wait_ge(mix_lo, g * 8 + c + 1)
                        hi, lo = mix[c % 2][:, 0, :], mix[c % 2][:, 1, :]
                        if i == 2:
                            for b in range(GB):
                                o = PS[base + b // 2][:, (b % 2) * C:(b % 2 + 1) * C]
                                t = slice(b * T, (b + 1) * T)
                                first = k == 0 and b % 2 == 0
                                mm(o, hi[:, t], wAh[:, i, k, :], start=first, stop=False, skip_group_check=True)
                                mm(o, hi[:, t], wAl[:, i, k, :], start=False, stop=False, skip_group_check=True)
                                last = mm(o, lo[:, t], wAh[:, i, k, :], start=False, stop=k == 1, skip_group_check=True)
                        else:
                            for m in range(2):
                                ms = slice(m * P, (m + 1) * P)
                                last = three(PS[base + m][:, :], wAh[:, i, k, ms], wAl[:, i, k, ms], hi, lo, k == 0, k == 1)
                        last.then_inc(mix_used, 1)

                def scores(p):
                    u, a = p // 2, p % 2
                    s = u % 4
                    if p == 0:
                        pe.wait_ge(v_ready, g * 2 + 2)
                        pe.wait_ge(g_ready, g * 2 + 2)
                    if p >= 4:
                        pe.wait_ge(pt_ready, g * 32 + p - 3)
                    if a == 0:
                        pe.wait_ge(wkv_in[s], g * 320 + 80 * (u // 4) + 80)
                    mm(PS[p % 4][:, :], kst[s][:, a, :], rbd[s][:, a, :, :], start=True, stop=True).then_inc(s_ready, 1)

                def mixed(p):
                    u, a = p // 2, p % 2
                    b, hg = u // 4, 2 * (u % 4) + a
                    pe.wait_ge(pt_ready, g * 32 + p + 1)
                    for j in range(4):
                        h = hg * 4 + j
                        o = (b % 2) * C + h * N
                        last = mm(PS[4 + b // 2][:, o:o + N], ring[:, p % 4, j * T:(j + 1) * T], tok[:, b, h * N:(h + 1) * N],
                                  start=True, stop=True)
                    last.then_inc(y_part, 1)

                for p in range(32):
                    scores(p)
                    if p >= 2:
                        mixed(p - 2)
                mixed(30)
                mixed(31)
                pe.wait_ge(zn_ready, g * 2 + 2)
                for b in range(GB):
                    for k in range(KC):
                        last = nc.tensor.transpose(PS[6 + k][:, b * T:(b + 1) * T],
                                                   zn[:, b // 2, (b % 2) * C + k * P:(b % 2) * C + (k + 1) * P], ident[:])
                last.then_inc(zn_turned, 1)

                def out_projection(wh, wl, done, hi_ready, lo_ready):
                    for b in range(GB):
                        t = slice(b * T, (b + 1) * T)
                        o = PS[b // 2][:, (b % 2) * C:(b % 2 + 1) * C]
                        for k in range(KC):
                            if b == 0:
                                pe.wait_ge(hi_ready, g * 2 + k + 1)
                                pe.wait_ge(lo_ready, g * 2 + k + 1)
                            mm(o, xT[:, 0, k, t], wh[:, k, :], start=(k == 0 and b % 2 == 0), stop=False, skip_group_check=True)
                            mm(o, xT[:, 0, k, t], wl[:, k, :], start=False, stop=False, skip_group_check=True)
                            last = mm(o, xT[:, 1, k, t], wh[:, k, :], start=False, stop=k == 1, skip_group_check=True)
                        if b % 2:
                            last.then_inc(done, 1)

                out_projection(wAh[:, 4], wAl[:, 4], wo_ready, y_hi, y_lo)

                pe.wait_ge(ctx_arrived, g * 16 + 16)
                pe.sem_inc(waited_pe, 1)
                for b in range(GB):
                    last = nc.tensor.transpose(PS[2][0:L, b * T:(b + 1) * T], cx[:, b, :], ident[:])
                last.then_inc(ctx_turned, 1)
                pe.wait_ge(cT_hi, g + 1)
                pe.wait_ge(cT_lo, g + 1)
                for m in range(2):
                    ms = slice(m * P, (m + 1) * P)
                    three(PS[3 + m][:, :], wKh[:, ms], wKl[:, ms], cT[:, 0, :], cT[:, 1, :], True, True).then_inc(kp_ready, 1)
                for b in range(GB):
                    o = PS[5 if b < 2 else 2][:, (b % 2) * C:(b % 2 + 1) * C]
                    t = slice(b * T, (b + 1) * T)
                    mm(o, cT[:, 0, t], wKh[:, C:2 * C], start=b % 2 == 0, stop=False, skip_group_check=True)
                    mm(o, cT[:, 0, t], wKl[:, C:2 * C], start=False, stop=False, skip_group_check=True)
                    last = mm(o, cT[:, 1, t], wKh[:, C:2 * C], start=False, stop=True, skip_group_check=True)
                    if b % 2:
                        last.then_inc(vp_ready, 1)
                turn_norm(1)
                for m in range(2):
                    ms = slice(m * P, (m + 1) * P)
                    for k in range(KC):
                        if m == 0:
                            pe.wait_ge(xT_hi, g * 4 + k + 1)
                            pe.wait_ge(xT_lo, g * 4 + k + 1)
                        last = three(PS[m][:, :], wXh[:, 0, k, ms], wXl[:, 0, k, ms], xT[:, 0, k, :], xT[:, 1, k, :], k == 0, k == 1)
                    last.then_inc(qp_ready, 1)

                def query_scores(u):
                    s = u % 3
                    pe.wait_ge(xa_in[s], g * (48 * len(range(s, 8, 3))) + 48 * (u // 3) + 48)
                    for qd in (2 * u, 2 * u + 1):
                        bank = PS[qd % 2]
                        if qd >= 2:
                            pe.wait_ge(max_ready, g * 16 + qd - 1)
                        else:
                            pe.wait_ge(qk_lo, g * 4 + 4)
                        mm(bank[:, :], identb[:], maskS[:].unsqueeze(1).to_broadcast([P, 4, P]), start=True, stop=False,
                           skip_group_check=True)
                        for i in range(4):
                            a, j = 2 * (qd % 2) + i // 2, i % 2
                            last = mm(bank[:, i * P:(i + 1) * P], qbd[s][:, a, j, :], kx[s][:, a, :], start=False,
                                      stop=i == 3, skip_group_check=True)
                        last.then_inc(sm_ready, 1)

                def turn_max(u):
                    pe.wait_ge(nm_step, g * 24 + 3 * u + 3)
                    if u >= 2:
                        pe.wait_ge(nmT_ready, g * 8 + u - 1)
                    nc.tensor.transpose(PS[6 + u % 2][:, :].bitcast(BF16)[0:16, 0:P], nm2[:, u % 2, :], identb[:]).then_inc(nm_turned, 1)

                def key_scores(u):
                    s = u % 3
                    pe.wait_ge(nmT_ready, g * 8 + u + 1)
                    for qd in (2 * u, 2 * u + 1):
                        bank = PS[2 + qd % 2]
                        if qd >= 2:
                            pe.wait_ge(p_ready, g * 16 + qd - 1)
                        else:
                            pe.wait_ge(xv_ready, g * 2 + 2)
                        mm(bank[:, :], identb[:], maskT[:].unsqueeze(1).to_broadcast([P, 4, P]), start=True, stop=False,
                           skip_group_check=True)
                        for i in range(2):
                            a = 2 * (qd % 2) + i
                            mm(bank[:, i * 256:(i + 1) * 256], kx[s][:, a, :], qbd[s][:, a, :, :], start=False, stop=False,
                               skip_group_check=True)
                        for i in range(4):
                            last = mm(bank[:, i * P:(i + 1) * P], selH[:, 4 * (qd % 2) + i, :], nmT[:, u % 2, :], start=False,
                                      stop=i == 3, skip_group_check=True)
                        last.then_inc(t_ready, 1)

                def attend(u):
                    for qd in (2 * u, 2 * u + 1):
                        b = qd // 4
                        if qd % 4 == 0:
                            if b >= 2:
                                pe.wait_ge(yo_ready, g * 4 + b - 1)
                            else:
                                pe.wait_ge(xv_ready, g * 2 + 2)
                        pe.wait_ge(p_ready, g * 16 + qd + 1)
                        for i in range(4):
                            h = 4 * (qd % 4) + i
                            last = mm(PS[4 + b % 2][:, h * (XD + 1):(h + 1) * (XD + 1)], ring[:, qd % 4, i * T:(i + 1) * T],
                                      xv[:, b, h, :], start=True, stop=True)
                        last.then_inc(o_part, 1)

                query_scores(0)
                turn_max(0)
                for u in range(8):
                    if u + 1 < 8:
                        query_scores(u + 1)
                    key_scores(u)
                    if u >= 1:
                        attend(u - 1)
                    if u + 1 < 8:
                        turn_max(u + 1)
                attend(7)
                pe.wait_ge(nmT_ready, g * 8 + 8)
                for b in range(GB):
                    pe.wait_ge(yo_ready, g * 4 + b + 1)
                    for k in range(KC):
                        last = nc.tensor.transpose(PS[6 + k][:, b * T:(b + 1) * T], tok[:, b, k * P:(k + 1) * P], ident[:])
                last.then_inc(yo_turned, 1)
                out_projection(wXh[:, 1], wXl[:, 1], wout_ready, yT_hi, yT_lo)

                turn_norm(2)
                for b in range(GB):
                    t = slice(b * T, (b + 1) * T)
                    o = PS[4][:, b * (E + 2):(b + 1) * (E + 2)]
                    for k in range(KC):
                        if b == 0:
                            pe.wait_ge(xT_hi, g * 4 + 2 + k + 1)
                            pe.wait_ge(xT_lo, g * 4 + 2 + k + 1)
                        mm(o, xT[:, 0, k, t], wRh[:, k, :], start=(k == 0 and b == 0), stop=False, skip_group_check=True)
                        mm(o, xT[:, 0, k, t], wRl[:, k, :], start=False, stop=False, skip_group_check=True)
                        last = mm(o, xT[:, 1, k, t], wRh[:, k, :], start=False, stop=k == 1, skip_group_check=True)
                last.then_inc(route_ready, 1)

                def gate_up(j):
                    js = slice(j * P, (j + 1) * P)
                    for bank, wh, wl, ready, used in ((PS[j % 2], wGh, wGl, gate_ready, silu_done),
                                                      (PS[2 + j % 2], wUh, wUl, up_ready, gu_done)):
                        if j >= 2:
                            pe.wait_ge(used, g * FB + j - 1)
                        for k in range(KC):
                            last = three(bank[:, :], wh[:, k, js], wl[:, k, js], xT[:, 0, k, :], xT[:, 1, k, :], k == 0, k == 1)
                        last.then_inc(ready, 1)

                def combine(j):
                    if j >= 2:
                        pe.wait_ge(h_done, g * FB + j - 1)
                    else:
                        pe.wait_ge(cwT_ready, g + 1)
                    mm(PS[4 + j % 2][:, :], selC[:, j * P:(j + 1) * P], cwT, start=True, stop=True).then_inc(cwb_ready, 1)

                def down(j):
                    pe.wait_ge(h_hi, g * FB + j + 1)
                    pe.wait_ge(h_lo, g * FB + j + 1)
                    hi, lo = hT[j % 2][:, 0, :], hT[j % 2][:, 1, :]
                    for b in range(GB):
                        t = slice(b * T, (b + 1) * T)
                        o = PS[6 + b // 2][:, (b % 2) * C:(b % 2 + 1) * C]
                        mm(o, hi[:, t], wDh[:, j, :], start=(j == 0 and b % 2 == 0), stop=False, skip_group_check=True)
                        mm(o, hi[:, t], wDl[:, j, :], start=False, stop=False, skip_group_check=True)
                        last = mm(o, lo[:, t], wDh[:, j, :], start=False, stop=j == FB - 1, skip_group_check=True)
                    last.then_inc(down_done, 1)

                gate_up(0)
                gate_up(1)
                pe.wait_ge(c3_ready, g + 1)
                for b in range(GB):
                    last = nc.tensor.transpose(PS[5][:, :].bitcast(BF16)[0:96, b * T:(b + 1) * T], c3[:, b, :], identb[:])
                last.then_inc(cw_turned, 1)
                combine(0)
                combine(1)
                for j in range(2, FB):
                    gate_up(j)
                    combine(j)
                    down(j - 2)
                down(FB - 2)
                down(FB - 1)

        @block.vector
        def _(dve):
            tt, ts, stt = nc.vector.tensor_tensor, nc.vector.tensor_scalar, nc.vector.scalar_tensor_tensor
            nc.vector.memset(rw_raw, 0.0).then_inc(dk_v, 1)
            dve.wait_ge(dk_a, 1)
            ts(td[:], td[:], 1.0e30, -1.0, ALU.min, ALU.mult).then_inc(dk_v, 1)
            for n in range(NSQ):
                dve.wait_ge(w_hi, n + 1)
                tt(SQ[n][2], PS[n % 2][:, :].rearrange("p (i o) -> p i o", i=KC), SQ[n][1].bitcast(F32), ALU.subtract).then_inc(w_lo, 1)
            dve.wait_ge(w_hi, NSQ + 1)
            tt(wKl[:], PS[NSQ % 2][0:L, :], wKh[:].bitcast(F32), ALU.subtract).then_inc(w_lo, 1)
            dve.wait_ge(w_hi, NSQ + 2)
            tt(wRl[:], PS[(NSQ + 1) % 2][:, 0:KC * (E + 2)].rearrange("p (k e) -> p k e", k=KC), wRh[:].bitcast(F32),
               ALU.subtract).then_inc(w_lo, 1)
            dve.wait_ge(dk_p, 2)
            for h in range(H):
                stt(decay[:, h, :], ident[:], tf[:, h:h + 1], decay[:, h, :], ALU.mult, ALU.add).then_inc(dk_v, 1)
            for n in range(0, NFW, 2):
                dve.wait_ge(f_hi, n + 1)
                tt(FW[n][1], fw_raw(n), FW[n][0].bitcast(F32), ALU.subtract).then_inc(f_lo[0], 1)
            dve.wait_ge(f_hi, NFW + 1)
            tt(wDl[0:64, FB - 1, :], tail_raw, wDh[0:64, FB - 1, :].bitcast(F32), ALU.subtract).then_inc(f_lo[0], 1)
            dve.wait_ge(dk_v, 2 + H)
            dve.wait_ge(consts, CONSTS)

            def pair(bank):
                return bank[:, :].rearrange("p (b c) -> p b c", b=2)

            dve.sem_inc(x3_ready, PRIMED)

            with dve.Fori(0, NG) as g:
                def layer_stats(s, src, lo=0, hi=GB):
                    for b in range(GB):
                        nc.vector.bn_stats(st[:, b, :], src[:, b, :]).then_inc(ln_stats, 1)
                    dve.wait_ge(ln_stats, g * 12 + 4 * s + GB)
                    dve.sem_inc(waited_dve, 1)
                    for b in range(GB):
                        nc.vector.bn_aggr(mv[:, b, :], st[:, b, :]).then_inc(ln_mean, 1)

                def layer_apply(s, src):
                    dve.wait_ge(ln_rstd, g * 3 + s + 1)
                    for b in range(GB):
                        ts(tok[:, b, :], src[:, b, :], mv[:, b, 0:1], rstd[:, b:b + 1], ALU.subtract, ALU.mult).then_inc(xn_ready, 1)

                dve.wait_ge(x_in, g * 16 + 16)
                layer_stats(0, tok)
                layer_apply(0, tok)
                dve.wait_ge(xn_turned, g * 12 + 4 + PRIMED)
                nc.vector.tensor_copy(xnT[:, 1, :, 1:T + 1], PS[7][:, :].rearrange("p (b t) -> p b t", b=GB)).then_inc(xnT_dve, 1)
                dve.wait_ge(out_done, g * 16 + 16 * PRIMED)
                dve.wait_ge(edge_zero, g + 1)
                dve.wait_ge(xnT_act, g + 1)
                tt(XX[:, 0], xnT[:, 0, :, 0:T], xnT[:, 0, :, 1:T + 1], ALU.subtract).then_inc(xx_ready, 1)
                dve.wait_ge(xnT_dve, g + 1)
                tt(XX[:, 1], xnT[:, 1, :, 0:T], xnT[:, 1, :, 1:T + 1], ALU.subtract).then_inc(xx_ready, 1)

                def mixed_input(c):
                    i, k = c // 2, c % 2
                    if c < 2:
                        dve.wait_ge(xx_ready, g * 2 + c + 1)
                    else:
                        dve.wait_ge(mix_lo, g * 8 + c - 1)
                    stt(xm[:, c % 2, :].rearrange("p (b t) -> p b t", b=GB), XX[:, k], cols[:, MR + i, k:k + 1],
                        xnT[:, k, :, 1:T + 1], ALU.mult, ALU.add).then_inc(xm_ready, 1)

                def rk_part(n):
                    i, m = n // 2, n % 2
                    dve.wait_ge(rk_hi, g * 4 + n + 1)
                    stt(stage[m][:, 1, :], PS[2 * i + m][:, :], cols[:, BR + i, m:m + 1], stage[m][:, 0, :].bitcast(F32),
                        ALU.add, ALU.subtract).then_inc(rk_lo, 1)

                for c in range(4):
                    mixed_input(c)
                rk_part(0)
                rk_part(1)
                mixed_input(4)
                mixed_input(5)
                rk_part(2)
                rk_part(3)
                mixed_input(6)
                mixed_input(7)
                dve.wait_ge(mix_used, g * 8 + 6)
                for q in range(2):
                    tt(tok[:, 2 * q:2 * q + 2, :], pair(PS[q]), bvB[:].unsqueeze(1).to_broadcast([P, 2, C]), ALU.add).then_inc(v_ready, 1)

                def weigh(p):
                    hg = 2 * ((p // 2) % 4) + p % 2
                    dve.wait_ge(s_ready, g * 32 + p + 1)
                    if p >= 4:
                        dve.wait_ge(y_part, g * 32 + p - 3)
                    tt(ring[:, p % 4, :].rearrange("p (j t) -> p j t", j=4), PS[p % 4][:, :].rearrange("p (j t) -> p j t", j=4),
                       decay[:, 4 * hg:4 * hg + 4, :], ALU.mult).then_inc(pt_ready, 1)

                def group_norm(q):
                    steps = [0]

                    def step(ins):
                        steps[0] += 1
                        ins.then_inc(gn_step, 1)
                        dve.wait_ge(gn_step, g * (2 * GN_STEPS) + q * GN_STEPS + steps[0])

                    heads = PS[4 + q][:, :].rearrange("p (h n) -> p h n", n=N)
                    zh = zn[:, q, :].rearrange("p (h n) -> p h n", n=N)
                    dve.wait_ge(y_part, g * 32 + 16 * (q + 1))
                    nc.vector.tensor_reduce(gs[:, 0, :], heads, AX, ALU.add).then_inc(gn_sum, 1)
                    dve.wait_ge(gn_sum, g * 2 + q + 1)
                    stt(zh, gs[:, 0, :].unsqueeze(2).to_broadcast([P, 64, N]), -1.0 / N, heads, ALU.mult, ALU.add).then_inc(gn_cent, 1)
                    dve.wait_ge(gn_sq, g * 2 + q + 1)
                    step(nc.vector.tensor_reduce(gs[:, 1, :], PS[6 + q][:, :].rearrange("p (h n) -> p h n", n=N), AX, ALU.add))
                    step(ts(gx[:], gs[:, 1, :], 1.0 / N, GN_EPS, ALU.mult, ALU.add))
                    step(ts(gy[:].bitcast(I32), gx[:].bitcast(I32), 1, None, ALU.logical_shift_right))
                    step(ts(gy[:].bitcast(I32), gy[:].bitcast(I32), -1.0, float(0x5F3759DF), ALU.mult, ALU.add))
                    for _ in range(3):
                        step(stt(gt[:], gy[:], -0.5, gx[:], ALU.mult, ALU.mult))
                        step(tt(gt[:], gt[:], gy[:], ALU.mult))
                        step(stt(gy[:], gt[:], 1.5, gy[:], ALU.add, ALU.mult))
                    assert steps[0] == GN_STEPS
                    tt(zh, zh, gy[:].unsqueeze(2).to_broadcast([P, 64, N]), ALU.mult).then_inc(zn_ready, 1)

                for p in range(32):
                    weigh(p)
                    if p == 20:
                        group_norm(0)
                group_norm(1)
                for m in range(2):
                    dve.wait_ge(y_aff, g * 2 + m + 1)
                    tt(ring[:, 2 + m, :], ring[:, m, :], gact[:, m, :], ALU.mult).then_inc(y_gated, 1)
                for m in range(2):
                    dve.wait_ge(y_hi, g * 2 + m + 1)
                    tt(xT[:, 1, m, :], ring[:, 2 + m, :], xT[:, 0, m, :].bitcast(F32), ALU.subtract).then_inc(y_lo, 1)
                dve.wait_ge(xbo_ready, g + 1)
                for q in range(2):
                    dve.wait_ge(wo_ready, g * 2 + q + 1)
                    tt(X[:, 2 * q:2 * q + 2, :], pair(PS[q]), X[:, 2 * q:2 * q + 2, :], ALU.add).then_inc(x1_ready, 1)

                dve.wait_ge(cT_hi, g + 1)
                tt(cT[:, 1, :], PS[2][0:L, :], cT[:, 0, :].bitcast(F32), ALU.subtract).then_inc(cT_lo, 1)
                dve.wait_ge(x1_ready, g * 2 + 2)
                layer_stats(1, X)
                for m in range(2):
                    dve.wait_ge(qk_hi, g * 4 + m + 1)
                    tt(stage[m][:, 1, :], PS[3 + m][:, :], stage[m][:, 0, :].bitcast(F32), ALU.subtract).then_inc(qk_lo, 1)
                dve.wait_ge(xv_one, g + 1)
                for q in range(2):
                    dve.wait_ge(vp_ready, g * 2 + q + 1)
                    nc.vector.tensor_copy(xv[:, 2 * q:2 * q + 2, :, 0:XD],
                                          PS[5 if q == 0 else 2][:, :].rearrange("p (b h d) -> p b h d", b=2, h=XH)).then_inc(xv_ready, 1)
                layer_apply(1, X)

                def norm_lo(s, done):
                    for k in range(2):
                        dve.wait_ge(xT_hi, g * 4 + 2 * (s - 1) + k + 1)
                        tt(xT[:, 1, k, :], PS[6 + k][:, :], xT[:, 0, k, :].bitcast(F32), ALU.subtract).then_inc(done, 1)

                norm_lo(1, xT_lo)
                for m in range(2):
                    dve.wait_ge(qk_hi, g * 4 + 2 + m + 1)
                    stt(stage[m][:, 1, :], PS[m][:, :], float(XD) ** -0.5, stage[m][:, 0, :].bitcast(F32), ALU.mult,
                        ALU.subtract).then_inc(qk_lo, 1)

                def maxima(u):
                    if u >= 2:
                        dve.wait_ge(nm_turned, g * 8 + u - 1)
                    for qd in (2 * u, 2 * u + 1):
                        dve.wait_ge(sm_ready, g * 16 + qd + 1)
                        nc.vector.tensor_reduce(nm[:, u % 2, 4 * (qd % 2):4 * (qd % 2) + 4],
                                                PS[qd % 2][:, :].rearrange("p (h t) -> p h t", h=4), AX, ALU.max,
                                                negate=True).then_inc(max_ready, 1)
                    dve.wait_ge(max_ready, g * 16 + 2 * u + 2)
                    nc.vector.tensor_copy(nm2[:, u % 2, 0:8], nm[:, u % 2, :]).then_inc(nm_step, 1)
                    dve.wait_ge(nm_step, g * 24 + 3 * u + 1)
                    tt(nmr[:, u % 2, :], nm[:, u % 2, :], nm2[:, u % 2, 0:8], ALU.subtract).then_inc(nm_step, 1)
                    dve.wait_ge(nm_step, g * 24 + 3 * u + 2)
                    nc.vector.tensor_copy(nm2[:, u % 2, 8:16], nmr[:, u % 2, :]).then_inc(nm_step, 1)

                def attended(b):
                    dve.wait_ge(o_part, g * 16 + 4 * b + 4)
                    o = PS[4 + b % 2][:, 0:XH * (XD + 1)].rearrange("p (h d) -> p h d", h=XH)
                    nc.vector.reciprocal(rec[:, b % 2, :], o[:, :, XD]).then_inc(rec_ready, 1)
                    dve.wait_ge(rec_ready, g * 4 + b + 1)
                    tt(tok[:, b, :].rearrange("p (h d) -> p h d", h=XH), o[:, :, 0:XD], rec[:, b % 2, :].unsqueeze(2).to_broadcast([P, XH, XD]),
                       ALU.mult).then_inc(yo_ready, 1)

                for u in range(8):
                    maxima(u)
                    if u >= 3 and u % 2 == 1:
                        attended((u - 3) // 2)
                attended(3)
                for k in range(2):
                    dve.wait_ge(yT_hi, g * 2 + k + 1)
                    tt(xT[:, 1, k, :], PS[6 + k][:, :], xT[:, 0, k, :].bitcast(F32), ALU.subtract).then_inc(yT_lo, 1)
                for q in range(2):
                    dve.wait_ge(wout_ready, g * 2 + q + 1)
                    tt(X[:, 2 * q:2 * q + 2, :], pair(PS[q]), X[:, 2 * q:2 * q + 2, :], ALU.add).then_inc(x2_ready, 1)

                dve.wait_ge(x2_ready, g * 2 + 2)
                layer_stats(2, X)
                layer_apply(2, X)
                norm_lo(2, xT_lo)

                steps = [0]

                def step(ins):
                    steps[0] += 1
                    ins.then_inc(r_step, 1)
                    dve.wait_ge(r_step, g * R_STEPS + steps[0])

                def over(a, n):
                    return a.unsqueeze(2).to_broadcast([P, GB, n])

                revb = rev[:].unsqueeze(1).to_broadcast([P, GB, E])
                dve.wait_ge(route_ready, g + 1)
                step(nc.vector.tensor_copy(lg, PS[4][:, 0:GB * (E + 2)].rearrange("p (b e) -> p b e", b=GB)))
                logits = lg[:, :, 0:E]
                for o, src, m in ((r_o1, logits, 0), (r_o2, r_l2, 2)):
                    step(nc.vector.tensor_reduce(r_m[:, m, :], src, AX, ALU.max))
                    step(tt(r_a, src, over(r_m[:, m, :], E), ALU.is_equal))
                    step(tt(r_a, r_a, revb, ALU.mult))
                    step(nc.vector.tensor_reduce(r_m[:, m + 1, :], r_a, AX, ALU.max))
                    step(tt(o, r_a, over(r_m[:, m + 1, :], E), ALU.is_equal))
                    if m == 0:
                        step(stt(r_l2, r_o1, -3.0e38, logits, ALU.mult, ALU.add))
                step(tt(r_z[:, :, 0], r_m[:, 2, :], r_m[:, 0, :], ALU.subtract))
                step(ts(r_z[:, :, 1], lg[:, :, E], -1.0, None, ALU.mult))
                assert steps[0] == R_EXP
                dve.wait_ge(r_exp, g + 1)
                step(ts(r_d, r_e, 1.0, None, ALU.add))
                step(nc.vector.reciprocal(r_w, r_d))
                step(tt(r_z[:, :, 0], r_e[:, :, 0], r_w[:, :, 0], ALU.mult))
                step(tt(r_o1, r_o1, over(r_w[:, :, 0], E), ALU.mult))
                step(tt(r_o2, r_o2, over(r_z[:, :, 0], E), ALU.mult))
                step(tt(cw[:, :, 0:E], r_o1, r_o2, ALU.add))
                step(nc.vector.tensor_copy(cw[:, :, E:E + 1], r_w[:, :, 1:2]))
                step(nc.vector.tensor_copy(c3[:, :, 0:E + 1], cw))
                step(tt(cr, cw, c3[:, :, 0:E + 1], ALU.subtract))
                step(nc.vector.tensor_copy(c3[:, :, 32:32 + E + 1], cr))
                step(tt(cr2, cr, c3[:, :, 32:32 + E + 1], ALU.subtract))
                assert steps[0] == R_STEPS, steps[0]
                nc.vector.tensor_copy(c3[:, :, 64:64 + E + 1], cr2).then_inc(c3_ready, 1)

                for j in range(FB):
                    dve.wait_ge(silu_done, g * FB + j + 1)
                    dve.wait_ge(up_ready, g * FB + j + 1)
                    if j >= 2:
                        dve.wait_ge(h_lo, g * FB + j - 1)
                    tt(ring[:, 2 + j % 2, :], ring[:, j % 2, :], PS[2 + j % 2][:, :], ALU.mult).then_inc(gu_done, 1)
                    dve.wait_ge(cwb_ready, g * FB + j + 1)
                    dve.wait_ge(gu_done, g * FB + j + 1)
                    tt(ring[:, 2 + j % 2, :], ring[:, 2 + j % 2, :], PS[4 + j % 2][:, :], ALU.mult).then_inc(h_done, 1)
                dve.wait_ge(down_done, g * FB + FB)
                for q in range(2):
                    tt(X[:, 2 * q:2 * q + 2, :], pair(PS[6 + q]), X[:, 2 * q:2 * q + 2, :], ALU.add).then_inc(x3_ready, 1)
    return nc


INPUTS = ['x', 'ctx_512', 'L0_attn_Wr', 'L0_attn_br', 'L0_attn_Wk', 'L0_attn_bk', 'L0_attn_Wv', 'L0_attn_bv', 'L0_attn_Wg',
          'L0_attn_bg', 'L0_attn_Wo', 'L0_attn_bo', 'L0_attn_ln_g', 'L0_attn_ln_b', 'L0_attn_maa_k', 'L0_attn_maa_v',
          'L0_attn_maa_r', 'L0_attn_maa_g', 'L0_attn_time_decay', 'L0_attn_time_faaaa', 'L0_xattn_Wq', 'L0_xattn_Wkv_expand',
          'L0_xattn_Wout', 'L0_ffn_router_w', 'L0_ffn_w_gate', 'L0_ffn_w_up', 'L0_ffn_w_down', 'L0_ffn_sw_gate',
          'L0_ffn_sw_up', 'L0_ffn_sw_down', 'L0_ffn_shared_gate_w']


def kernel(**inputs):
    import numpy as np
    import concourse.bacc as bacc
    from concourse.bass_utils import run_bass_kernel_spmd

    nc = bacc.Bacc("TRN2", target_bir_lowering=False, num_devices=1)
    arrays, args = {}, []
    for name in INPUTS:
        a = np.ascontiguousarray(inputs[name])
        arrays[f"in_{name}"] = a
        args.append(nc.dram_tensor(f"in_{name}", a.shape, mybir.dt.from_np(a.dtype), kind="ExternalInput").ap())
    shape = inputs['x'].shape
    args.append(nc.dram_tensor("out_x", shape, F32, kind="ExternalOutput").ap())
    decoder_layer(nc, *args)
    r = run_bass_kernel_spmd(nc, [arrays], core_ids=[0])
    return r.results[0]["out_x"]
```

```python
from contextlib import ExitStack

import concourse.bass as bass
from concourse import mybir

F32 = mybir.dt.float32
F32R = mybir.dt.float32r
BF16 = mybir.dt.bfloat16
I32 = mybir.dt.int32
ALU = mybir.AluOpType
ACT = mybir.ActivationFunctionType
AX = mybir.AxisListType.X

P = 128
NEG = -1.0e30


def decoder_layer(nc, x, ctx_in, Wr, br, Wk, bk, Wv, bv, Wg, bg, Wo, bo, ln_g, ln_b,
                  maa_k, maa_v, maa_r, maa_g, time_decay, time_faaaa, Wq, Wkv, Wout,
                  router_w, w_gate, w_up, w_down, sw_gate, sw_up, sw_down, shared_gate_w, out):
    B, T, C = x.shape
    H = time_decay.shape[0]
    N = C // H
    L = ctx_in.shape[2]
    XH = 16
    XD = C // XH
    E, _, I = w_gate.shape
    SI = sw_gate.shape[1]
    KC = C // P
    GB = 4
    NG = B // GB
    GT = GB * T
    NR = E * I
    NF = NR + SI
    FB = -(-NF // P)
    FP = FB * P
    LN_EPS = 1e-5
    GN_EPS = 1e-5 * 64
    assert T == P and KC == 2 and GT == 512 and N == 8 and XD == 16 and NF - (FB - 1) * P == 64

    es = ExitStack()
    with es:
        def sb(name, shape, dt):
            return es.enter_context(nc.sbuf_tensor(name, shape, dt))

        def sem(name):
            return es.enter_context(nc.semaphore(name))

        ident = sb("ident", [P, P], F32)
        identb = sb("identb", [P, P], BF16)
        wAh = sb("wAh", [P, 5, KC, C], F32R)
        wAl = sb("wAl", [P, 5, KC, C], F32R)
        wXh = sb("wXh", [P, 2, KC, C], F32R)
        wXl = sb("wXl", [P, 2, KC, C], F32R)
        wKh = sb("wKh", [L, 2 * C], F32R)
        wKl = sb("wKl", [L, 2 * C], F32R)
        wGh = sb("wGh", [P, KC, FP], F32R)
        wGl = sb("wGl", [P, KC, FP], F32R)
        wUh = sb("wUh", [P, KC, FP], F32R)
        wUl = sb("wUl", [P, KC, FP], F32R)
        wDh = sb("wDh", [P, FB, C], F32R)
        wDl = sb("wDl", [P, FB, C], F32R)
        wRh = sb("wRh", [P, KC, E + 2], F32R)
        wRl = sb("wRl", [P, KC, E + 2], F32R)
        selC = sb("selC", [96, FP], BF16)
        selH = sb("selH", [16, 8, P], BF16)
        maskS = sb("maskS", [P, P], BF16)
        maskT = sb("maskT", [P, P], BF16)
        decay = sb("decay", [P, H, P], F32)
        bvB = sb("bvB", [P, C], F32)
        boB = sb("boB", [P, C], F32)
        cols = sb("cols", [P, 9, KC], F32)
        BR, BK, BG, LNG, LNB, MR, MK, MV, MG = range(9)
        mhalf = sb("mhalf", [P, GB], F32)
        rev = sb("rev", [P, E], F32)

        AF = sb("AF", [P, 6216], F32)
        AR = sb("AR", [P, 5120], F32R)
        dist = AF[:, 5632:5760]
        cx = AF[:, 5192:5448].rearrange("p (b l) -> p b l", b=GB)
        st = sb("st", [P, GB, 6], F32)
        mv = sb("mv", [P, GB, 2], F32)
        ve = sb("ve", [P, GB], F32)
        rstd = sb("rstd", [P, GB], F32)
        headmean = sb("headmean", [P, P], F32)
        yc = sb("yc", [P, GT], F32)
        nm = sb("nm", [P, 2, 8], F32)
        nmr = sb("nmr", [P, 2, 8], F32)
        nm2 = sb("nm2", [P, 2, 16], BF16)
        nmT = sb("nmT", [16, 2, P], BF16)
        rec = sb("rec", [P, 2, XH], F32)
        td = AF[:, 6016:6016 + H]
        tf = AF[:, 6016 + H:6016 + 2 * H]
        cwT = AF[0:96, 5448:5704].bitcast(BF16)
        c3 = AF[:, 5704:5896].bitcast(BF16).rearrange("p (b n) -> p b n", b=GB)
        taken = [4104]

        def small(n, w):
            taken[0] += n * w
            return AF[:, taken[0] - n * w:taken[0]].rearrange("p (n w) -> p n w", n=n)

        lg = small(GB, E + 2)
        r_m = small(4, GB)
        r_a, r_o1, r_o2, r_l2 = (small(GB, E) for _ in range(4))
        r_z, r_e, r_d, r_w = (small(GB, 2) for _ in range(4))
        cw, cr, cr2 = (small(GB, E + 1) for _ in range(3))

        def tokens(a):
            return AF[:, a:a + GB * C].rearrange("p (b c) -> p b c", b=GB)

        X = tokens(0)
        XX = AF[:, 0:1024].rearrange("p (k b t) -> p k b t", k=KC, b=GB)
        tok = tokens(1024)
        R0 = 2048
        xnT = AF[:, R0:R0 + KC * GB * (T + 1)].rearrange("p (k b t) -> p k b t", k=KC, b=GB)
        xm = AF[:, R0 + 1032:R0 + 2056].rearrange("p (s n) -> p s n", s=2)
        ring = AF[:, R0:R0 + 2048].rearrange("p (s n) -> p s n", s=4)
        gact = AF[:, 4104:5128].rearrange("p (k n) -> p k n", k=KC)
        xv = AF[:, 4104:5192].rearrange("p (b h d) -> p b h d", b=GB, h=XH)
        VW = 4 * N
        vpad = AF[:, 5192:6216].rearrange("p (s n) -> p s n", s=2)
        QT = GT // 2
        gn_x, gn_y = ring[:, 3, 0:QT], ring[:, 3, QT:GT]

        def hl(a, n):
            return AR[:, a:a + 2 * n].rearrange("p (s n) -> p s n", s=2)

        mix = [hl(c * 1024, 512) for c in range(3)]
        rkst = [hl(3072 + n * 1024, 512) for n in range(2)]
        stage = [hl(2048 + n * 1024, 512) for n in range(2)]
        xT = AR[:, 0:2048].rearrange("p (s k n) -> p s k n", s=2, k=KC)
        cT = AR[0:L, 4096:5120].rearrange("p (s n) -> p s n", s=2)
        hT = [hl(2048 + s * 1024, 512) for s in range(2)]
        rbd = [AR[:, s * 2560:s * 2560 + 2048].rearrange("p (a j t) -> p a j t", a=4, j=4) for s in range(2)]
        kst4 = [AR[:, s * 2560 + 2048:s * 2560 + 2560].rearrange("p (a t) -> p a t", a=4) for s in range(2)]
        qst = [AR[:, s * 1024:s * 1024 + 512].rearrange("p (a t) -> p a t", a=4) for s in range(4)]
        kst = [AR[:, s * 1024 + 512:s * 1024 + 1024].rearrange("p (a t) -> p a t", a=4) for s in range(4)]

        rD = nc.dram_tensor("r_parts", (H, 4 * N, GT), F32, kind="Internal").ap()
        kD = nc.dram_tensor("k_parts", (H, 4 * N, GT), F32, kind="Internal").ap()
        qD = nc.dram_tensor("q_parts", (XH, 4 * XD, GT), F32, kind="Internal").ap()
        xkD = nc.dram_tensor("xk_parts", (XH, 4 * XD, GT), F32, kind="Internal").ap()

        PS = [es.enter_context(nc.psum_tensor(f"bank{i}", [P, 512], F32)) for i in range(8)]

        w_in = [sem(f"w_in{i}") for i in range(2)]
        small_in = sem("small_in")
        consts = sem("consts")
        w_tp = sem("w_tp")
        w_hi = sem("w_hi")
        w_lo = sem("w_lo")
        f_in = [sem(f"f_in{i}") for i in range(2)]
        f_hi = sem("f_hi")
        f_lo = [sem("f_lo_dve"), sem("f_lo_pool")]
        tail_in = sem("tail_in")
        pads = sem("pads")
        dk_i = sem("dk_i")
        dk_a = sem("dk_a")
        dk_p = sem("dk_p")
        dk_v = sem("dk_v")

        waited_pe = sem("waited_pe")
        waited_pool = sem("waited_pool")
        waited_dve = sem("waited_dve")

        x_in = sem("x_in")
        xres_in = sem("xres_in")
        ctx_arrived = sem("ctx_arrived")
        ln_stats = sem("ln_stats")
        ln_mean = sem("ln_mean")
        ln_var = sem("ln_var")
        ln_rstd = sem("ln_rstd")
        xn_ready = sem("xn_ready")
        xn_turned = sem("xn_turned")
        xnT_act = sem("xnT_act")
        xnT_dve = sem("xnT_dve")
        edge_zero = sem("edge_zero")
        xx_ready = sem("xx_ready")
        xm_ready = sem("xm_ready")
        mix_hi = sem("mix_hi")
        mix_lo = [sem("mix_lo_dve"), sem("mix_lo_pool")]
        mix_used = sem("mix_used")
        rk_hi = sem("rk_hi")
        rk_lo = sem("rk_lo")
        rk_out = [sem("rk_out0"), sem("rk_out1")]
        v_ready = sem("v_ready")
        g_ready = sem("g_ready")
        vpad_zero = sem("vpad_zero")
        vpad_ready = sem("vpad_ready")
        rbd_zero = [sem("rbd_zero0"), sem("rbd_zero1")]
        wkv_in = [sem(f"wkv_in{s}") for s in range(2)]
        s_ready = sem("s_ready")
        pt_ready = sem("pt_ready")
        y_part = sem("y_part")
        y_copied = sem("y_copied")
        gn_mean = sem("gn_mean")
        gn_cent = sem("gn_cent")
        gn_sq = sem("gn_sq")
        gn_var = sem("gn_var")
        gn_step = sem("gn_step")
        y_gated = sem("y_gated")
        y_hi = sem("y_hi")
        y_lo = sem("y_lo")
        wo_ready = sem("wo_ready")
        xbo_ready = sem("xbo_ready")
        x1_ready = sem("x1_ready")
        ctx_turned = sem("ctx_turned")
        cT_hi = sem("cT_hi")
        cT_lo = sem("cT_lo")
        kp_ready = sem("kp_ready")
        vp_ready = sem("vp_ready")
        xv_one = sem("xv_one")
        xv_ready = sem("xv_ready")
        xT_hi = sem("xT_hi")
        xT_lo = sem("xT_lo")
        qp_ready = sem("qp_ready")
        qk_hi = sem("qk_hi")
        qk_lo = sem("qk_lo")
        qk_out = [sem("qk_out0"), sem("qk_out1")]
        xa_in = [sem(f"xa_in{s}") for s in range(4)]
        sm_ready = sem("sm_ready")
        max_ready = sem("max_ready")
        nm_step = sem("nm_step")
        nm_turned = sem("nm_turned")
        nmT_ready = sem("nmT_ready")
        t_ready = sem("t_ready")
        p_ready = sem("p_ready")
        o_part = sem("o_part")
        rec_ready = sem("rec_ready")
        yo_ready = sem("yo_ready")
        yo_turned = sem("yo_turned")
        yT_hi = sem("yT_hi")
        yT_lo = sem("yT_lo")
        wout_ready = sem("wout_ready")
        x2_ready = sem("x2_ready")
        route_ready = sem("route_ready")
        r_step = sem("r_step")
        r_exp = sem("r_exp")
        c3_zero = sem("c3_zero")
        c3_ready = sem("c3_ready")
        cw_turned = sem("cw_turned")
        cwT_ready = sem("cwT_ready")
        gate_ready = sem("gate_ready")
        up_ready = sem("up_ready")
        cwb_ready = sem("cwb_ready")
        silu_done = sem("silu_done")
        gu_done = sem("gu_done")
        h_done = sem("h_done")
        h_hi = sem("h_hi")
        h_lo = sem("h_lo")
        down_done = sem("down_done")
        x3_ready = sem("x3_ready")
        out_done = sem("out_done")
        PRIMED = 1
        GN_STEPS = 13
        R_EXP = 14
        R_STEPS = 25

        CONSTS = 4 + 4 + 3 + 1 + 3 * 4 + 1 + E + 3

        block = es.enter_context(nc.Block())

        SQ = [(Wr, wAh[:, 0], wAl[:, 0]), (Wk, wAh[:, 1], wAl[:, 1]), (Wv, wAh[:, 2], wAl[:, 2]),
              (Wg, wAh[:, 3], wAl[:, 3]), (Wo, wAh[:, 4], wAl[:, 4]),
              (Wq, wXh[:, 0], wXl[:, 0]), (Wout, wXh[:, 1], wXl[:, 1])]
        NSQ = len(SQ)

        def sq_raw(n):
            return AF[:, 4608 + (n % 2) * 512:5120 + (n % 2) * 512].rearrange("p (o i) -> p o i", o=KC)

        kv_raw = AF[:, 4352:4608].rearrange("p (o l) -> p o l", o=4)
        FW = []
        for hi_t, lo_t, we, ws in ((wGh, wGl, w_gate, sw_gate), (wUh, wUl, w_up, sw_up)):
            for k in range(KC):
                FW.append((hi_t[:, k, 0:NF], lo_t[:, k, 0:NF], NF,
                           [(0, NR, we[:, k * P:(k + 1) * P, :].rearrange("e p i -> p e i"), E),
                            (NR, NF, ws[k * P:(k + 1) * P, :], 0)]))
        wd = w_down.rearrange("e i h -> (e i) h")
        RB = NR // P
        SB = SI // P
        for j0, j1, src in ((0, 6, wd), (6, RB, wd), (RB, RB + SB, sw_down)):
            s0 = (j0 - (RB if j0 >= RB else 0)) * P
            FW.append((wDh[:, j0:j1, :], wDl[:, j0:j1, :], (j1 - j0) * C,
                       [(0, (j1 - j0) * C, src[s0:s0 + (j1 - j0) * P, :].rearrange("(j p) c -> p j c", p=P), j1 - j0)]))
        NFW = len(FW)
        DMA_FW = [len(f[3]) for f in FW]

        def fw_raw(n):
            raw = AF[:, (n % 2) * NF:(n % 2) * NF + FW[n][2]]
            return raw.rearrange("p (j c) -> p j c", c=C) if len(FW[n][0].shape) == 3 else raw

        def fw_in(n):
            return 16 * sum(DMA_FW[m] for m in range(n % 2, n + 1, 2))

        tail_raw = AF[0:64, 4608:4608 + C]
        rw_raw = AF[0:E + 2, 5760:5760 + C]
        SMALL = 1 + 9 + 4 + 2

        @block.sync
        def _(sp):
            sp.dma_start(kv_raw, Wkv.rearrange("(o p) l -> p o l", p=P)).then_inc(small_in, 16)
            for n, v in ((BR, br), (BK, bk), (BG, bg), (LNG, ln_g), (LNB, ln_b), (MR, maa_r), (MK, maa_k), (MV, maa_v), (MG, maa_g)):
                with nc.allow_non_contiguous_dma(reason="256 values"):
                    sp.dma_start(cols[:, n, :], v.rearrange("(k p) -> p k", p=P)).then_inc(small_in, 16)
            sp.dma_start(td[:], time_decay.partition_broadcast(P)).then_inc(small_in, 16)
            sp.dma_start(tf[:], time_faaaa.partition_broadcast(P)).then_inc(small_in, 16)
            sp.dma_start(bvB[:], bv.partition_broadcast(P)).then_inc(small_in, 16)
            sp.dma_start(boB[:], bo.partition_broadcast(P)).then_inc(small_in, 16)
            sp.wait_ge(dk_v, 1)
            sp.dma_start(rw_raw[0:E, :], router_w).then_inc(small_in, 16)
            sp.dma_start(rw_raw[E:E + 1, :], shared_gate_w.unsqueeze(0)).then_inc(small_in, 16)
            for n in range(NSQ):
                if n >= 2:
                    sp.wait_ge(w_tp, n - 1)
                sp.dma_start(sq_raw(n), SQ[n][0].rearrange("(o p) i -> p o i", p=P)).then_inc(w_in[n % 2], 16)
            for n in range(NFW):
                if n >= 2:
                    sp.wait_ge(f_hi, n - 1)
                    sp.wait_ge(f_lo[n % 2], n // 2)
                for a, b, src, parts in FW[n][3]:
                    dst = AF[:, (n % 2) * NF + a:(n % 2) * NF + b]
                    if parts:
                        dst = dst.rearrange("p (e i) -> p e i", e=parts)
                    sp.dma_start(dst, src).then_inc(f_in[n % 2], 16)
            sp.wait_ge(w_tp, NSQ + 2)
            sp.dma_start(tail_raw, sw_down[SB * P:SI, :]).then_inc(tail_in, 16)
            sp.wait_ge(f_hi, NFW + 1)
            sp.wait_ge(f_lo[0], (NFW + 1) // 2 + 1)
            sp.wait_ge(f_lo[1], NFW // 2)

            with sp.Fori(0, NG) as g:
                sp.wait_ge(xn_turned, g * 12 + PRIMED)
                sp.dma_start(tok, x[bass.ds(g * GB, GB)].rearrange("b t c -> t b c")).then_inc(x_in, 16)
                for n in range(4):
                    m = n % 2
                    sp.wait_ge(rk_hi, g * 4 + n + 1)
                    sp.wait_ge(rk_lo, g * 4 + n + 1)
                    D, order = (rD, (0, 1, 0, 1)) if n < 2 else (kD, (0, 1, 1, 0))
                    for i, part in enumerate(order):
                        sp.dma_start(D[m * 16:(m + 1) * 16, i * N:(i + 1) * N, :],
                                     rkst[m][:, part, :].bitcast(F32)).then_inc(rk_out[m], 16)
                sp.wait_ge(xm_ready, g * 8 + 8)
                sp.dma_start(X, x[bass.ds(g * GB, GB)].rearrange("b t c -> t b c")).then_inc(xres_in, 16)
                for m in range(2):
                    sp.wait_ge(rk_out[m], g * 128 + 128)
                for u in range(8):
                    half, s, t0 = u // 4, u % 2, (u % 4) * T
                    if u >= 2:
                        sp.wait_ge(s_ready, g * 32 + 4 * (u - 2) + 4)
                    else:
                        sp.wait_ge(rbd_zero[s], g * 2 + 2)
                    first = half * 4 * P * GT + t0
                    src = bass.AP(kD.tensor, first, [[GT, P], [P * GT, 4], [1, T]])
                    sp.dma_start(kst4[s].bitcast(F32), src).then_inc(wkv_in[s], 16)
                    for j in range(4):
                        src = bass.AP(rD.tensor, first + j * 32 * GT, [[GT, 32], [P * GT, 4], [1, T]])
                        sp.dma_start(rbd[s][32 * j:32 * j + 32, :, j, :].bitcast(F32), src).then_inc(wkv_in[s], 16)
                sp.wait_ge(y_part, g * 32 + 32)
                sp.dma_start(cx, ctx_in[bass.ds(g * GB, GB)].rearrange("b t c -> t b c")).then_inc(ctx_arrived, 16)
                for n in range(4):
                    m = n % 2
                    sp.wait_ge(qk_hi, g * 4 + n + 1)
                    sp.wait_ge(qk_lo, g * 4 + n + 1)
                    D, order = (xkD, (0, 1, 1, 0)) if n < 2 else (qD, (0, 1, 0, 1))
                    for i, part in enumerate(order):
                        sp.dma_start(D[m * 8:(m + 1) * 8, i * XD:(i + 1) * XD, :],
                                     stage[m][:, part, :].bitcast(F32)).then_inc(qk_out[m], 16)
                for m in range(2):
                    sp.wait_ge(qk_out[m], g * 128 + 128)
                sp.wait_ge(qp_ready, g * 2 + 2)
                sp.wait_ge(vp_ready, g * 2 + 2)
                for u in range(8):
                    half, s, t0 = u % 2, u % 4, (u // 2) * T
                    if u >= 4:
                        sp.wait_ge(t_ready, g * 16 + 2 * (u - 4) + 2)
                    for D, dst in ((qD, qst), (xkD, kst)):
                        src = bass.AP(D.tensor, half * 4 * P * GT + t0, [[GT, P], [P * GT, 4], [1, T]])
                        sp.dma_start(dst[s].bitcast(F32), src).then_inc(xa_in[s], 16)
            sp.wait_ge(out_done, 16 * NG + 16 * PRIMED)

        @block.gpsimd
        def _(pool):
            done = [0]

            def made(ins):
                done[0] += 1
                ins.then_inc(consts, 1)
                pool.wait_ge(consts, done[0])

            for t in (ident, identb):
                made(pool.memset(t[:], 0.0))
                made(pool.affine_select(out=t[:], in_=t[:], compare_op=ALU.not_equal, fill=1.0, base=0,
                                        pattern=[[-1, P]], channel_multiplier=1))
            for t, sign in ((maskS, -1), (maskT, 1)):
                made(pool.memset(t[:], 0.0))
                made(pool.affine_select(out=t[:], in_=t[:], compare_op=ALU.is_ge, fill=NEG, base=0,
                                        pattern=[[sign, P]], channel_multiplier=-sign))
            made(pool.memset(selH[:], 0.0))
            for part in range(2):
                made(pool.affine_select(out=selH[:], in_=selH[:], compare_op=ALU.not_equal, fill=1.0,
                                        base=-8 * part, pattern=[[-1, 8], [0, P]], channel_multiplier=1))
            made(pool.memset(selC[:], 0.0))
            for part in range(3):
                rows = selC[32 * part:32 * part + E + 1, :]
                made(pool.memset(rows[:, 0:NF], 1.0))
                made(pool.affine_select(out=rows[:, 0:NF], in_=rows[:, 0:NF], compare_op=ALU.is_ge, fill=0.0,
                                        base=0, pattern=[[1, NF]], channel_multiplier=-I))
                made(pool.affine_select(out=rows[:, 0:NR], in_=rows[:, 0:NR], compare_op=ALU.is_ge, fill=0.0,
                                        base=I - 1, pattern=[[-1, NR]], channel_multiplier=I))
                made(pool.affine_select(out=rows[:, NR:NF], in_=rows[:, NR:NF], compare_op=ALU.is_ge, fill=0.0,
                                        base=-E, pattern=[[0, SI]], channel_multiplier=1))
            made(pool.memset(mhalf[:], -0.5))
            for n in range(E):
                made(pool.memset(rev[:, n:n + 1], float(E - n)))
            made(pool.memset(headmean[:], 1.0 / N))
            for base, sign in ((0, 1), (N - 1, -1)):
                made(pool.affine_select(out=headmean[:], in_=headmean[:], compare_op=ALU.is_ge, fill=0.0, base=base,
                                        pattern=[[-sign * N, P // N], [0, N]], channel_multiplier=sign))
            assert done[0] == CONSTS
            pool.iota(dist, pattern=[[1, P]], base=-1, channel_multiplier=-1,
                      allow_small_or_imprecise_dtypes=True).then_inc(dk_i, 1)
            pool.wait_ge(dk_i, 1)
            pool.tensor_scalar(dist, dist, 0.0, None, ALU.max).then_inc(dk_p, 1)
            pool.wait_ge(dk_a, 1 + H)
            pool.affine_select(out=decay[:], in_=decay[:], compare_op=ALU.is_gt, fill=0.0, base=0,
                               pattern=[[0, H], [1, P]], channel_multiplier=-1).then_inc(dk_p, 1)
            for t in (wGh, wGl, wUh, wUl):
                pool.memset(t[:, :, NF:FP].bitcast(F32), 0.0).then_inc(pads, 1)
            pool.wait_ge(pads, 4)
            for t in (wDh, wDl):
                pool.memset(t[64:P, FB - 1, :].bitcast(F32), 0.0).then_inc(pads, 1)
            pool.wait_ge(pads, 6)
            for n in range(1, NFW, 2):
                pool.wait_ge(f_hi, n + 1)
                hi, lo, raw = FW[n][0], FW[n][1], fw_raw(n)
                pool.tensor_tensor(lo, raw, hi.bitcast(F32), ALU.subtract).then_inc(f_lo[1], 1)

            with pool.Fori(0, NG) as g:
                def layer_rstd(s):
                    pool.wait_ge(ln_mean, g * 12 + 4 * s + 4)
                    pool.sem_inc(waited_pool, 1)
                    pool.tensor_scalar(ve[:], mv[:, :, 1], LN_EPS, None, ALU.add).then_inc(ln_var, 1)
                    pool.wait_ge(ln_var, g * 3 + s + 1)
                    pool.tensor_tensor(rstd[:], ve[:], mhalf[:], ALU.pow).then_inc(ln_rstd, 1)

                layer_rstd(0)
                pool.wait_ge(x3_ready, g * 2 + PRIMED)
                pool.sem_inc(waited_pool, 1)
                pool.memset(AF[:, 5192:6216], 0.0).then_inc(vpad_zero, 1)
                pool.memset(xnT[:, :, :, 0:1], 0.0).then_inc(edge_zero, 1)
                for c in range(1, 8, 2):
                    pool.wait_ge(mix_hi, g * 8 + c + 1)
                    pool.tensor_tensor(mix[c % 3][:, 1, :], xm[:, c % 2, :], mix[c % 3][:, 0, :].bitcast(F32),
                                       ALU.subtract).then_inc(mix_lo[1], 1)
                pool.wait_ge(xres_in, g * 16 + 16)
                pool.tensor_tensor(X, X, boB[:].unsqueeze(1).to_broadcast([P, GB, C]), ALU.add).then_inc(xbo_ready, 1)
                pool.wait_ge(mix_used, g * 8 + 8)
                for m in range(2):
                    pool.wait_ge(rk_out[m], g * 128 + 128)
                pool.sem_inc(waited_pool, 1)
                pool.memset(AR[:, 2560:4608].bitcast(F32), 0.0).then_inc(rbd_zero[1], 2)
                pool.wait_ge(y_lo, g * 2 + 2)
                pool.sem_inc(waited_pool, 1)
                pool.memset(xv[:, :, :, XD:XD + 1], 1.0).then_inc(xv_one, 1)
                pool.memset(c3, 0.0).then_inc(c3_zero, 1)
                layer_rstd(1)
                layer_rstd(2)
                for j in range(FB):
                    pool.wait_ge(h_hi, g * FB + j + 1)
                    pool.tensor_tensor(hT[j % 2][:, 1, :], ring[:, 2 + j % 2, :], hT[j % 2][:, 0, :].bitcast(F32),
                                       ALU.subtract).then_inc(h_lo, 1)

        @block.scalar
        def _(act):
            act.wait_ge(small_in, 16 * SMALL)
            act.activation(td[:], td[:], ACT.Exp).then_inc(dk_a, 1)
            act.wait_ge(dk_v, 2)
            act.wait_ge(dk_p, 1)
            for h in range(H):
                act.activation(decay[:, h, :], dist, ACT.Exp, scale=td[:, h:h + 1]).then_inc(dk_a, 1)
            for n in range(NSQ):
                act.wait_ge(w_tp, n + 1)
                act.activation(SQ[n][1], PS[n % 2][:, :].rearrange("p (i o) -> p i o", i=KC), ACT.Copy).then_inc(w_hi, 1)
            act.wait_ge(w_tp, NSQ + 1)
            act.activation(wKh[:], PS[NSQ % 2][0:L, :], ACT.Copy).then_inc(w_hi, 1)
            act.wait_ge(w_tp, NSQ + 2)
            act.activation(wRh[:], PS[(NSQ + 1) % 2][:, 0:KC * (E + 2)].rearrange("p (k e) -> p k e", k=KC), ACT.Copy).then_inc(w_hi, 1)
            for n in range(NFW):
                act.wait_ge(f_in[n % 2], fw_in(n))
                act.activation(FW[n][0], fw_raw(n), ACT.Copy).then_inc(f_hi, 1)
            act.wait_ge(tail_in, 16)
            act.activation(wDh[0:64, FB - 1, :], tail_raw, ACT.Copy).then_inc(f_hi, 1)

            act.sem_inc(out_done, 16 * PRIMED)

            with act.Fori(0, NG) as g:
                act.wait_ge(xn_turned, g * 12 + 4 + PRIMED)
                act.activation(xnT[:, 0, :, 1:T + 1], PS[6][:, :].rearrange("p (b t) -> p b t", b=GB), ACT.Copy).then_inc(xnT_act, 1)

                def mix_part(c):
                    act.wait_ge(xm_ready, g * 8 + c + 1)
                    if c >= 3:
                        act.wait_ge(mix_used, g * 8 + c - 2)
                    act.activation(mix[c % 3][:, 0, :], xm[:, c % 2, :], ACT.Copy).then_inc(mix_hi, 1)

                def rk_part(n):
                    i, m = n // 2, n % 2
                    act.wait_ge(mix_used, g * 8 + 2 * i + 2)
                    if i:
                        act.wait_ge(rk_out[m], g * 128 + 64)
                    act.activation(rkst[m][:, 0, :], PS[2 * i + m][:, :], ACT.Identity,
                                   bias=cols[:, BR + i, m:m + 1]).then_inc(rk_hi, 1)

                for c in range(4):
                    mix_part(c)
                rk_part(0)
                rk_part(1)
                mix_part(4)
                mix_part(5)
                rk_part(2)
                rk_part(3)
                mix_part(6)
                mix_part(7)
                act.wait_ge(mix_used, g * 8 + 8)
                for m in range(2):
                    act.activation(gact[:, m, :], PS[2 + m][:, :], ACT.Silu, bias=cols[:, BG, m:m + 1]).then_inc(g_ready, 1)

                def pad_v(u):
                    half, b = u // 4, u % 4
                    if u == 0:
                        act.wait_ge(v_ready, g * 2 + 2)
                        act.wait_ge(vpad_zero, g + 1)
                    if u >= 2:
                        act.wait_ge(y_part, g * 32 + 4 * (u - 1))
                    act.activation(vpad[:, u % 2, :].rearrange("p (h n) -> p h n", n=VW)[:, :, 0:N],
                                   tok[:, b, half * P:(half + 1) * P].rearrange("p (h n) -> p h n", n=N), ACT.Copy).then_inc(vpad_ready, 1)

                def copy_y(e):
                    act.wait_ge(y_part, g * 32 + 8 * (e + 1))
                    if e >= 2:
                        act.wait_ge(y_gated, g * 4 + e - 1)
                    h = slice((e % 2) * QT, (e % 2 + 1) * QT)
                    act.activation(yc[:, h], PS[4 + e % 2][:, 0:QT], ACT.Copy).then_inc(y_copied, 1)

                def square_y(e):
                    act.wait_ge(gn_cent, g * 4 + e + 1)
                    if e:
                        act.wait_ge(y_gated, g * 4 + e)
                    act.activation(gn_x, yc[:, (e % 2) * QT:(e % 2 + 1) * QT], ACT.Square).then_inc(gn_sq, 1)

                def gated_hi(q):
                    act.wait_ge(y_gated, g * 4 + 2 * q + 2)
                    if q == 0:
                        act.wait_ge(s_ready, g * 32 + 28)
                    act.activation(xT[:, 0, q, :], gact[:, q, :], ACT.Copy).then_inc(y_hi, 1)

                for u in range(4):
                    pad_v(u)
                copy_y(0)
                square_y(0)
                pad_v(4)
                pad_v(5)
                copy_y(1)
                square_y(1)
                pad_v(6)
                pad_v(7)
                copy_y(2)
                square_y(2)
                gated_hi(0)
                copy_y(3)
                square_y(3)
                gated_hi(1)
                act.wait_ge(ctx_turned, g + 1)
                act.activation(cT[:, 0, :], PS[2][0:L, :], ACT.Copy).then_inc(cT_hi, 1)
                for m in range(2):
                    act.wait_ge(kp_ready, g * 2 + m + 1)
                    act.activation(stage[m][:, 0, :], PS[3 + m][:, :], ACT.Copy).then_inc(qk_hi, 1)
                act.wait_ge(xn_turned, g * 12 + 8 + PRIMED)
                for k in range(2):
                    act.activation(xT[:, 0, k, :], PS[6 + k][:, :], ACT.Copy).then_inc(xT_hi, 1)
                for m in range(2):
                    act.wait_ge(qp_ready, g * 2 + m + 1)
                    act.wait_ge(qk_out[m], g * 128 + 64)
                    act.activation(stage[m][:, 0, :], PS[m][:, :], ACT.Copy, scale=float(XD) ** -0.5).then_inc(qk_hi, 1)

                def turned_max(u):
                    act.wait_ge(nm_turned, g * 8 + u + 1)
                    act.activation(nmT[:, u % 2, :], PS[6 + u % 2][:, :].bitcast(BF16)[0:16, 0:P], ACT.Copy).then_inc(nmT_ready, 1)

                def exps(u):
                    for qd in (2 * u, 2 * u + 1):
                        act.wait_ge(t_ready, g * 16 + qd + 1)
                        if qd >= 4:
                            act.wait_ge(o_part, g * 16 + qd - 3)
                        act.activation(ring[:, qd % 4, :], PS[2 + qd % 2][:, :], ACT.Exp).then_inc(p_ready, 1)

                turned_max(0)
                for u in range(8):
                    exps(u)
                    if u + 1 < 8:
                        turned_max(u + 1)
                act.wait_ge(yo_turned, g + 1)
                for k in range(2):
                    act.activation(xT[:, 0, k, :], PS[6 + k][:, :], ACT.Copy).then_inc(yT_hi, 1)
                act.wait_ge(xn_turned, g * 12 + 12 + PRIMED)
                for k in range(2):
                    act.activation(xT[:, 0, k, :], PS[6 + k][:, :], ACT.Copy).then_inc(xT_hi, 1)
                act.wait_ge(r_step, g * R_STEPS + R_EXP)
                act.activation(r_e[:], r_z[:], ACT.Exp).then_inc(r_exp, 1)

                def silu(j):
                    act.wait_ge(gate_ready, g * FB + j + 1)
                    if j >= 2:
                        act.wait_ge(gu_done, g * FB + j - 1)
                    act.activation(ring[:, j % 2, :], PS[j % 2][:, :], ACT.Silu).then_inc(silu_done, 1)

                silu(0)
                silu(1)
                act.wait_ge(cw_turned, g + 1)
                act.activation(cwT, PS[5][:, :].bitcast(BF16)[0:96, 0:GT], ACT.Copy).then_inc(cwT_ready, 1)
                for j in range(FB):
                    act.wait_ge(h_done, g * FB + j + 1)
                    if j >= 2:
                        act.wait_ge(down_done, g * FB + j - 1)
                    act.activation(hT[j % 2][:, 0, :], ring[:, 2 + j % 2, :], ACT.Copy).then_inc(h_hi, 1)
                    if j + 2 < FB:
                        silu(j + 2)
                act.wait_ge(x3_ready, g * 2 + 2 + PRIMED)
                act.dma_start(out[bass.ds(g * GB, GB)].rearrange("b t c -> t b c"), X).then_inc(out_done, 16)

        @block.tensor
        def _(pe):
            mm = nc.tensor.matmul
            pe.wait_ge(consts, 4)
            for n in range(NSQ):
                pe.wait_ge(w_in[n % 2], 16 * (n // 2 + 1))
                if n >= 2:
                    pe.wait_ge(w_lo, n - 1)
                for i in range(KC):
                    for o in range(KC):
                        last = nc.tensor.transpose(PS[n % 2][:, i * C + o * P:i * C + (o + 1) * P],
                                                   sq_raw(n)[:, o, i * P:(i + 1) * P], ident[:])
                last.then_inc(w_tp, 1)
            pe.wait_ge(small_in, 16 * SMALL)
            pe.wait_ge(w_lo, NSQ - 1)
            for o in range(4):
                last = nc.tensor.transpose(PS[NSQ % 2][0:L, o * P:(o + 1) * P], kv_raw[:, o, :], ident[:])
            last.then_inc(w_tp, 1)
            pe.wait_ge(w_lo, NSQ)
            for k in range(KC):
                last = nc.tensor.transpose(PS[(NSQ + 1) % 2][:, k * (E + 2):(k + 1) * (E + 2)], rw_raw[:, k * P:(k + 1) * P],
                                           ident[0:E + 2, 0:E + 2])
            last.then_inc(w_tp, 1)
            pe.wait_ge(w_lo, NSQ + 2)
            pe.wait_ge(f_lo[0], (NFW + 1) // 2 + 1)
            pe.wait_ge(f_lo[1], NFW // 2)
            pe.wait_ge(pads, 6)

            pe.sem_inc(xn_turned, PRIMED)

            with pe.Fori(0, NG) as g:
                def three(out_ap, wh, wl, xh, xl, start, stop, skip=False):
                    mm(out_ap, wh, xh, start=start, stop=False, skip_group_check=skip)
                    mm(out_ap, wh, xl, start=False, stop=False, skip_group_check=skip)
                    return mm(out_ap, wl, xh, start=False, stop=stop, skip_group_check=skip)

                def turn_norm(s):
                    for b in range(GB):
                        pe.wait_ge(xn_ready, g * 12 + 4 * s + b + 1)
                        for k in range(KC):
                            last = nc.tensor.transpose(PS[6 + k][:, b * T:(b + 1) * T], tok[:, b, k * P:(k + 1) * P], ident[:])
                        last.then_inc(xn_turned, 1)

                pe.wait_ge(x3_ready, g * 2 + PRIMED)
                turn_norm(0)
                for i in range(4):
                    base = 2 * (i % 2)
                    if i >= 2:
                        pe.wait_ge(rk_lo, g * 4 + 2 * (i - 1))
                    for k in range(KC):
                        c = 2 * i + k
                        pe.wait_ge(mix_hi, g * 8 + c + 1)
                        pe.wait_ge(mix_lo[c % 2], g * 4 + c // 2 + 1)
                        hi, lo = mix[c % 3][:, 0, :], mix[c % 3][:, 1, :]
                        if i == 2:
                            for b in range(GB):
                                o = PS[base + b // 2][:, (b % 2) * C:(b % 2 + 1) * C]
                                t = slice(b * T, (b + 1) * T)
                                first = k == 0 and b % 2 == 0
                                mm(o, hi[:, t], wAh[:, i, k, :], start=first, stop=False, skip_group_check=True)
                                mm(o, hi[:, t], wAl[:, i, k, :], start=False, stop=False, skip_group_check=True)
                                last = mm(o, lo[:, t], wAh[:, i, k, :], start=False, stop=k == 1, skip_group_check=True)
                        else:
                            for m in range(2):
                                ms = slice(m * P, (m + 1) * P)
                                last = three(PS[base + m][:, :], wAh[:, i, k, ms], wAl[:, i, k, ms], hi, lo, k == 0, k == 1)
                        last.then_inc(mix_used, 1)

                def scores(p):
                    u, i = p // 4, p % 4
                    s = u % 2
                    if p == 0:
                        pe.wait_ge(v_ready, g * 2 + 2)
                        pe.wait_ge(g_ready, g * 2 + 2)
                    if p >= 4:
                        pe.wait_ge(pt_ready, g * 32 + p - 3)
                    if i == 0:
                        pe.wait_ge(wkv_in[s], g * 320 + 80 * (u // 2) + 80)
                    mm(PS[i][:, :], kst4[s][:, i, :], rbd[s][:, i, :, :], start=True, stop=True).then_inc(s_ready, 1)

                def mixed(p):
                    u, i = p // 4, p % 4
                    b, e = u % 4, p // 8
                    if p % 8 == 0 and e >= 2:
                        pe.wait_ge(y_copied, g * 4 + e - 1)
                    if i == 0:
                        pe.wait_ge(vpad_ready, g * 8 + u + 1)
                    pe.wait_ge(pt_ready, g * 32 + p + 1)
                    for j in range(4):
                        a = (4 * i + j) * VW - j * N
                        last = mm(PS[4 + e % 2][32 * i:32 * i + 32, (b % 2) * T:(b % 2 + 1) * T], vpad[:, u % 2, a:a + VW],
                                  ring[:, p % 3, j * T:(j + 1) * T], start=j == 0, stop=j == 3, skip_group_check=True)
                    last.then_inc(y_part, 1)

                def norm_mean(e):
                    pe.wait_ge(y_copied, g * 4 + e + 1)
                    mm(PS[6 + e % 2][:, 0:QT], headmean[:], yc[:, (e % 2) * QT:(e % 2 + 1) * QT], start=True, stop=True).then_inc(gn_mean, 1)

                def norm_var(e):
                    pe.wait_ge(gn_sq, g * 4 + e + 1)
                    mm(PS[6 + e % 2][:, 0:QT], headmean[:], gn_x, start=True, stop=True).then_inc(gn_var, 1)

                for p in range(32):
                    scores(p)
                    if p >= 2:
                        mixed(p - 2)
                    if p >= 10 and p % 8 == 2:
                        norm_mean((p - 10) // 8)
                    if p >= 12 and p % 8 == 4:
                        norm_var((p - 12) // 8)
                mixed(30)
                mixed(31)
                norm_mean(3)
                norm_var(3)

                def out_projection(wh, wl, done, hi_ready, lo_ready):
                    for b in range(GB):
                        t = slice(b * T, (b + 1) * T)
                        o = PS[b // 2][:, (b % 2) * C:(b % 2 + 1) * C]
                        for k in range(KC):
                            if b == 0:
                                pe.wait_ge(hi_ready, g * 2 + k + 1)
                                pe.wait_ge(lo_ready, g * 2 + k + 1)
                            mm(o, xT[:, 0, k, t], wh[:, k, :], start=(k == 0 and b % 2 == 0), stop=False, skip_group_check=True)
                            mm(o, xT[:, 0, k, t], wl[:, k, :], start=False, stop=False, skip_group_check=True)
                            last = mm(o, xT[:, 1, k, t], wh[:, k, :], start=False, stop=k == 1, skip_group_check=True)
                        if b % 2:
                            last.then_inc(done, 1)

                out_projection(wAh[:, 4], wAl[:, 4], wo_ready, y_hi, y_lo)

                pe.wait_ge(ctx_arrived, g * 16 + 16)
                pe.sem_inc(waited_pe, 1)
                for b in range(GB):
                    last = nc.tensor.transpose(PS[2][0:L, b * T:(b + 1) * T], cx[:, b, :], ident[:])
                last.then_inc(ctx_turned, 1)
                pe.wait_ge(cT_hi, g + 1)
                pe.wait_ge(cT_lo, g + 1)
                for m in range(2):
                    ms = slice(m * P, (m + 1) * P)
                    three(PS[3 + m][:, :], wKh[:, ms], wKl[:, ms], cT[:, 0, :], cT[:, 1, :], True, True).then_inc(kp_ready, 1)
                for b in range(GB):
                    o = PS[5 if b < 2 else 2][:, (b % 2) * C:(b % 2 + 1) * C]
                    t = slice(b * T, (b + 1) * T)
                    mm(o, cT[:, 0, t], wKh[:, C:2 * C], start=b % 2 == 0, stop=False, skip_group_check=True)
                    mm(o, cT[:, 0, t], wKl[:, C:2 * C], start=False, stop=False, skip_group_check=True)
                    last = mm(o, cT[:, 1, t], wKh[:, C:2 * C], start=False, stop=True, skip_group_check=True)
                    if b % 2:
                        last.then_inc(vp_ready, 1)
                turn_norm(1)
                for m in range(2):
                    ms = slice(m * P, (m + 1) * P)
                    for k in range(KC):
                        if m == 0:
                            pe.wait_ge(xT_hi, g * 4 + k + 1)
                            pe.wait_ge(xT_lo, g * 4 + k + 1)
                        last = three(PS[m][:, :], wXh[:, 0, k, ms], wXl[:, 0, k, ms], xT[:, 0, k, :], xT[:, 1, k, :], k == 0, k == 1)
                    last.then_inc(qp_ready, 1)

                def query_scores(u):
                    s = u % 4
                    pe.wait_ge(xa_in[s], g * 64 + 32 * (u // 4) + 32)
                    for j in range(2):
                        qd = 2 * u + j
                        if qd >= 2:
                            pe.wait_ge(max_ready, g * 16 + qd - 1)
                        else:
                            pe.wait_ge(qk_lo, g * 4 + 4)
                        mm(PS[j][:, :], identb[:], maskS[:].unsqueeze(1).to_broadcast([P, 4, P]), start=True, stop=False,
                           skip_group_check=True)
                    for j in range(2):
                        rows = slice(64 * j, 64 * j + 64)
                        for i in range(4):
                            last = mm(PS[j][:, i * P:(i + 1) * P], qst[s][rows, i, :], kst[s][rows, i, :], start=False,
                                      stop=i == 3, skip_group_check=True)
                        last.then_inc(sm_ready, 1)

                def turn_max(u):
                    pe.wait_ge(nm_step, g * 24 + 3 * u + 3)
                    if u >= 2:
                        pe.wait_ge(nmT_ready, g * 8 + u - 1)
                    nc.tensor.transpose(PS[6 + u % 2][:, :].bitcast(BF16)[0:16, 0:P], nm2[:, u % 2, :], identb[:]).then_inc(nm_turned, 1)

                def key_scores(u):
                    s = u % 4
                    for j in range(2):
                        qd = 2 * u + j
                        if qd >= 2:
                            pe.wait_ge(p_ready, g * 16 + qd - 1)
                        else:
                            pe.wait_ge(xv_ready, g * 2 + 2)
                        mm(PS[2 + j][:, :], identb[:], maskT[:].unsqueeze(1).to_broadcast([P, 4, P]), start=True, stop=False,
                           skip_group_check=True)
                    for j in range(2):
                        rows = slice(64 * j, 64 * j + 64)
                        for i in range(4):
                            mm(PS[2 + j][:, i * P:(i + 1) * P], kst[s][rows, i, :], qst[s][rows, i, :], start=False, stop=False,
                               skip_group_check=True)
                    pe.wait_ge(nmT_ready, g * 8 + u + 1)
                    for j in range(2):
                        for i in range(4):
                            last = mm(PS[2 + j][:, i * P:(i + 1) * P], selH[:, 4 * j + i, :], nmT[:, u % 2, :], start=False,
                                      stop=i == 3, skip_group_check=True)
                        last.then_inc(t_ready, 1)

                def attend(u):
                    for qd in (2 * u, 2 * u + 1):
                        b = qd // 4
                        if qd % 4 == 0:
                            if b >= 2:
                                pe.wait_ge(yo_ready, g * 4 + b - 1)
                            else:
                                pe.wait_ge(xv_ready, g * 2 + 2)
                        pe.wait_ge(p_ready, g * 16 + qd + 1)
                        for i in range(4):
                            h = 8 * (u % 2) + 2 * i + qd % 2
                            last = mm(PS[4 + b % 2][:, h * (XD + 1):(h + 1) * (XD + 1)], ring[:, qd % 4, i * T:(i + 1) * T],
                                      xv[:, b, h, :], start=True, stop=True)
                        last.then_inc(o_part, 1)

                query_scores(0)
                turn_max(0)
                for u in range(8):
                    if u + 1 < 8:
                        query_scores(u + 1)
                    key_scores(u)
                    if u >= 1:
                        attend(u - 1)
                    if u + 1 < 8:
                        turn_max(u + 1)
                attend(7)
                pe.wait_ge(nmT_ready, g * 8 + 8)
                for b in range(GB):
                    pe.wait_ge(yo_ready, g * 4 + b + 1)
                    for k in range(KC):
                        last = nc.tensor.transpose(PS[6 + k][:, b * T:(b + 1) * T], tok[:, b, k * P:(k + 1) * P], ident[:])
                last.then_inc(yo_turned, 1)
                out_projection(wXh[:, 1], wXl[:, 1], wout_ready, yT_hi, yT_lo)

                turn_norm(2)
                for b in range(GB):
                    t = slice(b * T, (b + 1) * T)
                    o = PS[4][:, b * (E + 2):(b + 1) * (E + 2)]
                    for k in range(KC):
                        if b == 0:
                            pe.wait_ge(xT_hi, g * 4 + 2 + k + 1)
                            pe.wait_ge(xT_lo, g * 4 + 2 + k + 1)
                        mm(o, xT[:, 0, k, t], wRh[:, k, :], start=(k == 0 and b == 0), stop=False, skip_group_check=True)
                        mm(o, xT[:, 0, k, t], wRl[:, k, :], start=False, stop=False, skip_group_check=True)
                        last = mm(o, xT[:, 1, k, t], wRh[:, k, :], start=False, stop=k == 1, skip_group_check=True)
                last.then_inc(route_ready, 1)

                def gate_up(j):
                    js = slice(j * P, (j + 1) * P)
                    for bank, wh, wl, ready, used in ((PS[j % 2], wGh, wGl, gate_ready, silu_done),
                                                      (PS[2 + j % 2], wUh, wUl, up_ready, gu_done)):
                        if j >= 2:
                            pe.wait_ge(used, g * FB + j - 1)
                        for k in range(KC):
                            last = three(bank[:, :], wh[:, k, js], wl[:, k, js], xT[:, 0, k, :], xT[:, 1, k, :], k == 0, k == 1)
                        last.then_inc(ready, 1)

                def combine(j):
                    if j >= 2:
                        pe.wait_ge(h_done, g * FB + j - 1)
                    else:
                        pe.wait_ge(cwT_ready, g + 1)
                    mm(PS[4 + j % 2][:, :], selC[:, j * P:(j + 1) * P], cwT, start=True, stop=True).then_inc(cwb_ready, 1)

                def down(j):
                    pe.wait_ge(h_hi, g * FB + j + 1)
                    pe.wait_ge(h_lo, g * FB + j + 1)
                    hi, lo = hT[j % 2][:, 0, :], hT[j % 2][:, 1, :]
                    for b in range(GB):
                        t = slice(b * T, (b + 1) * T)
                        o = PS[6 + b // 2][:, (b % 2) * C:(b % 2 + 1) * C]
                        mm(o, hi[:, t], wDh[:, j, :], start=(j == 0 and b % 2 == 0), stop=False, skip_group_check=True)
                        mm(o, hi[:, t], wDl[:, j, :], start=False, stop=False, skip_group_check=True)
                        last = mm(o, lo[:, t], wDh[:, j, :], start=False, stop=j == FB - 1, skip_group_check=True)
                    last.then_inc(down_done, 1)

                gate_up(0)
                gate_up(1)
                pe.wait_ge(c3_ready, g + 1)
                for b in range(GB):
                    last = nc.tensor.transpose(PS[5][:, :].bitcast(BF16)[0:96, b * T:(b + 1) * T], c3[:, b, :], identb[:])
                last.then_inc(cw_turned, 1)
                combine(0)
                combine(1)
                for j in range(2, FB):
                    gate_up(j)
                    combine(j)
                    down(j - 2)
                down(FB - 2)
                down(FB - 1)

        @block.vector
        def _(dve):
            tt, ts, stt = nc.vector.tensor_tensor, nc.vector.tensor_scalar, nc.vector.scalar_tensor_tensor
            nc.vector.memset(rw_raw, 0.0).then_inc(dk_v, 1)
            dve.wait_ge(dk_a, 1)
            ts(td[:], td[:], 1.0e30, -1.0, ALU.min, ALU.mult).then_inc(dk_v, 1)
            for n in range(NSQ):
                dve.wait_ge(w_hi, n + 1)
                tt(SQ[n][2], PS[n % 2][:, :].rearrange("p (i o) -> p i o", i=KC), SQ[n][1].bitcast(F32), ALU.subtract).then_inc(w_lo, 1)
            dve.wait_ge(w_hi, NSQ + 1)
            tt(wKl[:], PS[NSQ % 2][0:L, :], wKh[:].bitcast(F32), ALU.subtract).then_inc(w_lo, 1)
            dve.wait_ge(w_hi, NSQ + 2)
            tt(wRl[:], PS[(NSQ + 1) % 2][:, 0:KC * (E + 2)].rearrange("p (k e) -> p k e", k=KC), wRh[:].bitcast(F32),
               ALU.subtract).then_inc(w_lo, 1)
            dve.wait_ge(dk_p, 2)
            for h in range(H):
                stt(decay[:, h, :], ident[:], tf[:, h:h + 1], decay[:, h, :], ALU.mult, ALU.add).then_inc(dk_v, 1)
            for n in range(0, NFW, 2):
                dve.wait_ge(f_hi, n + 1)
                tt(FW[n][1], fw_raw(n), FW[n][0].bitcast(F32), ALU.subtract).then_inc(f_lo[0], 1)
            dve.wait_ge(f_hi, NFW + 1)
            tt(wDl[0:64, FB - 1, :], tail_raw, wDh[0:64, FB - 1, :].bitcast(F32), ALU.subtract).then_inc(f_lo[0], 1)
            dve.wait_ge(dk_v, 2 + H)
            dve.wait_ge(consts, CONSTS)

            def pair(bank):
                return bank[:, :].rearrange("p (b c) -> p b c", b=2)

            dve.sem_inc(x3_ready, PRIMED)

            with dve.Fori(0, NG) as g:
                def layer_stats(s, src, lo=0, hi=GB):
                    for b in range(GB):
                        nc.vector.bn_stats(st[:, b, :], src[:, b, :]).then_inc(ln_stats, 1)
                    dve.wait_ge(ln_stats, g * 12 + 4 * s + GB)
                    dve.sem_inc(waited_dve, 1)
                    for b in range(GB):
                        nc.vector.bn_aggr(mv[:, b, :], st[:, b, :]).then_inc(ln_mean, 1)

                def layer_apply(s, src):
                    dve.wait_ge(ln_rstd, g * 3 + s + 1)
                    for b in range(GB):
                        ts(tok[:, b, :], src[:, b, :], mv[:, b, 0:1], rstd[:, b:b + 1], ALU.subtract, ALU.mult).then_inc(xn_ready, 1)

                dve.wait_ge(x_in, g * 16 + 16)
                layer_stats(0, tok)
                layer_apply(0, tok)
                dve.wait_ge(xn_turned, g * 12 + 4 + PRIMED)
                nc.vector.tensor_copy(xnT[:, 1, :, 1:T + 1], PS[7][:, :].rearrange("p (b t) -> p b t", b=GB)).then_inc(xnT_dve, 1)
                dve.wait_ge(out_done, g * 16 + 16 * PRIMED)
                dve.wait_ge(edge_zero, g + 1)
                dve.wait_ge(xnT_act, g + 1)
                tt(XX[:, 0], xnT[:, 0, :, 0:T], xnT[:, 0, :, 1:T + 1], ALU.subtract).then_inc(xx_ready, 1)
                dve.wait_ge(xnT_dve, g + 1)
                tt(XX[:, 1], xnT[:, 1, :, 0:T], xnT[:, 1, :, 1:T + 1], ALU.subtract).then_inc(xx_ready, 1)

                def mixed_input(c):
                    i, k = c // 2, c % 2
                    if c < 2:
                        dve.wait_ge(xx_ready, g * 2 + c + 1)
                    elif c % 2:
                        dve.wait_ge(mix_lo[1], g * 4 + c // 2)
                    else:
                        dve.wait_ge(mix_lo[0], g * 4 + c // 2)
                    stt(xm[:, c % 2, :].rearrange("p (b t) -> p b t", b=GB), XX[:, k], cols[:, MR + i, k:k + 1],
                        xnT[:, k, :, 1:T + 1], ALU.mult, ALU.add).then_inc(xm_ready, 1)

                def mixed_lo(c):
                    dve.wait_ge(mix_hi, g * 8 + c + 1)
                    tt(mix[c % 3][:, 1, :], xm[:, c % 2, :], mix[c % 3][:, 0, :].bitcast(F32), ALU.subtract).then_inc(mix_lo[0], 1)

                def rk_part(n):
                    i, m = n // 2, n % 2
                    dve.wait_ge(rk_hi, g * 4 + n + 1)
                    stt(rkst[m][:, 1, :], PS[2 * i + m][:, :], cols[:, BR + i, m:m + 1], rkst[m][:, 0, :].bitcast(F32),
                        ALU.add, ALU.subtract).then_inc(rk_lo, 1)

                mixed_input(0)
                mixed_input(1)
                for c in range(0, 8, 2):
                    mixed_lo(c)
                    if c + 2 < 8:
                        mixed_input(c + 2)
                        mixed_input(c + 3)
                    if c in (2, 4):
                        rk_part(c - 2)
                        rk_part(c - 1)
                dve.wait_ge(mix_used, g * 8 + 6)
                for q in range(2):
                    tt(tok[:, 2 * q:2 * q + 2, :], pair(PS[q]), bvB[:].unsqueeze(1).to_broadcast([P, 2, C]), ALU.add).then_inc(v_ready, 1)

                dve.wait_ge(mix_used, g * 8 + 8)
                dve.sem_inc(waited_dve, 1)
                nc.vector.memset(AR[:, 0:2048].bitcast(F32), 0.0).then_inc(rbd_zero[0], 2)

                def weigh(p):
                    first = 16 * (p // 16) + 4 * (p % 4)
                    dve.wait_ge(s_ready, g * 32 + p + 1)
                    if p >= 3:
                        dve.wait_ge(y_part, g * 32 + p - 2)
                    tt(ring[:, p % 3, :].rearrange("p (j t) -> p j t", j=4), PS[p % 4][:, :].rearrange("p (j t) -> p j t", j=4),
                       decay[:, first:first + 4, :], ALU.mult).then_inc(pt_ready, 1)

                def center(e):
                    h = slice((e % 2) * QT, (e % 2 + 1) * QT)
                    dve.wait_ge(gn_mean, g * 4 + e + 1)
                    tt(yc[:, h], yc[:, h], PS[6 + e % 2][:, 0:QT], ALU.subtract).then_inc(gn_cent, 1)

                def norm_step(e, n):
                    q, h = e // 2, slice((e % 2) * QT, (e % 2 + 1) * QT)
                    gn_t = PS[6 + e % 2][:, QT:GT]
                    if n == 0:
                        dve.wait_ge(gn_var, g * 4 + e + 1)
                        ins = ts(gn_x, PS[6 + e % 2][:, 0:QT], GN_EPS, None, ALU.add)
                    else:
                        dve.wait_ge(gn_step, g * (4 * GN_STEPS) + e * GN_STEPS + n)
                        if n == 1:
                            ins = ts(gn_y.bitcast(I32), gn_x.bitcast(I32), 1, None, ALU.logical_shift_right)
                        elif n == 2:
                            ins = ts(gn_y.bitcast(I32), gn_y.bitcast(I32), -1.0, float(0x5F3759DF), ALU.mult, ALU.add)
                        elif n == 12:
                            ins = stt(yc[:, h], yc[:, h], cols[:, LNG, q:q + 1], gn_y, ALU.mult, ALU.mult)
                        elif n % 3 == 0:
                            ins = stt(gn_t, gn_y, -0.5, gn_x, ALU.mult, ALU.mult)
                        elif n % 3 == 1:
                            ins = tt(gn_t, gn_t, gn_y, ALU.mult)
                        else:
                            ins = stt(gn_y, gn_t, 1.5, gn_y, ALU.add, ALU.mult)
                    ins.then_inc(gn_step, 1)

                def gate_y(e):
                    q, h = e // 2, slice((e % 2) * QT, (e % 2 + 1) * QT)
                    dve.wait_ge(gn_step, g * (4 * GN_STEPS) + (e + 1) * GN_STEPS)
                    stt(gact[:, q, h], yc[:, h], cols[:, LNB, q:q + 1], gact[:, q, h], ALU.add, ALU.mult).then_inc(y_gated, 1)

                def gated_lo(q):
                    dve.wait_ge(y_hi, g * 2 + q + 1)
                    tt(xT[:, 1, q, :], gact[:, q, :], xT[:, 0, q, :].bitcast(F32), ALU.subtract).then_inc(y_lo, 1)

                def norm_steps(e, n0, n1):
                    for n in range(n0, n1):
                        norm_step(e, n)
                    if n1 == GN_STEPS:
                        gate_y(e)

                for p in range(32):
                    weigh(p)
                    if p >= 11 and p % 8 == 3:
                        center((p - 11) // 8)
                    e, r = (p - 13) // 8, (p - 13) % 8
                    if p >= 13 and r < 5:
                        norm_steps(e, 3 * r, min(3 * r + 3, GN_STEPS))
                norm_steps(2, 9, GN_STEPS)
                center(3)
                gated_lo(0)
                norm_steps(3, 0, GN_STEPS)
                gated_lo(1)
                dve.wait_ge(xbo_ready, g + 1)
                for q in range(2):
                    dve.wait_ge(wo_ready, g * 2 + q + 1)
                    tt(X[:, 2 * q:2 * q + 2, :], pair(PS[q]), X[:, 2 * q:2 * q + 2, :], ALU.add).then_inc(x1_ready, 1)

                dve.wait_ge(cT_hi, g + 1)
                tt(cT[:, 1, :], PS[2][0:L, :], cT[:, 0, :].bitcast(F32), ALU.subtract).then_inc(cT_lo, 1)
                dve.wait_ge(x1_ready, g * 2 + 2)
                layer_stats(1, X)
                for m in range(2):
                    dve.wait_ge(qk_hi, g * 4 + m + 1)
                    tt(stage[m][:, 1, :], PS[3 + m][:, :], stage[m][:, 0, :].bitcast(F32), ALU.subtract).then_inc(qk_lo, 1)
                dve.wait_ge(xv_one, g + 1)
                for q in range(2):
                    dve.wait_ge(vp_ready, g * 2 + q + 1)
                    nc.vector.tensor_copy(xv[:, 2 * q:2 * q + 2, :, 0:XD],
                                          PS[5 if q == 0 else 2][:, :].rearrange("p (b h d) -> p b h d", b=2, h=XH)).then_inc(xv_ready, 1)
                layer_apply(1, X)

                def norm_lo(s, done):
                    for k in range(2):
                        dve.wait_ge(xT_hi, g * 4 + 2 * (s - 1) + k + 1)
                        tt(xT[:, 1, k, :], PS[6 + k][:, :], xT[:, 0, k, :].bitcast(F32), ALU.subtract).then_inc(done, 1)

                norm_lo(1, xT_lo)
                for m in range(2):
                    dve.wait_ge(qk_hi, g * 4 + 2 + m + 1)
                    stt(stage[m][:, 1, :], PS[m][:, :], float(XD) ** -0.5, stage[m][:, 0, :].bitcast(F32), ALU.mult,
                        ALU.subtract).then_inc(qk_lo, 1)

                def maxima(u):
                    if u >= 2:
                        dve.wait_ge(nm_turned, g * 8 + u - 1)
                    for qd in (2 * u, 2 * u + 1):
                        dve.wait_ge(sm_ready, g * 16 + qd + 1)
                        nc.vector.tensor_reduce(nm[:, u % 2, 4 * (qd % 2):4 * (qd % 2) + 4],
                                                PS[qd % 2][:, :].rearrange("p (h t) -> p h t", h=4), AX, ALU.max,
                                                negate=True).then_inc(max_ready, 1)
                    dve.wait_ge(max_ready, g * 16 + 2 * u + 2)
                    nc.vector.tensor_copy(nm2[:, u % 2, 0:8], nm[:, u % 2, :]).then_inc(nm_step, 1)
                    dve.wait_ge(nm_step, g * 24 + 3 * u + 1)
                    tt(nmr[:, u % 2, :], nm[:, u % 2, :], nm2[:, u % 2, 0:8], ALU.subtract).then_inc(nm_step, 1)
                    dve.wait_ge(nm_step, g * 24 + 3 * u + 2)
                    nc.vector.tensor_copy(nm2[:, u % 2, 8:16], nmr[:, u % 2, :]).then_inc(nm_step, 1)

                def attended(b):
                    dve.wait_ge(o_part, g * 16 + 4 * b + 4)
                    o = PS[4 + b % 2][:, 0:XH * (XD + 1)].rearrange("p (h d) -> p h d", h=XH)
                    nc.vector.reciprocal(rec[:, b % 2, :], o[:, :, XD]).then_inc(rec_ready, 1)
                    dve.wait_ge(rec_ready, g * 4 + b + 1)
                    tt(tok[:, b, :].rearrange("p (h d) -> p h d", h=XH), o[:, :, 0:XD], rec[:, b % 2, :].unsqueeze(2).to_broadcast([P, XH, XD]),
                       ALU.mult).then_inc(yo_ready, 1)

                for u in range(8):
                    maxima(u)
                    if u >= 3 and u % 2 == 1:
                        attended((u - 3) // 2)
                attended(3)
                for k in range(2):
                    dve.wait_ge(yT_hi, g * 2 + k + 1)
                    tt(xT[:, 1, k, :], PS[6 + k][:, :], xT[:, 0, k, :].bitcast(F32), ALU.subtract).then_inc(yT_lo, 1)
                for q in range(2):
                    dve.wait_ge(wout_ready, g * 2 + q + 1)
                    tt(X[:, 2 * q:2 * q + 2, :], pair(PS[q]), X[:, 2 * q:2 * q + 2, :], ALU.add).then_inc(x2_ready, 1)

                dve.wait_ge(x2_ready, g * 2 + 2)
                layer_stats(2, X)
                layer_apply(2, X)
                norm_lo(2, xT_lo)

                steps = [0]

                def step(ins):
                    steps[0] += 1
                    ins.then_inc(r_step, 1)
                    dve.wait_ge(r_step, g * R_STEPS + steps[0])

                def over(a, n):
                    return a.unsqueeze(2).to_broadcast([P, GB, n])

                revb = rev[:].unsqueeze(1).to_broadcast([P, GB, E])
                dve.wait_ge(route_ready, g + 1)
                step(nc.vector.tensor_copy(lg, PS[4][:, 0:GB * (E + 2)].rearrange("p (b e) -> p b e", b=GB)))
                logits = lg[:, :, 0:E]
                for o, src, m in ((r_o1, logits, 0), (r_o2, r_l2, 2)):
                    step(nc.vector.tensor_reduce(r_m[:, m, :], src, AX, ALU.max))
                    step(tt(r_a, src, over(r_m[:, m, :], E), ALU.is_equal))
                    step(tt(r_a, r_a, revb, ALU.mult))
                    step(nc.vector.tensor_reduce(r_m[:, m + 1, :], r_a, AX, ALU.max))
                    step(tt(o, r_a, over(r_m[:, m + 1, :], E), ALU.is_equal))
                    if m == 0:
                        step(stt(r_l2, r_o1, -3.0e38, logits, ALU.mult, ALU.add))
                step(tt(r_z[:, :, 0], r_m[:, 2, :], r_m[:, 0, :], ALU.subtract))
                step(ts(r_z[:, :, 1], lg[:, :, E], -1.0, None, ALU.mult))
                assert steps[0] == R_EXP
                dve.wait_ge(r_exp, g + 1)
                step(ts(r_d, r_e, 1.0, None, ALU.add))
                step(nc.vector.reciprocal(r_w, r_d))
                step(tt(r_z[:, :, 0], r_e[:, :, 0], r_w[:, :, 0], ALU.mult))
                step(tt(r_o1, r_o1, over(r_w[:, :, 0], E), ALU.mult))
                step(tt(r_o2, r_o2, over(r_z[:, :, 0], E), ALU.mult))
                step(tt(cw[:, :, 0:E], r_o1, r_o2, ALU.add))
                step(nc.vector.tensor_copy(cw[:, :, E:E + 1], r_w[:, :, 1:2]))
                dve.wait_ge(c3_zero, g + 1)
                step(nc.vector.tensor_copy(c3[:, :, 0:E + 1], cw))
                step(tt(cr, cw, c3[:, :, 0:E + 1], ALU.subtract))
                step(nc.vector.tensor_copy(c3[:, :, 32:32 + E + 1], cr))
                step(tt(cr2, cr, c3[:, :, 32:32 + E + 1], ALU.subtract))
                assert steps[0] == R_STEPS, steps[0]
                nc.vector.tensor_copy(c3[:, :, 64:64 + E + 1], cr2).then_inc(c3_ready, 1)

                for j in range(FB):
                    dve.wait_ge(silu_done, g * FB + j + 1)
                    dve.wait_ge(up_ready, g * FB + j + 1)
                    if j >= 2:
                        dve.wait_ge(h_lo, g * FB + j - 1)
                    tt(ring[:, 2 + j % 2, :], ring[:, j % 2, :], PS[2 + j % 2][:, :], ALU.mult).then_inc(gu_done, 1)
                    dve.wait_ge(cwb_ready, g * FB + j + 1)
                    dve.wait_ge(gu_done, g * FB + j + 1)
                    tt(ring[:, 2 + j % 2, :], ring[:, 2 + j % 2, :], PS[4 + j % 2][:, :], ALU.mult).then_inc(h_done, 1)
                dve.wait_ge(down_done, g * FB + FB)
                for q in range(2):
                    tt(X[:, 2 * q:2 * q + 2, :], pair(PS[6 + q]), X[:, 2 * q:2 * q + 2, :], ALU.add).then_inc(x3_ready, 1)
    return nc


INPUTS = ['x', 'ctx_512', 'L0_attn_Wr', 'L0_attn_br', 'L0_attn_Wk', 'L0_attn_bk', 'L0_attn_Wv', 'L0_attn_bv', 'L0_attn_Wg',
          'L0_attn_bg', 'L0_attn_Wo', 'L0_attn_bo', 'L0_attn_ln_g', 'L0_attn_ln_b', 'L0_attn_maa_k', 'L0_attn_maa_v',
          'L0_attn_maa_r', 'L0_attn_maa_g', 'L0_attn_time_decay', 'L0_attn_time_faaaa', 'L0_xattn_Wq', 'L0_xattn_Wkv_expand',
          'L0_xattn_Wout', 'L0_ffn_router_w', 'L0_ffn_w_gate', 'L0_ffn_w_up', 'L0_ffn_w_down', 'L0_ffn_sw_gate',
          'L0_ffn_sw_up', 'L0_ffn_sw_down', 'L0_ffn_shared_gate_w']


def kernel(**inputs):
    import numpy as np
    import concourse.bacc as bacc
    from concourse.bass_utils import run_bass_kernel_spmd

    nc = bacc.Bacc("TRN2", target_bir_lowering=False, num_devices=1)
    arrays, args = {}, []
    for name in INPUTS:
        a = np.ascontiguousarray(inputs[name])
        arrays[f"in_{name}"] = a
        args.append(nc.dram_tensor(f"in_{name}", a.shape, mybir.dt.from_np(a.dtype), kind="ExternalInput").ap())
    shape = inputs['x'].shape
    args.append(nc.dram_tensor("out_x", shape, F32, kind="ExternalOutput").ap())
    decoder_layer(nc, *args)
    r = run_bass_kernel_spmd(nc, [arrays], core_ids=[0])
    return r.results[0]["out_x"]
```

```python
from contextlib import ExitStack

import concourse.bass as bass
from concourse import mybir

F32 = mybir.dt.float32
F32R = mybir.dt.float32r
BF16 = mybir.dt.bfloat16
I32 = mybir.dt.int32
ALU = mybir.AluOpType
ACT = mybir.ActivationFunctionType
AX = mybir.AxisListType.X

P = 128
NEG = -1.0e30


def decoder_layer(nc, x, ctx_in, Wr, br, Wk, bk, Wv, bv, Wg, bg, Wo, bo, ln_g, ln_b,
                  maa_k, maa_v, maa_r, maa_g, time_decay, time_faaaa, Wq, Wkv, Wout,
                  router_w, w_gate, w_up, w_down, sw_gate, sw_up, sw_down, shared_gate_w, out):
    B, T, C = x.shape
    H = time_decay.shape[0]
    N = C // H
    L = ctx_in.shape[2]
    XH = 16
    XD = C // XH
    E, _, I = w_gate.shape
    SI = sw_gate.shape[1]
    KC = C // P
    GB = 4
    NG = B // GB
    GT = GB * T
    NR = E * I
    NF = NR + SI
    FB = -(-NF // P)
    FP = FB * P
    LN_EPS = 1e-5
    GN_EPS = 1e-5 * 64
    assert T == P and KC == 2 and GT == 512 and N == 8 and XD == 16 and NF - (FB - 1) * P == 64

    es = ExitStack()
    with es:
        def sb(name, shape, dt):
            return es.enter_context(nc.sbuf_tensor(name, shape, dt))

        def sem(name):
            return es.enter_context(nc.semaphore(name))

        ident = sb("ident", [P, P], F32)
        identb = sb("identb", [P, P], BF16)
        wAh = sb("wAh", [P, 5, KC, C], F32R)
        wAl = sb("wAl", [P, 5, KC, C], F32R)
        wXh = sb("wXh", [P, 2, KC, C], F32R)
        wXl = sb("wXl", [P, 2, KC, C], F32R)
        wKh = sb("wKh", [L, 2 * C], F32R)
        wKl = sb("wKl", [L, 2 * C], F32R)
        wGh = sb("wGh", [P, KC, FP], F32R)
        wGl = sb("wGl", [P, KC, FP], F32R)
        wUh = sb("wUh", [P, KC, FP], F32R)
        wUl = sb("wUl", [P, KC, FP], F32R)
        wDh = sb("wDh", [P, FB, C], F32R)
        wDl = sb("wDl", [P, FB, C], F32R)
        wRh = sb("wRh", [P, KC, E + 2], F32R)
        wRl = sb("wRl", [P, KC, E + 2], F32R)
        selC = sb("selC", [96, FP], BF16)
        onesb = sb("onesb", [P, P], BF16)
        maskS = sb("maskS", [P, P], BF16)
        maskT = sb("maskT", [P, P], BF16)
        decay = sb("decay", [P, H, P], F32)
        bvB = sb("bvB", [P, C], F32)
        boB = sb("boB", [P, C], F32)
        cols = sb("cols", [P, 9, KC], F32)
        BR, BK, BG, LNG, LNB, MR, MK, MV, MG = range(9)
        mhalf = sb("mhalf", [P, GB], F32)
        rev = sb("rev", [P, E], F32)

        AF = sb("AF", [P, 6216], F32)
        AR = sb("AR", [P, 5120], F32R)
        dist = AF[:, 5632:5760]
        cx = AF[:, 5192:5448].rearrange("p (b l) -> p b l", b=GB)
        st = sb("st", [P, GB, 6], F32)
        mv = sb("mv", [P, GB, 2], F32)
        ve = sb("ve", [P, GB], F32)
        rstd = sb("rstd", [P, GB], F32)
        headmean = sb("headmean", [P, P], F32)
        yc = sb("yc", [P, GT], F32)
        nm = sb("nm", [P, 2, 4], F32)
        nm2 = sb("nm2", [P, 2, 2, 4], BF16)
        rec = sb("rec", [P, 2, XH], F32)
        td = AF[:, 6016:6016 + H]
        tf = AF[:, 6016 + H:6016 + 2 * H]
        cwT = AF[0:96, 5448:5704].bitcast(BF16)
        c3 = AF[:, 5704:5896].bitcast(BF16).rearrange("p (b n) -> p b n", b=GB)
        taken = [4104]

        def small(n, w):
            taken[0] += n * w
            return AF[:, taken[0] - n * w:taken[0]].rearrange("p (n w) -> p n w", n=n)

        lg = small(GB, E + 2)
        r_m = small(4, GB)
        r_a, r_o1, r_o2, r_l2 = (small(GB, E) for _ in range(4))
        r_z, r_e, r_d, r_w = (small(GB, 2) for _ in range(4))
        cw, cr, cr2 = (small(GB, E + 1) for _ in range(3))

        def tokens(a):
            return AF[:, a:a + GB * C].rearrange("p (b c) -> p b c", b=GB)

        X = tokens(0)
        XX = AF[:, 0:1024].rearrange("p (k b t) -> p k b t", k=KC, b=GB)
        tok = tokens(1024)
        R0 = 2048
        xnT = AF[:, R0:R0 + KC * GB * (T + 1)].rearrange("p (k b t) -> p k b t", k=KC, b=GB)
        xm = AF[:, R0 + 1032:R0 + 2056].rearrange("p (s n) -> p s n", s=2)
        ring = AF[:, R0:R0 + 2048].rearrange("p (s n) -> p s n", s=4)
        gact = AF[:, 4104:5128].rearrange("p (k n) -> p k n", k=KC)
        xv = AF[:, 4104:5192].rearrange("p (b h d) -> p b h d", b=GB, h=XH)
        nmd = AF[:, 5192:6216].bitcast(BF16).rearrange("p (s r h t) -> p s r h t", s=2, r=2, h=4)
        VW = 4 * N
        vpad = AF[:, 5192:6216].rearrange("p (s n) -> p s n", s=2)
        QT = GT // 2
        gn_x, gn_y = ring[:, 3, 0:QT], ring[:, 3, QT:GT]

        def hl(a, n):
            return AR[:, a:a + 2 * n].rearrange("p (s n) -> p s n", s=2)

        mix = [hl(c * 1024, 512) for c in range(3)]
        rst = [hl(3072 + n * 1024, 512) for n in range(2)]
        kst_out = [AF[:, a:a + 1024].bitcast(F32R).rearrange("p (s n) -> p s n", s=2) for a in (4104, 5192)]
        stage = [hl(2048 + n * 1024, 512) for n in range(2)]
        xT = AR[:, 0:2048].rearrange("p (s k n) -> p s k n", s=2, k=KC)
        cT = AR[0:L, 4096:5120].rearrange("p (s n) -> p s n", s=2)
        hT = [hl(2048 + s * 1024, 512) for s in range(2)]
        rbd = [AR[:, s * 2560:s * 2560 + 2048].rearrange("p (a j t) -> p a j t", a=4, j=4) for s in range(2)]
        kst4 = [AR[:, s * 2560 + 2048:s * 2560 + 2560].rearrange("p (a t) -> p a t", a=4) for s in range(2)]
        def xslot(a, n):
            return [AR[:, s * 1536 + a:s * 1536 + a + n] for s in range(3)]

        qst = [t.rearrange("p (a t) -> p a t", a=2) for t in xslot(0, 256)]
        kst = [t.rearrange("p (a t) -> p a t", a=2) for t in xslot(256, 256)]
        qbd = [t.rearrange("p (a j t) -> p a j t", a=2, j=2) for t in xslot(512, 512)]
        kbd = [t.rearrange("p (a j t) -> p a j t", a=2, j=2) for t in xslot(1024, 512)]
        stacks, blocks = xslot(0, 512), xslot(512, 1024)
        XQ = 16
        XS = [len(range(s, XQ, 3)) for s in range(3)]

        rD = nc.dram_tensor("r_parts", (C, 4, GT), F32, kind="Internal").ap()
        kD = nc.dram_tensor("k_parts", (C, 4, GT), F32, kind="Internal").ap()
        qkD = nc.dram_tensor("qk_parts", (C // 64, 2, 64, 4, GT), F32, kind="Internal").ap()

        PS = [es.enter_context(nc.psum_tensor(f"bank{i}", [P, 512], F32)) for i in range(8)]

        w_in = [sem(f"w_in{i}") for i in range(2)]
        small_in = sem("small_in")
        consts = sem("consts")
        w_tp = sem("w_tp")
        w_hi = sem("w_hi")
        w_lo = sem("w_lo")
        f_in = [sem(f"f_in{i}") for i in range(2)]
        f_hi = sem("f_hi")
        f_lo = [sem("f_lo_dve"), sem("f_lo_pool")]
        tail_in = sem("tail_in")
        pads = sem("pads")
        dk_i = sem("dk_i")
        dk_a = sem("dk_a")
        dk_p = sem("dk_p")
        dk_v = sem("dk_v")

        waited_pe = sem("waited_pe")
        waited_pool = sem("waited_pool")
        waited_dve = sem("waited_dve")

        x_in = sem("x_in")
        xres_in = sem("xres_in")
        ctx_arrived = sem("ctx_arrived")
        ln_stats = sem("ln_stats")
        ln_mean = sem("ln_mean")
        ln_var = sem("ln_var")
        ln_rstd = sem("ln_rstd")
        xn_ready = sem("xn_ready")
        xn_turned = sem("xn_turned")
        xnT_act = sem("xnT_act")
        xnT_dve = sem("xnT_dve")
        edge_zero = sem("edge_zero")
        xx_ready = sem("xx_ready")
        xm_ready = sem("xm_ready")
        mix_hi = sem("mix_hi")
        mix_lo = [sem("mix_lo_dve"), sem("mix_lo_pool")]
        mix_used = sem("mix_used")
        rk_hi = sem("rk_hi")
        rk_lo = sem("rk_lo")
        rk_out = [sem("rk_out0"), sem("rk_out1")]
        v_ready = sem("v_ready")
        g_ready = sem("g_ready")
        vpad_zero = sem("vpad_zero")
        vpad_ready = sem("vpad_ready")
        rbd_zero = [sem("rbd_zero0"), sem("rbd_zero1")]
        wkv_in = [sem(f"wkv_in{s}") for s in range(2)]
        s_ready = sem("s_ready")
        pt_ready = sem("pt_ready")
        y_part = sem("y_part")
        y_copied = sem("y_copied")
        gn_mean = sem("gn_mean")
        gn_cent = sem("gn_cent")
        gn_sq = sem("gn_sq")
        gn_var = sem("gn_var")
        gn_step = sem("gn_step")
        y_gated = sem("y_gated")
        y_hi = sem("y_hi")
        y_lo = [sem("y_lo_pool"), sem("y_lo_dve")]
        wo_ready = sem("wo_ready")
        xbo_ready = sem("xbo_ready")
        x1_ready = sem("x1_ready")
        ctx_turned = sem("ctx_turned")
        cT_hi = sem("cT_hi")
        cT_lo = sem("cT_lo")
        kp_ready = sem("kp_ready")
        vp_ready = sem("vp_ready")
        xv_one = sem("xv_one")
        xv_ready = sem("xv_ready")
        xT_hi = sem("xT_hi")
        xT_lo = sem("xT_lo")
        qp_ready = sem("qp_ready")
        qk_hi = sem("qk_hi")
        qk_lo = sem("qk_lo")
        qk_out = [sem("qk_out0"), sem("qk_out1")]
        xbd_zero = [sem(f"xbd_zero{s}") for s in range(3)]
        xa_in = [sem(f"xa_in{s}") for s in range(3)]
        x_scored = sem("x_scored")
        sm_ready = sem("sm_ready")
        max_ready = sem("max_ready")
        nm_step = sem("nm_step")
        nm_diag = [sem("nm_diag_hi"), sem("nm_diag_lo")]
        t_ready = sem("t_ready")
        p_ready = sem("p_ready")
        o_part = sem("o_part")
        rec_ready = sem("rec_ready")
        yo_ready = sem("yo_ready")
        yo_turned = sem("yo_turned")
        yT_hi = sem("yT_hi")
        yT_lo = sem("yT_lo")
        wout_ready = sem("wout_ready")
        x2_ready = sem("x2_ready")
        route_ready = sem("route_ready")
        r_step = sem("r_step")
        r_exp = sem("r_exp")
        c3_zero = sem("c3_zero")
        c3_ready = sem("c3_ready")
        cw_turned = sem("cw_turned")
        cwT_ready = sem("cwT_ready")
        gate_ready = sem("gate_ready")
        up_ready = sem("up_ready")
        cwb_ready = sem("cwb_ready")
        silu_done = sem("silu_done")
        gu_done = sem("gu_done")
        h_done = sem("h_done")
        h_hi = sem("h_hi")
        h_lo = sem("h_lo")
        down_done = sem("down_done")
        x3_ready = sem("x3_ready")
        out_done = sem("out_done")
        PRIMED = 1
        GN_STEPS = 13
        R_EXP = 14
        R_STEPS = 25

        CONSTS = 4 + 4 + 1 + 1 + 3 * 4 + 1 + E + 3

        block = es.enter_context(nc.Block())

        SQ = [(Wr, wAh[:, 0], wAl[:, 0]), (Wk, wAh[:, 1], wAl[:, 1]), (Wv, wAh[:, 2], wAl[:, 2]),
              (Wg, wAh[:, 3], wAl[:, 3]), (Wo, wAh[:, 4], wAl[:, 4]),
              (Wq, wXh[:, 0], wXl[:, 0]), (Wout, wXh[:, 1], wXl[:, 1])]
        NSQ = len(SQ)

        def sq_raw(n):
            return AF[:, 4608 + (n % 2) * 512:5120 + (n % 2) * 512].rearrange("p (o i) -> p o i", o=KC)

        kv_raw = AF[:, 4352:4608].rearrange("p (o l) -> p o l", o=4)
        FW = []
        for hi_t, lo_t, we, ws in ((wGh, wGl, w_gate, sw_gate), (wUh, wUl, w_up, sw_up)):
            for k in range(KC):
                FW.append((hi_t[:, k, 0:NF], lo_t[:, k, 0:NF], NF,
                           [(0, NR, we[:, k * P:(k + 1) * P, :].rearrange("e p i -> p e i"), E),
                            (NR, NF, ws[k * P:(k + 1) * P, :], 0)]))
        wd = w_down.rearrange("e i h -> (e i) h")
        RB = NR // P
        SB = SI // P
        for j0, j1, src in ((0, 6, wd), (6, RB, wd), (RB, RB + SB, sw_down)):
            s0 = (j0 - (RB if j0 >= RB else 0)) * P
            FW.append((wDh[:, j0:j1, :], wDl[:, j0:j1, :], (j1 - j0) * C,
                       [(0, (j1 - j0) * C, src[s0:s0 + (j1 - j0) * P, :].rearrange("(j p) c -> p j c", p=P), j1 - j0)]))
        NFW = len(FW)
        DMA_FW = [len(f[3]) for f in FW]

        FS = 2

        def fw_slot(n, a, b):
            return AF[:, (n % FS) * NF + a:(n % FS) * NF + b]

        def fw_raw(n):
            raw = fw_slot(n, 0, FW[n][2])
            return raw.rearrange("p (j c) -> p j c", c=C) if len(FW[n][0].shape) == 3 else raw

        def fw_part(n, pool_side):
            size = FW[n][0].shape[1]
            cut = (2 * size + 1) // 3
            w = slice(cut, size) if pool_side else slice(0, cut)
            return FW[n][0][:, w], FW[n][1][:, w], fw_raw(n)[:, w]

        def fw_in(n):
            return 16 * sum(DMA_FW[m] for m in range(n % FS, n + 1, FS))

        tail_raw = AF[0:64, 4608:4608 + C]
        rw_raw = AF[0:E + 2, 5760:5760 + C]
        SMALL = 1 + 9 + 4 + 2

        @block.sync
        def _(sp):
            sp.dma_start(kv_raw, Wkv.rearrange("(o p) l -> p o l", p=P)).then_inc(small_in, 16)
            for n, v in ((BR, br), (BK, bk), (BG, bg), (LNG, ln_g), (LNB, ln_b), (MR, maa_r), (MK, maa_k), (MV, maa_v), (MG, maa_g)):
                with nc.allow_non_contiguous_dma(reason="256 values"):
                    sp.dma_start(cols[:, n, :], v.rearrange("(k p) -> p k", p=P)).then_inc(small_in, 16)
            sp.dma_start(td[:], time_decay.partition_broadcast(P)).then_inc(small_in, 16)
            sp.dma_start(tf[:], time_faaaa.partition_broadcast(P)).then_inc(small_in, 16)
            sp.dma_start(bvB[:], bv.partition_broadcast(P)).then_inc(small_in, 16)
            sp.dma_start(boB[:], bo.partition_broadcast(P)).then_inc(small_in, 16)
            sp.wait_ge(dk_v, 1)
            sp.dma_start(rw_raw[0:E, :], router_w).then_inc(small_in, 16)
            sp.dma_start(rw_raw[E:E + 1, :], shared_gate_w.unsqueeze(0)).then_inc(small_in, 16)
            for n in range(NSQ):
                if n >= 2:
                    sp.wait_ge(w_tp, n - 1)
                sp.dma_start(sq_raw(n), SQ[n][0].rearrange("(o p) i -> p o i", p=P)).then_inc(w_in[n % 2], 16)
            for n in range(NFW):
                if n >= FS:
                    sp.wait_ge(f_hi, n - FS + 1)
                    sp.wait_ge(f_lo[0], n - FS + 1)
                    sp.wait_ge(f_lo[1], n - FS + 1)
                for a, b, src, parts in FW[n][3]:
                    dst = fw_slot(n, a, b)
                    if parts:
                        dst = dst.rearrange("p (e i) -> p e i", e=parts)
                    sp.dma_start(dst, src).then_inc(f_in[n % FS], 16)
            sp.wait_ge(w_tp, NSQ + 2)
            sp.dma_start(tail_raw, sw_down[SB * P:SI, :]).then_inc(tail_in, 16)
            sp.wait_ge(f_hi, NFW + 1)
            sp.wait_ge(f_lo[0], NFW + 1)
            sp.wait_ge(f_lo[1], NFW)

            def store_twice(D, m, first, src, done):
                n = src.shape[1]
                dst = bass.AP(D.tensor, m * P * 4 * GT + first * GT, [[4 * GT, P], [n, 2], [1, n]])
                sp.dma_start(dst, src.bitcast(F32).unsqueeze(1).to_broadcast([P, 2, n])).then_inc(done, 16)

            def store_qk(z, m, first, src, done):
                n = src.shape[1]
                for w in range(2):
                    dst = bass.AP(qkD.tensor, ((2 * m + w) * 2 + z) * 256 * GT + first * GT, [[4 * GT, 64], [n, 2], [1, n]])
                    sp.dma_start(dst, src[64 * w:64 * w + 64, :].bitcast(F32).unsqueeze(1).to_broadcast([64, 2, n])).then_inc(done, 16)

            with sp.Fori(0, NG) as g:
                sp.wait_ge(xn_turned, g * 12 + PRIMED)
                sp.dma_start(tok, x[bass.ds(g * GB, GB)].rearrange("b t c -> t b c")).then_inc(x_in, 16)
                for m in range(2):
                    sp.wait_ge(rk_hi, g * 4 + m + 1)
                    sp.wait_ge(rk_lo, g * 4 + m + 1)
                    store_twice(rD, m, 0, AR[:, 3072 + m * 1024:4096 + m * 1024], rk_out[m])
                    sp.wait_ge(rk_hi, g * 4 + m + 3)
                    store_twice(kD, m, 0, kst_out[m][:, 0, :], rk_out[m])
                    sp.wait_ge(rk_lo, g * 4 + m + 3)
                    store_twice(kD, m, 2, kst_out[m][:, 1, :], rk_out[m])
                sp.wait_ge(rk_out[0], g * 48 + 48)
                for u in range(8):
                    half, s, t0 = u // 4, u % 2, (u % 4) * T
                    if u >= 2:
                        sp.wait_ge(s_ready, g * 32 + 4 * (u - 2) + 4)
                    else:
                        sp.wait_ge(rbd_zero[s], g * 2 + 2)
                    if u == 4:
                        sp.wait_ge(rk_out[1], g * 48 + 48)
                    first = half * 4 * P * GT + t0
                    src = bass.AP(kD.tensor, first, [[GT, P], [P * GT, 4], [1, T]])
                    sp.dma_start(kst4[s].bitcast(F32), src).then_inc(wkv_in[s], 16)
                    for j in range(4):
                        src = bass.AP(rD.tensor, first + j * 32 * GT, [[GT, 32], [P * GT, 4], [1, T]])
                        sp.dma_start(rbd[s][32 * j:32 * j + 32, :, j, :].bitcast(F32), src).then_inc(wkv_in[s], 16)
                    if u == 0:
                        sp.wait_ge(xm_ready, g * 8 + 8)
                        sp.dma_start(X, x[bass.ds(g * GB, GB)].rearrange("b t c -> t b c")).then_inc(xres_in, 16)
                sp.wait_ge(y_part, g * 32 + 28)
                sp.dma_start(cx, ctx_in[bass.ds(g * GB, GB)].rearrange("b t c -> t b c")).then_inc(ctx_arrived, 16)
                for n in range(4):
                    m = n % 2
                    sp.wait_ge(qk_hi, g * 4 + n + 1)
                    if n < 2:
                        store_qk(1, m, 0, stage[m][:, 0, :], qk_out[m])
                        sp.wait_ge(qk_lo, g * 4 + n + 1)
                        store_qk(1, m, 2, stage[m][:, 1, :], qk_out[m])
                    else:
                        sp.wait_ge(qk_lo, g * 4 + n + 1)
                        store_qk(0, m, 0, AR[:, 2048 + m * 1024:3072 + m * 1024], qk_out[m])
                for qd in range(XQ):
                    s = qd % 3
                    if qd == 0:
                        sp.wait_ge(qk_out[0], g * 96 + 96)
                    if qd == 2:
                        sp.wait_ge(qk_out[1], g * 96 + 96)
                    if qd >= 3:
                        sp.wait_ge(x_scored, g * 16 + qd - 2)
                    else:
                        sp.wait_ge(xbd_zero[s], g * 2 + 2)
                    first = (qd % 4) * 4 * P * GT + (qd // 4) * T
                    src = bass.AP(qkD.tensor, first, [[GT, P], [P * GT, 4], [1, T]])
                    sp.dma_start(stacks[s].bitcast(F32).rearrange("p (a t) -> p a t", a=4), src).then_inc(xa_in[s], 16)
                    for j in range(2):
                        src = bass.AP(qkD.tensor, first + j * 64 * GT, [[GT, 64], [P * GT, 4], [1, T]])
                        dst = blocks[s].bitcast(F32).rearrange("p (a j t) -> p a j t", a=4, j=2)
                        sp.dma_start(dst[64 * j:64 * j + 64, :, j, :], src).then_inc(xa_in[s], 16)
            sp.wait_ge(out_done, 16 * NG + 16 * PRIMED)

        @block.gpsimd
        def _(pool):
            done = [0]

            def made(ins):
                done[0] += 1
                ins.then_inc(consts, 1)
                pool.wait_ge(consts, done[0])

            for t in (ident, identb):
                made(pool.memset(t[:], 0.0))
                made(pool.affine_select(out=t[:], in_=t[:], compare_op=ALU.not_equal, fill=1.0, base=0,
                                        pattern=[[-1, P]], channel_multiplier=1))
            pool.iota(dist, pattern=[[1, P]], base=-1, channel_multiplier=-1,
                      allow_small_or_imprecise_dtypes=True).then_inc(dk_i, 1)
            pool.wait_ge(dk_i, 1)
            pool.tensor_scalar(dist, dist, 0.0, None, ALU.max).then_inc(dk_p, 1)
            for t, sign in ((maskS, -1), (maskT, 1)):
                made(pool.memset(t[:], 0.0))
                made(pool.affine_select(out=t[:], in_=t[:], compare_op=ALU.is_ge, fill=NEG, base=0,
                                        pattern=[[sign, P]], channel_multiplier=-sign))
            made(pool.memset(onesb[:], 1.0))
            made(pool.memset(selC[:], 0.0))
            for part in range(3):
                rows = selC[32 * part:32 * part + E + 1, :]
                made(pool.memset(rows[:, 0:NF], 1.0))
                made(pool.affine_select(out=rows[:, 0:NF], in_=rows[:, 0:NF], compare_op=ALU.is_ge, fill=0.0,
                                        base=0, pattern=[[1, NF]], channel_multiplier=-I))
                made(pool.affine_select(out=rows[:, 0:NR], in_=rows[:, 0:NR], compare_op=ALU.is_ge, fill=0.0,
                                        base=I - 1, pattern=[[-1, NR]], channel_multiplier=I))
                made(pool.affine_select(out=rows[:, NR:NF], in_=rows[:, NR:NF], compare_op=ALU.is_ge, fill=0.0,
                                        base=-E, pattern=[[0, SI]], channel_multiplier=1))
            made(pool.memset(mhalf[:], -0.5))
            for n in range(E):
                made(pool.memset(rev[:, n:n + 1], float(E - n)))
            made(pool.memset(headmean[:], 1.0 / N))
            for base, sign in ((0, 1), (N - 1, -1)):
                made(pool.affine_select(out=headmean[:], in_=headmean[:], compare_op=ALU.is_ge, fill=0.0, base=base,
                                        pattern=[[-sign * N, P // N], [0, N]], channel_multiplier=sign))
            assert done[0] == CONSTS
            for t in (wGh, wGl, wUh, wUl):
                pool.memset(t[:, :, NF:FP].bitcast(F32), 0.0).then_inc(pads, 1)
            pool.wait_ge(pads, 4)
            for t in (wDh, wDl):
                pool.memset(t[64:P, FB - 1, :].bitcast(F32), 0.0).then_inc(pads, 1)
            pool.wait_ge(pads, 6)
            for n in range(NFW):
                pool.wait_ge(f_hi, n + 1)
                hi, lo, raw = fw_part(n, True)
                pool.tensor_tensor(lo, raw, hi.bitcast(F32), ALU.subtract).then_inc(f_lo[1], 1)
                if n in (1, 3):
                    hs = slice((n // 2) * H // 2, (n // 2 + 1) * H // 2)
                    pool.wait_ge(dk_a, 1 + (n // 2 + 1) * H // 2)
                    pool.affine_select(out=decay[:, hs, :], in_=decay[:, hs, :], compare_op=ALU.is_gt, fill=0.0, base=0,
                                       pattern=[[0, H // 2], [1, P]], channel_multiplier=-1).then_inc(dk_p, 1)

            with pool.Fori(0, NG) as g:
                def layer_rstd(s):
                    pool.wait_ge(ln_mean, g * 12 + 4 * s + 4)
                    pool.sem_inc(waited_pool, 1)
                    pool.tensor_scalar(ve[:], mv[:, :, 1], LN_EPS, None, ALU.add).then_inc(ln_var, 1)
                    pool.wait_ge(ln_var, g * 3 + s + 1)
                    pool.tensor_tensor(rstd[:], ve[:], mhalf[:], ALU.pow).then_inc(ln_rstd, 1)

                layer_rstd(0)
                pool.wait_ge(x3_ready, g * 2 + PRIMED)
                pool.sem_inc(waited_pool, 1)
                pool.memset(xnT[:, :, :, 0:1], 0.0).then_inc(edge_zero, 1)
                for c in range(1, 8, 2):
                    pool.wait_ge(mix_hi, g * 8 + c + 1)
                    pool.tensor_tensor(mix[c % 3][:, 1, :], xm[:, c % 2, :], mix[c % 3][:, 0, :].bitcast(F32),
                                       ALU.subtract).then_inc(mix_lo[1], 1)
                pool.wait_ge(mix_used, g * 8 + 8)
                for m in range(2):
                    pool.wait_ge(rk_out[m], g * 48 + 48)
                pool.sem_inc(waited_pool, 1)
                pool.memset(AF[:, 5192:6216], 0.0).then_inc(vpad_zero, 1)
                pool.memset(AR[:, 2560:4608].bitcast(F32), 0.0).then_inc(rbd_zero[1], 2)
                pool.wait_ge(xres_in, g * 16 + 16)
                pool.tensor_tensor(X, X, boB[:].unsqueeze(1).to_broadcast([P, GB, C]), ALU.add).then_inc(xbo_ready, 1)
                pool.wait_ge(y_hi, g * 2 + 1)
                pool.tensor_tensor(xT[:, 1, 0, :], gact[:, 0, :], xT[:, 0, 0, :].bitcast(F32), ALU.subtract).then_inc(y_lo[0], 1)
                for q in range(2):
                    pool.wait_ge(y_lo[q], g + 1)
                pool.sem_inc(waited_pool, 1)
                pool.memset(xv[:, :, :, XD:XD + 1], 1.0).then_inc(xv_one, 1)
                layer_rstd(1)
                pool.wait_ge(vp_ready, g * 2 + 2)
                pool.wait_ge(qp_ready, g * 2 + 2)
                pool.sem_inc(waited_pool, 1)
                pool.memset(blocks[0].bitcast(F32), 0.0).then_inc(xbd_zero[0], 2)
                for m in range(2):
                    pool.wait_ge(qk_out[m], g * 96 + 96)
                    pool.sem_inc(waited_pool, 1)
                    pool.memset(blocks[1 + m].bitcast(F32), 0.0).then_inc(xbd_zero[1 + m], 2)
                for qd in range(XQ):
                    s = qd % 2
                    pool.wait_ge(nm_step, g * 32 + 2 * qd + 2)
                    if qd >= 2:
                        pool.wait_ge(t_ready, g * 16 + qd - 1)
                    pool.tensor_tensor(nmd[:, s, 1, :, :], identb[:].unsqueeze(1).to_broadcast([P, 4, P]),
                                       nm2[:, s, 1, :].unsqueeze(2).to_broadcast([P, 4, P]), ALU.mult).then_inc(nm_diag[1], 1)
                pool.wait_ge(t_ready, g * 16 + 16)
                pool.sem_inc(waited_pool, 1)
                pool.memset(c3, 0.0).then_inc(c3_zero, 1)
                layer_rstd(2)
                for j in range(FB):
                    pool.wait_ge(h_hi, g * FB + j + 1)
                    pool.tensor_tensor(hT[j % 2][:, 1, :], ring[:, 2 + j % 2, :], hT[j % 2][:, 0, :].bitcast(F32),
                                       ALU.subtract).then_inc(h_lo, 1)

        @block.scalar
        def _(act):
            act.wait_ge(small_in, 16 * SMALL)
            act.activation(td[:], td[:], ACT.Exp).then_inc(dk_a, 1)
            for n in range(NSQ):
                act.wait_ge(w_tp, n + 1)
                act.activation(SQ[n][1], PS[n % 2][:, :].rearrange("p (i o) -> p i o", i=KC), ACT.Copy).then_inc(w_hi, 1)
            act.wait_ge(w_tp, NSQ + 1)
            act.activation(wKh[:], PS[NSQ % 2][0:L, :], ACT.Copy).then_inc(w_hi, 1)
            act.wait_ge(w_tp, NSQ + 2)
            act.activation(wRh[:], PS[(NSQ + 1) % 2][:, 0:KC * (E + 2)].rearrange("p (k e) -> p k e", k=KC), ACT.Copy).then_inc(w_hi, 1)
            for n in range(NFW):
                act.wait_ge(f_in[n % FS], fw_in(n))
                act.activation(FW[n][0], fw_raw(n), ACT.Copy).then_inc(f_hi, 1)
                if n < 4:
                    if n == 0:
                        act.wait_ge(dk_v, 2)
                        act.wait_ge(dk_p, 1)
                    for h in range(n * H // 4, (n + 1) * H // 4):
                        act.activation(decay[:, h, :], dist, ACT.Exp, scale=td[:, h:h + 1]).then_inc(dk_a, 1)
            act.wait_ge(tail_in, 16)
            act.activation(wDh[0:64, FB - 1, :], tail_raw, ACT.Copy).then_inc(f_hi, 1)

            act.sem_inc(out_done, 16 * PRIMED)

            with act.Fori(0, NG) as g:
                act.wait_ge(xn_turned, g * 12 + 4 + PRIMED)
                act.activation(xnT[:, 0, :, 1:T + 1], PS[6][:, :].rearrange("p (b t) -> p b t", b=GB), ACT.Copy).then_inc(xnT_act, 1)

                def mix_part(c):
                    act.wait_ge(xm_ready, g * 8 + c + 1)
                    if c >= 3:
                        act.wait_ge(mix_used, g * 8 + c - 2)
                    act.activation(mix[c % 3][:, 0, :], xm[:, c % 2, :], ACT.Copy).then_inc(mix_hi, 1)

                def rk_part(n):
                    i, m = n // 2, n % 2
                    act.wait_ge(mix_used, g * 8 + 2 * i + 2)
                    act.activation((rst, kst_out)[i][m][:, 0, :], PS[2 * i + m][:, :], ACT.Identity,
                                   bias=cols[:, BR + i, m:m + 1]).then_inc(rk_hi, 1)

                for c in range(4):
                    mix_part(c)
                rk_part(0)
                rk_part(1)
                mix_part(4)
                mix_part(5)
                rk_part(2)
                rk_part(3)
                mix_part(6)
                mix_part(7)
                act.wait_ge(mix_used, g * 8 + 8)
                act.wait_ge(rk_out[0], g * 48 + 48)
                for m in range(2):
                    act.activation(gact[:, m, :], PS[2 + m][:, :], ACT.Silu, bias=cols[:, BG, m:m + 1]).then_inc(g_ready, 1)

                def pad_v(u):
                    half, b = u // 4, u % 4
                    if u == 0:
                        act.wait_ge(v_ready, g * 2 + 2)
                        act.wait_ge(vpad_zero, g + 1)
                    if u >= 2:
                        act.wait_ge(y_part, g * 32 + 4 * (u - 1))
                    act.activation(vpad[:, u % 2, :].rearrange("p (h n) -> p h n", n=VW)[:, :, 0:N],
                                   tok[:, b, half * P:(half + 1) * P].rearrange("p (h n) -> p h n", n=N), ACT.Copy).then_inc(vpad_ready, 1)

                def copy_y(e):
                    act.wait_ge(y_part, g * 32 + 8 * (e + 1))
                    if e >= 2:
                        act.wait_ge(y_gated, g * 4 + e - 1)
                    h = slice((e % 2) * QT, (e % 2 + 1) * QT)
                    act.activation(yc[:, h], PS[4 + e % 2][:, 0:QT], ACT.Copy).then_inc(y_copied, 1)

                def square_y(e):
                    act.wait_ge(gn_cent, g * 4 + e + 1)
                    if e:
                        act.wait_ge(y_gated, g * 4 + e)
                    act.activation(gn_x, yc[:, (e % 2) * QT:(e % 2 + 1) * QT], ACT.Square).then_inc(gn_sq, 1)

                def gated_hi(q):
                    act.wait_ge(y_gated, g * 4 + 2 * q + 2)
                    if q == 0:
                        act.wait_ge(s_ready, g * 32 + 28)
                    act.activation(xT[:, 0, q, :], gact[:, q, :], ACT.Copy).then_inc(y_hi, 1)

                for u in range(4):
                    pad_v(u)
                copy_y(0)
                square_y(0)
                pad_v(4)
                pad_v(5)
                copy_y(1)
                square_y(1)
                pad_v(6)
                pad_v(7)
                copy_y(2)
                square_y(2)
                gated_hi(0)
                copy_y(3)
                square_y(3)
                act.wait_ge(ctx_turned, g + 1)
                act.activation(cT[:, 0, :], PS[2][0:L, :], ACT.Copy).then_inc(cT_hi, 1)
                for m in range(2):
                    act.wait_ge(kp_ready, g * 2 + m + 1)
                    act.activation(stage[m][:, 0, :], PS[3 + m][:, :], ACT.Copy).then_inc(qk_hi, 1)
                gated_hi(1)
                act.wait_ge(xn_turned, g * 12 + 8 + PRIMED)
                for k in range(2):
                    act.activation(xT[:, 0, k, :], PS[6 + k][:, :], ACT.Copy).then_inc(xT_hi, 1)
                for m in range(2):
                    act.wait_ge(qp_ready, g * 2 + m + 1)
                    act.wait_ge(qk_out[m], g * 96 + 64)
                    act.activation(stage[m][:, 0, :], PS[m][:, :], ACT.Copy, scale=float(XD) ** -0.5).then_inc(qk_hi, 1)

                def exps(qd):
                    act.wait_ge(t_ready, g * 16 + qd + 1)
                    if qd >= 4:
                        act.wait_ge(o_part, g * 16 + qd - 3)
                    act.activation(ring[:, qd % 4, :], PS[2 + qd % 2][:, :], ACT.Exp).then_inc(p_ready, 1)

                for qd in range(XQ):
                    exps(qd)
                act.wait_ge(yo_turned, g + 1)
                for k in range(2):
                    act.activation(xT[:, 0, k, :], PS[6 + k][:, :], ACT.Copy).then_inc(yT_hi, 1)
                act.wait_ge(xn_turned, g * 12 + 12 + PRIMED)
                for k in range(2):
                    act.activation(xT[:, 0, k, :], PS[6 + k][:, :], ACT.Copy).then_inc(xT_hi, 1)
                act.wait_ge(r_step, g * R_STEPS + R_EXP)
                act.activation(r_e[:], r_z[:], ACT.Exp).then_inc(r_exp, 1)

                def silu(j):
                    act.wait_ge(gate_ready, g * FB + j + 1)
                    if j >= 2:
                        act.wait_ge(gu_done, g * FB + j - 1)
                    act.activation(ring[:, j % 2, :], PS[j % 2][:, :], ACT.Silu).then_inc(silu_done, 1)

                silu(0)
                silu(1)
                act.wait_ge(cw_turned, g + 1)
                act.activation(cwT, PS[5][:, :].bitcast(BF16)[0:96, 0:GT], ACT.Copy).then_inc(cwT_ready, 1)
                for j in range(FB):
                    act.wait_ge(h_done, g * FB + j + 1)
                    if j >= 2:
                        act.wait_ge(down_done, g * FB + j - 1)
                    act.activation(hT[j % 2][:, 0, :], ring[:, 2 + j % 2, :], ACT.Copy).then_inc(h_hi, 1)
                    if j + 2 < FB:
                        silu(j + 2)
                act.wait_ge(x3_ready, g * 2 + 2 + PRIMED)
                act.dma_start(out[bass.ds(g * GB, GB)].rearrange("b t c -> t b c"), X).then_inc(out_done, 16)

        @block.tensor
        def _(pe):
            mm = nc.tensor.matmul
            pe.wait_ge(consts, 4)
            for n in range(NSQ):
                pe.wait_ge(w_in[n % 2], 16 * (n // 2 + 1))
                if n >= 2:
                    pe.wait_ge(w_lo, n - 1)
                for i in range(KC):
                    for o in range(KC):
                        last = nc.tensor.transpose(PS[n % 2][:, i * C + o * P:i * C + (o + 1) * P],
                                                   sq_raw(n)[:, o, i * P:(i + 1) * P], ident[:])
                last.then_inc(w_tp, 1)
            pe.wait_ge(small_in, 16 * SMALL)
            pe.wait_ge(w_lo, NSQ - 1)
            for o in range(4):
                last = nc.tensor.transpose(PS[NSQ % 2][0:L, o * P:(o + 1) * P], kv_raw[:, o, :], ident[:])
            last.then_inc(w_tp, 1)
            pe.wait_ge(w_lo, NSQ)
            for k in range(KC):
                last = nc.tensor.transpose(PS[(NSQ + 1) % 2][:, k * (E + 2):(k + 1) * (E + 2)], rw_raw[:, k * P:(k + 1) * P],
                                           ident[0:E + 2, 0:E + 2])
            last.then_inc(w_tp, 1)
            pe.wait_ge(w_lo, NSQ + 2)
            pe.wait_ge(f_lo[0], NFW + 1)
            pe.wait_ge(f_lo[1], NFW)
            pe.wait_ge(pads, 6)

            pe.sem_inc(xn_turned, PRIMED)

            with pe.Fori(0, NG) as g:
                def three(out_ap, wh, wl, xh, xl, start, stop, skip=False):
                    mm(out_ap, wh, xh, start=start, stop=False, skip_group_check=skip)
                    mm(out_ap, wh, xl, start=False, stop=False, skip_group_check=skip)
                    return mm(out_ap, wl, xh, start=False, stop=stop, skip_group_check=skip)

                def turn_norm(s):
                    for b in range(GB):
                        pe.wait_ge(xn_ready, g * 12 + 4 * s + b + 1)
                        for k in range(KC):
                            last = nc.tensor.transpose(PS[6 + k][:, b * T:(b + 1) * T], tok[:, b, k * P:(k + 1) * P], ident[:])
                        last.then_inc(xn_turned, 1)

                pe.wait_ge(x3_ready, g * 2 + PRIMED)
                turn_norm(0)
                for i in range(4):
                    base = 2 * (i % 2)
                    if i >= 2:
                        pe.wait_ge(rk_lo, g * 4 + 2 * (i - 1))
                    for k in range(KC):
                        c = 2 * i + k
                        pe.wait_ge(mix_hi, g * 8 + c + 1)
                        pe.wait_ge(mix_lo[c % 2], g * 4 + c // 2 + 1)
                        hi, lo = mix[c % 3][:, 0, :], mix[c % 3][:, 1, :]
                        if i == 2:
                            for b in range(GB):
                                o = PS[base + b // 2][:, (b % 2) * C:(b % 2 + 1) * C]
                                t = slice(b * T, (b + 1) * T)
                                first = k == 0 and b % 2 == 0
                                mm(o, hi[:, t], wAh[:, i, k, :], start=first, stop=False, skip_group_check=True)
                                mm(o, hi[:, t], wAl[:, i, k, :], start=False, stop=False, skip_group_check=True)
                                last = mm(o, lo[:, t], wAh[:, i, k, :], start=False, stop=k == 1, skip_group_check=True)
                        else:
                            for m in range(2):
                                ms = slice(m * P, (m + 1) * P)
                                last = three(PS[base + m][:, :], wAh[:, i, k, ms], wAl[:, i, k, ms], hi, lo, k == 0, k == 1)
                        last.then_inc(mix_used, 1)

                def scores(p):
                    u, i = p // 4, p % 4
                    s = u % 2
                    if p == 0:
                        pe.wait_ge(v_ready, g * 2 + 2)
                        pe.wait_ge(g_ready, g * 2 + 2)
                    if p >= 4:
                        pe.wait_ge(pt_ready, g * 32 + p - 3)
                    if i == 0:
                        pe.wait_ge(wkv_in[s], g * 320 + 80 * (u // 2) + 80)
                    mm(PS[i][:, :], kst4[s][:, i, :], rbd[s][:, i, :, :], start=True, stop=True).then_inc(s_ready, 1)

                def mixed(p):
                    u, i = p // 4, p % 4
                    b, e = u % 4, p // 8
                    if p % 8 == 0 and e >= 2:
                        pe.wait_ge(y_copied, g * 4 + e - 1)
                    if i == 0:
                        pe.wait_ge(vpad_ready, g * 8 + u + 1)
                    pe.wait_ge(pt_ready, g * 32 + p + 1)
                    for j in range(4):
                        a = (4 * i + j) * VW - j * N
                        last = mm(PS[4 + e % 2][32 * i:32 * i + 32, (b % 2) * T:(b % 2 + 1) * T], vpad[:, u % 2, a:a + VW],
                                  ring[:, p % 3, j * T:(j + 1) * T], start=j == 0, stop=j == 3, skip_group_check=True)
                    last.then_inc(y_part, 1)

                def norm_mean(e):
                    pe.wait_ge(y_copied, g * 4 + e + 1)
                    mm(PS[6 + e % 2][:, 0:QT], headmean[:], yc[:, (e % 2) * QT:(e % 2 + 1) * QT], start=True, stop=True).then_inc(gn_mean, 1)

                def norm_var(e):
                    pe.wait_ge(gn_sq, g * 4 + e + 1)
                    mm(PS[6 + e % 2][:, 0:QT], headmean[:], gn_x, start=True, stop=True).then_inc(gn_var, 1)

                for p in range(32):
                    scores(p)
                    if p >= 3:
                        mixed(p - 3)
                    if p >= 11 and p % 8 == 3:
                        norm_mean((p - 11) // 8)
                    if p >= 13 and p % 8 == 5:
                        norm_var((p - 13) // 8)
                mixed(29)
                mixed(30)
                mixed(31)
                norm_mean(3)
                pe.wait_ge(ctx_arrived, g * 16 + 16)
                pe.sem_inc(waited_pe, 1)
                for b in range(GB):
                    last = nc.tensor.transpose(PS[2][0:L, b * T:(b + 1) * T], cx[:, b, :], ident[:])
                last.then_inc(ctx_turned, 1)
                norm_var(3)
                pe.wait_ge(cT_hi, g + 1)
                pe.wait_ge(cT_lo, g + 1)
                for m in range(2):
                    ms = slice(m * P, (m + 1) * P)
                    three(PS[3 + m][:, :], wKh[:, ms], wKl[:, ms], cT[:, 0, :], cT[:, 1, :], True, True).then_inc(kp_ready, 1)
                for b in range(GB):
                    o = PS[5 if b < 2 else 2][:, (b % 2) * C:(b % 2 + 1) * C]
                    t = slice(b * T, (b + 1) * T)
                    mm(o, cT[:, 0, t], wKh[:, C:2 * C], start=b % 2 == 0, stop=False, skip_group_check=True)
                    mm(o, cT[:, 0, t], wKl[:, C:2 * C], start=False, stop=False, skip_group_check=True)
                    last = mm(o, cT[:, 1, t], wKh[:, C:2 * C], start=False, stop=True, skip_group_check=True)
                    if b % 2:
                        last.then_inc(vp_ready, 1)

                def out_projection(wh, wl, done, hi_ready, lo_ready):
                    for k in range(KC):
                        for b in range(GB):
                            t = slice(b * T, (b + 1) * T)
                            o = PS[b // 2][:, (b % 2) * C:(b % 2 + 1) * C]
                            if b == 0:
                                pe.wait_ge(hi_ready, g * 2 + k + 1)
                                pe.wait_ge(*lo_ready[k])
                            mm(o, xT[:, 0, k, t], wh[:, k, :], start=(k == 0 and b % 2 == 0), stop=False, skip_group_check=True)
                            mm(o, xT[:, 0, k, t], wl[:, k, :], start=False, stop=False, skip_group_check=True)
                            last = mm(o, xT[:, 1, k, t], wh[:, k, :], start=False, stop=k == 1, skip_group_check=True)
                            if k == 1 and b % 2:
                                last.then_inc(done, 1)

                out_projection(wAh[:, 4], wAl[:, 4], wo_ready, y_hi, [(y_lo[0], g + 1), (y_lo[1], g + 1)])

                turn_norm(1)
                for m in range(2):
                    ms = slice(m * P, (m + 1) * P)
                    for k in range(KC):
                        if m == 0:
                            pe.wait_ge(xT_hi, g * 4 + k + 1)
                            pe.wait_ge(xT_lo, g * 4 + k + 1)
                        last = three(PS[m][:, :], wXh[:, 0, k, ms], wXl[:, 0, k, ms], xT[:, 0, k, :], xT[:, 1, k, :], k == 0, k == 1)
                    last.then_inc(qp_ready, 1)

                def query_scores(qd):
                    s, bank = qd % 3, PS[qd % 2]
                    pe.wait_ge(xa_in[s], g * (48 * XS[s]) + 48 * (qd // 3) + 48)
                    if qd >= 2:
                        pe.wait_ge(max_ready, g * 16 + qd - 1)
                    else:
                        pe.wait_ge(qk_lo, g * 4 + 4)
                    mm(bank[:, :], identb[:], maskS[:].unsqueeze(1).to_broadcast([P, 4, P]), start=True, stop=False,
                       skip_group_check=True)
                    for i in range(2):
                        last = mm(bank[:, i * 2 * P:(i + 1) * 2 * P], qst[s][:, i, :], kbd[s][:, i, :, :], start=False,
                                  stop=i == 1, skip_group_check=True)
                    last.then_inc(sm_ready, 1)

                def key_scores(qd):
                    s, bank = qd % 3, PS[2 + qd % 2]
                    if qd >= 2:
                        pe.wait_ge(p_ready, g * 16 + qd - 1)
                    else:
                        pe.wait_ge(xv_ready, g * 2 + 2)
                    mm(bank[:, :], identb[:], maskT[:].unsqueeze(1).to_broadcast([P, 4, P]), start=True, stop=False,
                       skip_group_check=True)
                    for i in range(2):
                        last = mm(bank[:, i * 2 * P:(i + 1) * 2 * P], kst[s][:, i, :], qbd[s][:, i, :, :], start=False, stop=False,
                                  skip_group_check=True)
                    last.then_inc(x_scored, 1)

                def less_maxima(qd):
                    bank = PS[2 + qd % 2]
                    for part in range(2):
                        pe.wait_ge(nm_diag[part], g * 16 + qd + 1)
                        last = mm(bank[:, :], onesb[:], nmd[:, qd % 2, part, :, :], start=False, stop=part == 1,
                                  skip_group_check=True)
                    last.then_inc(t_ready, 1)

                def attend(qd):
                    b = qd // 4
                    if qd % 4 == 0:
                        if b >= 2:
                            pe.wait_ge(yo_ready, g * 4 + b - 1)
                        else:
                            pe.wait_ge(xv_ready, g * 2 + 2)
                    pe.wait_ge(p_ready, g * 16 + qd + 1)
                    for n in range(4):
                        h = 4 * (qd % 4) + n
                        last = mm(PS[4 + b % 2][:, h * (XD + 1):(h + 1) * (XD + 1)], ring[:, qd % 4, n * T:(n + 1) * T],
                                  xv[:, b, h, :], start=True, stop=True)
                    last.then_inc(o_part, 1)

                query_scores(0)
                key_scores(0)
                for qd in range(XQ):
                    if qd + 1 < XQ:
                        query_scores(qd + 1)
                        key_scores(qd + 1)
                    less_maxima(qd)
                    if qd >= 1:
                        attend(qd - 1)
                attend(XQ - 1)
                for b in range(GB):
                    pe.wait_ge(yo_ready, g * 4 + b + 1)
                    for k in range(KC):
                        last = nc.tensor.transpose(PS[6 + k][:, b * T:(b + 1) * T], tok[:, b, k * P:(k + 1) * P], ident[:])
                last.then_inc(yo_turned, 1)
                out_projection(wXh[:, 1], wXl[:, 1], wout_ready, yT_hi, [(yT_lo, g * 2 + 1), (yT_lo, g * 2 + 2)])

                turn_norm(2)
                for b in range(GB):
                    t = slice(b * T, (b + 1) * T)
                    o = PS[4][:, b * (E + 2):(b + 1) * (E + 2)]
                    for k in range(KC):
                        if b == 0:
                            pe.wait_ge(xT_hi, g * 4 + 2 + k + 1)
                            pe.wait_ge(xT_lo, g * 4 + 2 + k + 1)
                        mm(o, xT[:, 0, k, t], wRh[:, k, :], start=(k == 0 and b == 0), stop=False, skip_group_check=True)
                        mm(o, xT[:, 0, k, t], wRl[:, k, :], start=False, stop=False, skip_group_check=True)
                        last = mm(o, xT[:, 1, k, t], wRh[:, k, :], start=False, stop=k == 1, skip_group_check=True)
                last.then_inc(route_ready, 1)

                def gate_up(j):
                    js = slice(j * P, (j + 1) * P)
                    for bank, wh, wl, ready, used in ((PS[j % 2], wGh, wGl, gate_ready, silu_done),
                                                      (PS[2 + j % 2], wUh, wUl, up_ready, gu_done)):
                        if j >= 2:
                            pe.wait_ge(used, g * FB + j - 1)
                        for k in range(KC):
                            last = three(bank[:, :], wh[:, k, js], wl[:, k, js], xT[:, 0, k, :], xT[:, 1, k, :], k == 0, k == 1)
                        last.then_inc(ready, 1)

                def combine(j):
                    if j >= 2:
                        pe.wait_ge(h_done, g * FB + j - 1)
                    else:
                        pe.wait_ge(cwT_ready, g + 1)
                    mm(PS[4 + j % 2][:, :], selC[:, j * P:(j + 1) * P], cwT, start=True, stop=True).then_inc(cwb_ready, 1)

                def down(j):
                    pe.wait_ge(h_hi, g * FB + j + 1)
                    pe.wait_ge(h_lo, g * FB + j + 1)
                    hi, lo = hT[j % 2][:, 0, :], hT[j % 2][:, 1, :]
                    for b in range(GB):
                        t = slice(b * T, (b + 1) * T)
                        o = PS[6 + b // 2][:, (b % 2) * C:(b % 2 + 1) * C]
                        mm(o, hi[:, t], wDh[:, j, :], start=(j == 0 and b % 2 == 0), stop=False, skip_group_check=True)
                        mm(o, hi[:, t], wDl[:, j, :], start=False, stop=False, skip_group_check=True)
                        last = mm(o, lo[:, t], wDh[:, j, :], start=False, stop=j == FB - 1, skip_group_check=True)
                    last.then_inc(down_done, 1)

                gate_up(0)
                gate_up(1)
                pe.wait_ge(c3_ready, g + 1)
                for b in range(GB):
                    last = nc.tensor.transpose(PS[5][:, :].bitcast(BF16)[0:96, b * T:(b + 1) * T], c3[:, b, :], identb[:])
                last.then_inc(cw_turned, 1)
                combine(0)
                combine(1)
                for j in range(2, FB):
                    gate_up(j)
                    combine(j)
                    down(j - 2)
                down(FB - 2)
                down(FB - 1)

        @block.vector
        def _(dve):
            tt, ts, stt = nc.vector.tensor_tensor, nc.vector.tensor_scalar, nc.vector.scalar_tensor_tensor
            nc.vector.memset(rw_raw, 0.0).then_inc(dk_v, 1)
            dve.wait_ge(dk_a, 1)
            ts(td[:], td[:], 1.0e30, -1.0, ALU.min, ALU.mult).then_inc(dk_v, 1)
            for n in range(NSQ):
                dve.wait_ge(w_hi, n + 1)
                tt(SQ[n][2], PS[n % 2][:, :].rearrange("p (i o) -> p i o", i=KC), SQ[n][1].bitcast(F32), ALU.subtract).then_inc(w_lo, 1)
            dve.wait_ge(w_hi, NSQ + 1)
            tt(wKl[:], PS[NSQ % 2][0:L, :], wKh[:].bitcast(F32), ALU.subtract).then_inc(w_lo, 1)
            dve.wait_ge(w_hi, NSQ + 2)
            tt(wRl[:], PS[(NSQ + 1) % 2][:, 0:KC * (E + 2)].rearrange("p (k e) -> p k e", k=KC), wRh[:].bitcast(F32),
               ALU.subtract).then_inc(w_lo, 1)
            for n in range(NFW):
                dve.wait_ge(f_hi, n + 1)
                hi, lo, raw = fw_part(n, False)
                tt(lo, raw, hi.bitcast(F32), ALU.subtract).then_inc(f_lo[0], 1)
                if n in (2, 4):
                    dve.wait_ge(dk_p, n // 2 + 1)
                    for h in range((n // 2 - 1) * H // 2, (n // 2) * H // 2):
                        stt(decay[:, h, :], ident[:], tf[:, h:h + 1], decay[:, h, :], ALU.mult, ALU.add).then_inc(dk_v, 1)
            dve.wait_ge(f_hi, NFW + 1)
            tt(wDl[0:64, FB - 1, :], tail_raw, wDh[0:64, FB - 1, :].bitcast(F32), ALU.subtract).then_inc(f_lo[0], 1)
            dve.wait_ge(dk_v, 2 + H)
            dve.wait_ge(consts, CONSTS)

            def pair(bank):
                return bank[:, :].rearrange("p (b c) -> p b c", b=2)

            dve.sem_inc(x3_ready, PRIMED)

            with dve.Fori(0, NG) as g:
                def layer_stats(s, src):
                    for b in range(GB):
                        nc.vector.bn_stats(st[:, b, :], src[:, b, :]).then_inc(ln_stats, 1)
                    dve.wait_ge(ln_stats, g * 12 + 4 * s + GB)
                    dve.sem_inc(waited_dve, 1)
                    for b in range(GB):
                        nc.vector.bn_aggr(mv[:, b, :], st[:, b, :]).then_inc(ln_mean, 1)

                def layer_apply(s, src):
                    dve.wait_ge(ln_rstd, g * 3 + s + 1)
                    for b in range(GB):
                        ts(tok[:, b, :], src[:, b, :], mv[:, b, 0:1], rstd[:, b:b + 1], ALU.subtract, ALU.mult).then_inc(xn_ready, 1)

                dve.wait_ge(x_in, g * 16 + 16)
                layer_stats(0, tok)
                layer_apply(0, tok)
                dve.wait_ge(xn_turned, g * 12 + 4 + PRIMED)
                nc.vector.tensor_copy(xnT[:, 1, :, 1:T + 1], PS[7][:, :].rearrange("p (b t) -> p b t", b=GB)).then_inc(xnT_dve, 1)
                dve.wait_ge(out_done, g * 16 + 16 * PRIMED)
                dve.wait_ge(edge_zero, g + 1)
                dve.wait_ge(xnT_act, g + 1)
                tt(XX[:, 0], xnT[:, 0, :, 0:T], xnT[:, 0, :, 1:T + 1], ALU.subtract).then_inc(xx_ready, 1)
                dve.wait_ge(xnT_dve, g + 1)
                tt(XX[:, 1], xnT[:, 1, :, 0:T], xnT[:, 1, :, 1:T + 1], ALU.subtract).then_inc(xx_ready, 1)

                def mixed_input(c):
                    i, k = c // 2, c % 2
                    if c < 2:
                        dve.wait_ge(xx_ready, g * 2 + c + 1)
                    elif c % 2:
                        dve.wait_ge(mix_lo[1], g * 4 + c // 2)
                    else:
                        dve.wait_ge(mix_lo[0], g * 4 + c // 2)
                    stt(xm[:, c % 2, :].rearrange("p (b t) -> p b t", b=GB), XX[:, k], cols[:, MR + i, k:k + 1],
                        xnT[:, k, :, 1:T + 1], ALU.mult, ALU.add).then_inc(xm_ready, 1)

                def mixed_lo(c):
                    dve.wait_ge(mix_hi, g * 8 + c + 1)
                    tt(mix[c % 3][:, 1, :], xm[:, c % 2, :], mix[c % 3][:, 0, :].bitcast(F32), ALU.subtract).then_inc(mix_lo[0], 1)

                def rk_part(n):
                    i, m = n // 2, n % 2
                    dve.wait_ge(rk_hi, g * 4 + n + 1)
                    to = (rst, kst_out)[i][m]
                    stt(to[:, 1, :], PS[2 * i + m][:, :], cols[:, BR + i, m:m + 1], to[:, 0, :].bitcast(F32),
                        ALU.add, ALU.subtract).then_inc(rk_lo, 1)

                mixed_input(0)
                mixed_input(1)
                for c in range(0, 8, 2):
                    mixed_lo(c)
                    if c + 2 < 8:
                        mixed_input(c + 2)
                        mixed_input(c + 3)
                    if c in (2, 4):
                        rk_part(c - 2)
                        rk_part(c - 1)
                dve.wait_ge(mix_used, g * 8 + 6)
                for q in range(2):
                    tt(tok[:, 2 * q:2 * q + 2, :], pair(PS[q]), bvB[:].unsqueeze(1).to_broadcast([P, 2, C]), ALU.add).then_inc(v_ready, 1)

                for n in range(2):
                    dve.wait_ge(mix_used, g * 8 + 7 + n)
                    dve.sem_inc(waited_dve, 1)
                    nc.vector.memset(AR[:, n * 1024:(n + 1) * 1024].bitcast(F32), 0.0).then_inc(rbd_zero[0], 1)

                def weigh(p):
                    first = 16 * (p // 16) + 4 * (p % 4)
                    dve.wait_ge(s_ready, g * 32 + p + 1)
                    if p >= 3:
                        dve.wait_ge(y_part, g * 32 + p - 2)
                    tt(ring[:, p % 3, :].rearrange("p (j t) -> p j t", j=4), PS[p % 4][:, :].rearrange("p (j t) -> p j t", j=4),
                       decay[:, first:first + 4, :], ALU.mult).then_inc(pt_ready, 1)

                def center(e):
                    h = slice((e % 2) * QT, (e % 2 + 1) * QT)
                    dve.wait_ge(gn_mean, g * 4 + e + 1)
                    tt(yc[:, h], yc[:, h], PS[6 + e % 2][:, 0:QT], ALU.subtract).then_inc(gn_cent, 1)

                def norm_step(e, n):
                    q, h = e // 2, slice((e % 2) * QT, (e % 2 + 1) * QT)
                    gn_t = PS[6 + e % 2][:, QT:GT]
                    if n == 0:
                        dve.wait_ge(gn_var, g * 4 + e + 1)
                        ins = ts(gn_x, PS[6 + e % 2][:, 0:QT], GN_EPS, None, ALU.add)
                    else:
                        dve.wait_ge(gn_step, g * (4 * GN_STEPS) + e * GN_STEPS + n)
                        if n == 1:
                            ins = ts(gn_y.bitcast(I32), gn_x.bitcast(I32), 1, None, ALU.logical_shift_right)
                        elif n == 2:
                            ins = ts(gn_y.bitcast(I32), gn_y.bitcast(I32), -1.0, float(0x5F3759DF), ALU.mult, ALU.add)
                        elif n == 12:
                            ins = stt(yc[:, h], yc[:, h], cols[:, LNG, q:q + 1], gn_y, ALU.mult, ALU.mult)
                        elif n % 3 == 0:
                            ins = stt(gn_t, gn_y, -0.5, gn_x, ALU.mult, ALU.mult)
                        elif n % 3 == 1:
                            ins = tt(gn_t, gn_t, gn_y, ALU.mult)
                        else:
                            ins = stt(gn_y, gn_t, 1.5, gn_y, ALU.add, ALU.mult)
                    ins.then_inc(gn_step, 1)

                def gate_y(e):
                    q, h = e // 2, slice((e % 2) * QT, (e % 2 + 1) * QT)
                    dve.wait_ge(gn_step, g * (4 * GN_STEPS) + (e + 1) * GN_STEPS)
                    stt(gact[:, q, h], yc[:, h], cols[:, LNB, q:q + 1], gact[:, q, h], ALU.add, ALU.mult).then_inc(y_gated, 1)

                def gated_lo(q):
                    dve.wait_ge(y_hi, g * 2 + q + 1)
                    tt(xT[:, 1, q, :], gact[:, q, :], xT[:, 0, q, :].bitcast(F32), ALU.subtract).then_inc(y_lo[1], 1)

                def norm_steps(e, n0, n1):
                    for n in range(n0, n1):
                        norm_step(e, n)
                    if n1 == GN_STEPS:
                        gate_y(e)

                for p in range(32):
                    weigh(p)
                    if p >= 11 and p % 8 == 3:
                        center((p - 11) // 8)
                    e, r = (p - 13) // 8, (p - 13) % 8
                    if p >= 13 and r < 5:
                        norm_steps(e, 3 * r, min(3 * r + 3, GN_STEPS))
                norm_steps(2, 9, GN_STEPS)
                center(3)
                dve.wait_ge(cT_hi, g + 1)
                tt(cT[:, 1, :], PS[2][0:L, :], cT[:, 0, :].bitcast(F32), ALU.subtract).then_inc(cT_lo, 1)
                norm_steps(3, 0, GN_STEPS)
                gated_lo(1)
                for m in range(2):
                    dve.wait_ge(qk_hi, g * 4 + m + 1)
                    tt(stage[m][:, 1, :], PS[3 + m][:, :], stage[m][:, 0, :].bitcast(F32), ALU.subtract).then_inc(qk_lo, 1)
                dve.wait_ge(xbo_ready, g + 1)
                for q in range(2):
                    dve.wait_ge(wo_ready, g * 2 + q + 1)
                    tt(X[:, 2 * q:2 * q + 2, :], pair(PS[q]), X[:, 2 * q:2 * q + 2, :], ALU.add).then_inc(x1_ready, 1)

                dve.wait_ge(x1_ready, g * 2 + 2)
                layer_stats(1, X)
                dve.wait_ge(xv_one, g + 1)
                for q in range(2):
                    dve.wait_ge(vp_ready, g * 2 + q + 1)
                    nc.vector.tensor_copy(xv[:, 2 * q:2 * q + 2, :, 0:XD],
                                          PS[5 if q == 0 else 2][:, :].rearrange("p (b h d) -> p b h d", b=2, h=XH)).then_inc(xv_ready, 1)
                layer_apply(1, X)

                def norm_lo(s, done):
                    for k in range(2):
                        dve.wait_ge(xT_hi, g * 4 + 2 * (s - 1) + k + 1)
                        tt(xT[:, 1, k, :], PS[6 + k][:, :], xT[:, 0, k, :].bitcast(F32), ALU.subtract).then_inc(done, 1)

                norm_lo(1, xT_lo)
                for m in range(2):
                    dve.wait_ge(qk_hi, g * 4 + 2 + m + 1)
                    stt(stage[m][:, 1, :], PS[m][:, :], float(XD) ** -0.5, stage[m][:, 0, :].bitcast(F32), ALU.mult,
                        ALU.subtract).then_inc(qk_lo, 1)

                def maxima(qd):
                    s = qd % 2
                    if qd >= 2:
                        for part in range(2):
                            dve.wait_ge(nm_diag[part], g * 16 + qd - 1)
                    dve.wait_ge(sm_ready, g * 16 + qd + 1)
                    nc.vector.tensor_reduce(nm[:, s, :], PS[s][:, :].rearrange("p (h t) -> p h t", h=4), AX, ALU.max,
                                            negate=True).then_inc(max_ready, 1)
                    dve.wait_ge(max_ready, g * 16 + qd + 1)
                    nc.vector.tensor_copy(nm2[:, s, 0, :], nm[:, s, :]).then_inc(nm_step, 1)
                    dve.wait_ge(nm_step, g * 32 + 2 * qd + 1)
                    tt(nm2[:, s, 1, :], nm[:, s, :], nm2[:, s, 0, :], ALU.subtract).then_inc(nm_step, 1)
                    if qd >= 2:
                        dve.wait_ge(t_ready, g * 16 + qd - 1)
                    tt(nmd[:, s, 0, :, :], identb[:].unsqueeze(1).to_broadcast([P, 4, P]),
                       nm2[:, s, 0, :].unsqueeze(2).to_broadcast([P, 4, P]), ALU.mult).then_inc(nm_diag[0], 1)

                def attended(b):
                    dve.wait_ge(o_part, g * 16 + 4 * b + 4)
                    o = PS[4 + b % 2][:, 0:XH * (XD + 1)].rearrange("p (h d) -> p h d", h=XH)
                    nc.vector.reciprocal(rec[:, b % 2, :], o[:, :, XD]).then_inc(rec_ready, 1)
                    dve.wait_ge(rec_ready, g * 4 + b + 1)
                    tt(tok[:, b, :].rearrange("p (h d) -> p h d", h=XH), o[:, :, 0:XD], rec[:, b % 2, :].unsqueeze(2).to_broadcast([P, XH, XD]),
                       ALU.mult).then_inc(yo_ready, 1)

                for qd in range(XQ):
                    maxima(qd)
                    if qd >= 6 and qd % 4 == 2:
                        attended((qd - 6) // 4)
                attended(3)
                for k in range(2):
                    dve.wait_ge(yT_hi, g * 2 + k + 1)
                    tt(xT[:, 1, k, :], PS[6 + k][:, :], xT[:, 0, k, :].bitcast(F32), ALU.subtract).then_inc(yT_lo, 1)
                for q in range(2):
                    dve.wait_ge(wout_ready, g * 2 + q + 1)
                    tt(X[:, 2 * q:2 * q + 2, :], pair(PS[q]), X[:, 2 * q:2 * q + 2, :], ALU.add).then_inc(x2_ready, 1)

                dve.wait_ge(x2_ready, g * 2 + 2)
                layer_stats(2, X)
                layer_apply(2, X)
                norm_lo(2, xT_lo)

                steps = [0]

                def step(ins):
                    steps[0] += 1
                    ins.then_inc(r_step, 1)
                    dve.wait_ge(r_step, g * R_STEPS + steps[0])

                def over(a, n):
                    return a.unsqueeze(2).to_broadcast([P, GB, n])

                revb = rev[:].unsqueeze(1).to_broadcast([P, GB, E])
                dve.wait_ge(route_ready, g + 1)
                step(nc.vector.tensor_copy(lg, PS[4][:, 0:GB * (E + 2)].rearrange("p (b e) -> p b e", b=GB)))
                logits = lg[:, :, 0:E]
                for o, src, m in ((r_o1, logits, 0), (r_o2, r_l2, 2)):
                    step(nc.vector.tensor_reduce(r_m[:, m, :], src, AX, ALU.max))
                    step(tt(r_a, src, over(r_m[:, m, :], E), ALU.is_equal))
                    step(tt(r_a, r_a, revb, ALU.mult))
                    step(nc.vector.tensor_reduce(r_m[:, m + 1, :], r_a, AX, ALU.max))
                    step(tt(o, r_a, over(r_m[:, m + 1, :], E), ALU.is_equal))
                    if m == 0:
                        step(stt(r_l2, r_o1, -3.0e38, logits, ALU.mult, ALU.add))
                step(tt(r_z[:, :, 0], r_m[:, 2, :], r_m[:, 0, :], ALU.subtract))
                step(ts(r_z[:, :, 1], lg[:, :, E], -1.0, None, ALU.mult))
                assert steps[0] == R_EXP
                dve.wait_ge(r_exp, g + 1)
                step(ts(r_d, r_e, 1.0, None, ALU.add))
                step(nc.vector.reciprocal(r_w, r_d))
                step(tt(r_z[:, :, 0], r_e[:, :, 0], r_w[:, :, 0], ALU.mult))
                step(tt(r_o1, r_o1, over(r_w[:, :, 0], E), ALU.mult))
                step(tt(r_o2, r_o2, over(r_z[:, :, 0], E), ALU.mult))
                step(tt(cw[:, :, 0:E], r_o1, r_o2, ALU.add))
                step(nc.vector.tensor_copy(cw[:, :, E:E + 1], r_w[:, :, 1:2]))
                dve.wait_ge(c3_zero, g + 1)
                step(nc.vector.tensor_copy(c3[:, :, 0:E + 1], cw))
                step(tt(cr, cw, c3[:, :, 0:E + 1], ALU.subtract))
                step(nc.vector.tensor_copy(c3[:, :, 32:32 + E + 1], cr))
                step(tt(cr2, cr, c3[:, :, 32:32 + E + 1], ALU.subtract))
                assert steps[0] == R_STEPS, steps[0]
                nc.vector.tensor_copy(c3[:, :, 64:64 + E + 1], cr2).then_inc(c3_ready, 1)

                for j in range(FB):
                    dve.wait_ge(silu_done, g * FB + j + 1)
                    dve.wait_ge(up_ready, g * FB + j + 1)
                    if j >= 2:
                        dve.wait_ge(h_lo, g * FB + j - 1)
                    tt(ring[:, 2 + j % 2, :], ring[:, j % 2, :], PS[2 + j % 2][:, :], ALU.mult).then_inc(gu_done, 1)
                    dve.wait_ge(cwb_ready, g * FB + j + 1)
                    dve.wait_ge(gu_done, g * FB + j + 1)
                    tt(ring[:, 2 + j % 2, :], ring[:, 2 + j % 2, :], PS[4 + j % 2][:, :], ALU.mult).then_inc(h_done, 1)
                dve.wait_ge(down_done, g * FB + FB)
                for q in range(2):
                    tt(X[:, 2 * q:2 * q + 2, :], pair(PS[6 + q]), X[:, 2 * q:2 * q + 2, :], ALU.add).then_inc(x3_ready, 1)
    return nc


INPUTS = ['x', 'ctx_512', 'L0_attn_Wr', 'L0_attn_br', 'L0_attn_Wk', 'L0_attn_bk', 'L0_attn_Wv', 'L0_attn_bv', 'L0_attn_Wg',
          'L0_attn_bg', 'L0_attn_Wo', 'L0_attn_bo', 'L0_attn_ln_g', 'L0_attn_ln_b', 'L0_attn_maa_k', 'L0_attn_maa_v',
          'L0_attn_maa_r', 'L0_attn_maa_g', 'L0_attn_time_decay', 'L0_attn_time_faaaa', 'L0_xattn_Wq', 'L0_xattn_Wkv_expand',
          'L0_xattn_Wout', 'L0_ffn_router_w', 'L0_ffn_w_gate', 'L0_ffn_w_up', 'L0_ffn_w_down', 'L0_ffn_sw_gate',
          'L0_ffn_sw_up', 'L0_ffn_sw_down', 'L0_ffn_shared_gate_w']


def kernel(**inputs):
    import numpy as np
    import concourse.bacc as bacc
    from concourse.bass_utils import run_bass_kernel_spmd

    nc = bacc.Bacc("TRN2", target_bir_lowering=False, num_devices=1)
    arrays, args = {}, []
    for name in INPUTS:
        a = np.ascontiguousarray(inputs[name])
        arrays[f"in_{name}"] = a
        args.append(nc.dram_tensor(f"in_{name}", a.shape, mybir.dt.from_np(a.dtype), kind="ExternalInput").ap())
    shape = inputs['x'].shape
    args.append(nc.dram_tensor("out_x", shape, F32, kind="ExternalOutput").ap())
    decoder_layer(nc, *args)
    r = run_bass_kernel_spmd(nc, [arrays], core_ids=[0])
    return r.results[0]["out_x"]
```
